# Optimizing a Trainium2 kernel written in Bass

```python
import numpy as np
import jax
import jax.numpy as jnp

def _softmax(x, axis=-1):
    return jax.nn.softmax(x, axis=axis)

def _gelu(x):
    return jax.nn.gelu(x, approximate=True)

def _silu(x):
    return jax.nn.silu(x)

def _sigmoid(x):
    return jax.nn.sigmoid(x)

def _layernorm(x, axis=-1, eps=1e-05):
    m = jnp.mean(x, axis=axis, keepdims=True)
    v = jnp.var(x, axis=axis, keepdims=True)
    return (x - m) / jnp.sqrt(v + eps)

def _scatter_add(tgt, idx, src, axis=0):
    return tgt.at[idx].add(src)

def _segment_sum(src, seg, n):
    return jax.ops.segment_sum(src, seg, n)
kernel_name = 'mk_early_fusion_d2_tok_img768_r4_1d703c'

def setup_inputs(seed: int=0):
    np.random.seed(seed)
    _w = jnp.asarray

    def _rec_inputs():
        import jax
        import jax.numpy as jnp
        _rk = jax.random.key(seed)
        x = -0.000356955 + 1 * jax.random.normal(jax.random.fold_in(_rk, 1), (32, 3, 128, 128), jnp.float32)
        txt = -0.000277325 + 0.02 * jax.random.normal(jax.random.fold_in(_rk, 2), (32, 32, 192), jnp.float32)
        return (x, txt)
    x, txt = _rec_inputs()

    def _L0_tok_setup():
        import jax, jax.numpy as jnp
        import numpy as np
        PATCH = 16

        def _binary_activation(x):
            out1 = jnp.where(x < -1.0, -1.0, x * x + 2.0 * x)
            out2 = jnp.where(x < 0.0, out1, -x * x + 2.0 * x)
            out3 = jnp.where(x < 1.0, out2, 1.0)
            return out3 + jax.lax.stop_gradient(jnp.sign(x) - out3)

        def _binarize_weights(w):
            sf = jax.lax.stop_gradient(jnp.mean(jnp.abs(w), axis=(1, 2, 3), keepdims=True))
            clipped = jnp.clip(w, -1.0, 1.0)
            return clipped + jax.lax.stop_gradient(sf * jnp.sign(w) - clipped)
        key = jax.random.key(seed)
        k1, k2 = jax.random.split(key)
        x = jax.random.normal(k1, (128, 3, 224, 224), dtype=jnp.float32)
        weight = jax.random.uniform(k2, (192, 3, PATCH, PATCH), dtype=jnp.float32) * 0.001
        move_bias = jnp.zeros((3,), dtype=jnp.float32)
        return {'x': x, 'weight': weight, 'move_bias': move_bias}
    _L0_tok_all = _L0_tok_setup()
    _L0_tok_in = {k: v for k, v in _L0_tok_all.items() if k in ('weight', 'move_bias')}
    del _L0_tok_all

    def _L0_attn_setup():
        import jax, jax.numpy as jnp
        import numpy as np
        EMBED_DIM = 192
        NUM_HEADS = 12
        HEAD_DIM = EMBED_DIM // NUM_HEADS
        SCALE = float(np.sqrt(HEAD_DIM))
        key = jax.random.key(seed)
        ks = jax.random.split(key, 9)
        B, S, D = (1, 1024, EMBED_DIM)
        w_std = 1.0 / np.sqrt(D)
        x = jax.random.normal(ks[0], (B, S, D), dtype=jnp.float32)
        Wq = jax.random.uniform(ks[1], (D, D), jnp.float32, -w_std, w_std)
        bq = jax.random.uniform(ks[2], (D,), jnp.float32, -w_std, w_std)
        Wk = jax.random.uniform(ks[3], (D, D), jnp.float32, -w_std, w_std)
        bk = jax.random.uniform(ks[4], (D,), jnp.float32, -w_std, w_std)
        Wv = jax.random.uniform(ks[5], (D, D), jnp.float32, -w_std, w_std)
        bv = jax.random.uniform(ks[6], (D,), jnp.float32, -w_std, w_std)
        Wo = jax.random.uniform(ks[7], (D, D), jnp.float32, -w_std, w_std)
        bo = jax.random.uniform(ks[8], (D,), jnp.float32, -w_std, w_std)
        return {'x': x, 'Wq': Wq, 'bq': bq, 'Wk': Wk, 'bk': bk, 'Wv': Wv, 'bv': bv, 'Wo': Wo, 'bo': bo}
    _L0_attn_all = _L0_attn_setup()
    _L0_attn_in = {k: v for k, v in _L0_attn_all.items() if k in ('Wq', 'bq', 'Wk', 'bk', 'Wv', 'bv', 'Wo', 'bo')}
    del _L0_attn_all

    def _L0_ffn_setup():
        import jax, jax.numpy as jnp
        import numpy as np
        EPS_NORM = 1e-05
        RMS_EPS = 1e-05

        def _l2_normalize(v):
            n = jnp.sqrt(jnp.sum(v * v, axis=-1, keepdims=True))
            return v / jnp.maximum(n, EPS_NORM)

        def _rms_norm(x, weight, eps):
            ms = jnp.mean(x * x, axis=-1, keepdims=True)
            return x * jax.lax.rsqrt(ms + eps) * weight
        key = jax.random.key(seed)
        ks = jax.random.split(key, 6)
        B, T, D = (8, 1024, 192)
        S, F = (64, 768)
        x = jax.random.normal(ks[0], (B, T, D), dtype=jnp.float32)
        slots = 0.02 * jax.random.normal(ks[1], (S, D), dtype=jnp.float32)
        scale = jnp.ones((S,), dtype=jnp.float32)
        fc1_weight = 0.02 * jax.random.normal(ks[2], (S, D, F), dtype=jnp.float32)
        fc1_bias = jnp.zeros((S, F), dtype=jnp.float32)
        fc2_weight = 0.02 * jax.random.normal(ks[3], (S, F, D), dtype=jnp.float32)
        fc2_bias = jnp.zeros((S, D), dtype=jnp.float32)
        norm_weight = jnp.ones((D,), dtype=jnp.float32)
        return {'x': x, 'slots': slots, 'scale': scale, 'fc1_weight': fc1_weight, 'fc1_bias': fc1_bias, 'fc2_weight': fc2_weight, 'fc2_bias': fc2_bias, 'norm_weight': norm_weight}
    _L0_ffn_all = _L0_ffn_setup()
    _L0_ffn_in = {k: v for k, v in _L0_ffn_all.items() if k in ('slots', 'scale', 'fc1_weight', 'fc1_bias', 'fc2_weight', 'fc2_bias', 'norm_weight')}
    del _L0_ffn_all

    def _L1_attn_setup():
        import jax, jax.numpy as jnp
        import numpy as np
        BLOCK_SIZE = 64
        N_EMBD = 192
        HEAD_SIZE = 192

        def _rope_tables(T, dim, theta0=10000.0):
            j = jnp.arange(dim // 2, dtype=jnp.float32)
            theta = jnp.float32(theta0) ** (-2.0 * j / jnp.float32(dim))
            ang = jnp.arange(T, dtype=jnp.float32)[:, None] * theta[None, :]
            return (jnp.cos(ang), jnp.sin(ang))

        def _apply_rope(t, cos, sin):
            B, T, D = t.shape
            tr = t.reshape(B, T, D // 2, 2)
            re, im = (tr[..., 0], tr[..., 1])
            out_re = re * cos[None] - im * sin[None]
            out_im = re * sin[None] + im * cos[None]
            return jnp.stack([out_re, out_im], axis=-1).reshape(B, T, D)
        key = jax.random.key(seed)
        k1, k2, k3, k4 = jax.random.split(key, 4)
        B, T = (128, BLOCK_SIZE)
        x = jax.random.normal(k1, (B, T, N_EMBD), dtype=jnp.float32)
        Wq = jax.random.normal(k2, (N_EMBD, HEAD_SIZE), dtype=jnp.float32) * 0.02
        Wk = jax.random.normal(k3, (N_EMBD, HEAD_SIZE), dtype=jnp.float32) * 0.02
        Wv = jax.random.normal(k4, (N_EMBD, HEAD_SIZE), dtype=jnp.float32) * 0.02
        return {'x': x, 'Wq': Wq, 'Wk': Wk, 'Wv': Wv}
    _L1_attn_all = _L1_attn_setup()
    _L1_attn_in = {k: v for k, v in _L1_attn_all.items() if k in ('Wq', 'Wk', 'Wv')}
    del _L1_attn_all

    def _L1_ffn_setup():
        import jax, jax.numpy as jnp
        import numpy as np
        D_MODEL = 192
        N_EXPERTS = 8
        TOP_K = 2
        D_FF = 4 * D_MODEL
        key = jax.random.key(seed)
        ks = jax.random.split(key, 6)
        B, S = (2, 512)
        x = jax.random.normal(ks[0], (B, S, D_MODEL), dtype=jnp.float32)
        Wr = jax.random.normal(ks[1], (D_MODEL, N_EXPERTS), dtype=jnp.float32) * 0.02
        W1 = jax.random.normal(ks[2], (N_EXPERTS, D_MODEL, D_FF), dtype=jnp.float32) * 0.02
        b1 = jnp.zeros((N_EXPERTS, D_FF), dtype=jnp.float32)
        W2 = jax.random.normal(ks[3], (N_EXPERTS, D_FF, D_MODEL), dtype=jnp.float32) * 0.02
        b2 = jnp.zeros((N_EXPERTS, D_MODEL), dtype=jnp.float32)
        return {'x': x, 'Wr': Wr, 'W1': W1, 'b1': b1, 'W2': W2, 'b2': b2}
    _L1_ffn_all = _L1_ffn_setup()
    _L1_ffn_in = {k: v for k, v in _L1_ffn_all.items() if k in ('Wr', 'W1', 'b1', 'W2', 'b2')}
    del _L1_ffn_all
    return {'x': x, 'txt': txt, 'L0_tok_weight': _L0_tok_in['weight'], 'L0_tok_move_bias': _L0_tok_in['move_bias'], 'L0_attn_Wq': _L0_attn_in['Wq'], 'L0_attn_bq': _L0_attn_in['bq'], 'L0_attn_Wk': _L0_attn_in['Wk'], 'L0_attn_bk': _L0_attn_in['bk'], 'L0_attn_Wv': _L0_attn_in['Wv'], 'L0_attn_bv': _L0_attn_in['bv'], 'L0_attn_Wo': _L0_attn_in['Wo'], 'L0_attn_bo': _L0_attn_in['bo'], 'L0_ffn_slots': _L0_ffn_in['slots'], 'L0_ffn_scale': _L0_ffn_in['scale'], 'L0_ffn_fc1_weight': _L0_ffn_in['fc1_weight'], 'L0_ffn_fc1_bias': _L0_ffn_in['fc1_bias'], 'L0_ffn_fc2_weight': _L0_ffn_in['fc2_weight'], 'L0_ffn_fc2_bias': _L0_ffn_in['fc2_bias'], 'L0_ffn_norm_weight': _L0_ffn_in['norm_weight'], 'L1_attn_Wq': _L1_attn_in['Wq'], 'L1_attn_Wk': _L1_attn_in['Wk'], 'L1_attn_Wv': _L1_attn_in['Wv'], 'L1_ffn_Wr': _L1_ffn_in['Wr'], 'L1_ffn_W1': _L1_ffn_in['W1'], 'L1_ffn_b1': _L1_ffn_in['b1'], 'L1_ffn_W2': _L1_ffn_in['W2'], 'L1_ffn_b2': _L1_ffn_in['b2']}

def reference(x, txt, L0_tok_weight, L0_tok_move_bias, L0_attn_Wq, L0_attn_bq, L0_attn_Wk, L0_attn_bk, L0_attn_Wv, L0_attn_bv, L0_attn_Wo, L0_attn_bo, L0_ffn_slots, L0_ffn_scale, L0_ffn_fc1_weight, L0_ffn_fc1_bias, L0_ffn_fc2_weight, L0_ffn_fc2_bias, L0_ffn_norm_weight, L1_attn_Wq, L1_attn_Wk, L1_attn_Wv, L1_ffn_Wr, L1_ffn_W1, L1_ffn_b1, L1_ffn_W2, L1_ffn_b2):
    import jax
    import jax.numpy as jnp

    def _L0_tok_ref(x, weight, move_bias):
        import jax, jax.numpy as jnp
        import numpy as np
        PATCH = 16

        def _binary_activation(x):
            out1 = jnp.where(x < -1.0, -1.0, x * x + 2.0 * x)
            out2 = jnp.where(x < 0.0, out1, -x * x + 2.0 * x)
            out3 = jnp.where(x < 1.0, out2, 1.0)
            return out3 + jax.lax.stop_gradient(jnp.sign(x) - out3)

        def _binarize_weights(w):
            sf = jax.lax.stop_gradient(jnp.mean(jnp.abs(w), axis=(1, 2, 3), keepdims=True))
            clipped = jnp.clip(w, -1.0, 1.0)
            return clipped + jax.lax.stop_gradient(sf * jnp.sign(w) - clipped)
        B = x.shape[0]
        embed_dim = weight.shape[0]
        xb = _binary_activation(x + move_bias.reshape(1, -1, 1, 1))
        bw = _binarize_weights(weight)
        y = jax.lax.conv_general_dilated(xb, bw, window_strides=(PATCH, PATCH), padding=((1, 1), (1, 1)), dimension_numbers=('NCHW', 'OIHW', 'NCHW'))
        y = y.reshape(B, embed_dim, -1).transpose(0, 2, 1)
        return y

    def _L0_attn_ref(x, Wq, bq, Wk, bk, Wv, bv, Wo, bo):
        import jax, jax.numpy as jnp
        import numpy as np
        EMBED_DIM = 192
        NUM_HEADS = 12
        HEAD_DIM = EMBED_DIM // NUM_HEADS
        SCALE = float(np.sqrt(HEAD_DIM))
        B, S, D = x.shape
        H, Dh = (NUM_HEADS, HEAD_DIM)
        q = (x @ Wq + bq).reshape(B, S, H, Dh).transpose(0, 2, 1, 3)
        k = (x @ Wk + bk).reshape(B, S, H, Dh).transpose(0, 2, 1, 3)
        v = (x @ Wv + bv).reshape(B, S, H, Dh).transpose(0, 2, 1, 3)
        scores = jnp.einsum('bhqd,bhkd->bhqk', q, k) / SCALE
        attn = jax.nn.softmax(scores, axis=-1)
        out = jnp.einsum('bhqk,bhkd->bhqd', attn, v)
        out = out.transpose(0, 2, 1, 3).reshape(B, S, D)
        return out @ Wo + bo

    def _L0_ffn_ref(x, slots, scale, fc1_weight, fc1_bias, fc2_weight, fc2_bias, norm_weight):
        import jax, jax.numpy as jnp
        import numpy as np
        EPS_NORM = 1e-05
        RMS_EPS = 1e-05

        def _l2_normalize(v):
            n = jnp.sqrt(jnp.sum(v * v, axis=-1, keepdims=True))
            return v / jnp.maximum(n, EPS_NORM)

        def _rms_norm(x, weight, eps):
            ms = jnp.mean(x * x, axis=-1, keepdims=True)
            return x * jax.lax.rsqrt(ms + eps) * weight
        xn = _rms_norm(x, norm_weight, RMS_EPS)
        tok = _l2_normalize(xn)
        sl = _l2_normalize(slots) * scale[:, None]
        logits = jnp.einsum('sd,btd->bst', sl, tok)
        dispatch_w = jax.nn.softmax(logits, axis=-1)
        combine_w = jax.nn.softmax(logits, axis=-2)
        y = jnp.einsum('btd,bst->bsd', xn, dispatch_w)
        y = jnp.einsum('sio,bsi->bso', fc1_weight, y) + fc1_bias
        y = jax.nn.gelu(y, approximate=False)
        y = jnp.einsum('sio,bsi->bso', fc2_weight, y) + fc2_bias
        out = jnp.einsum('bsd,bst->btd', y, combine_w)
        return out

    def _L1_attn_ref(x, Wq, Wk, Wv):
        import jax, jax.numpy as jnp
        import numpy as np
        BLOCK_SIZE = 64
        N_EMBD = 192
        HEAD_SIZE = 192

        def _rope_tables(T, dim, theta0=10000.0):
            j = jnp.arange(dim // 2, dtype=jnp.float32)
            theta = jnp.float32(theta0) ** (-2.0 * j / jnp.float32(dim))
            ang = jnp.arange(T, dtype=jnp.float32)[:, None] * theta[None, :]
            return (jnp.cos(ang), jnp.sin(ang))

        def _apply_rope(t, cos, sin):
            B, T, D = t.shape
            tr = t.reshape(B, T, D // 2, 2)
            re, im = (tr[..., 0], tr[..., 1])
            out_re = re * cos[None] - im * sin[None]
            out_im = re * sin[None] + im * cos[None]
            return jnp.stack([out_re, out_im], axis=-1).reshape(B, T, D)
        B, T, C = x.shape
        q = x @ Wq
        k = x @ Wk
        v = x @ Wv
        cos, sin = _rope_tables(T, HEAD_SIZE)
        q = _apply_rope(q, cos, sin)
        k = _apply_rope(k, cos, sin)
        scale = jnp.float32(HEAD_SIZE) ** (-0.5)
        wei = jnp.einsum('bqd,bkd->bqk', q, k) * scale
        causal = jnp.tril(jnp.ones((T, T), dtype=bool))
        wei = jnp.where(causal[None], wei, -jnp.inf)
        wei = jax.nn.softmax(wei, axis=-1)
        out = jnp.einsum('bqk,bkd->bqd', wei, v)
        return out

    def _L1_ffn_ref(x, Wr, W1, b1, W2, b2):
        import jax, jax.numpy as jnp
        import numpy as np
        D_MODEL = 192
        N_EXPERTS = 8
        TOP_K = 2
        D_FF = 4 * D_MODEL
        B, S, D = x.shape
        T = B * S
        x_flat = x.reshape(T, D)
        gate_logits = x_flat @ Wr
        topw, topi = jax.lax.top_k(gate_logits, TOP_K)
        topw = jax.nn.softmax(topw, axis=-1)
        combine = jnp.zeros((T, N_EXPERTS), dtype=x.dtype)
        combine = combine.at[jnp.arange(T)[:, None], topi].add(topw)
        h = jax.nn.relu(jnp.einsum('td,edh->eth', x_flat, W1) + b1[:, None, :])
        y = jnp.einsum('eth,ehd->etd', h, W2) + b2[:, None, :]
        out = jnp.einsum('te,etd->td', combine, y)
        return out.reshape(B, S, D)
    h = _L0_tok_ref(x, L0_tok_weight, L0_tok_move_bias)
    h = jnp.concatenate([h, txt], axis=1)
    h = h + _L0_attn_ref(_layernorm(h, axis=-1), L0_attn_Wq, L0_attn_bq, L0_attn_Wk, L0_attn_bk, L0_attn_Wv, L0_attn_bv, L0_attn_Wo, L0_attn_bo)
    h = h + _L0_ffn_ref(_layernorm(h, axis=-1), L0_ffn_slots, L0_ffn_scale, L0_ffn_fc1_weight, L0_ffn_fc1_bias, L0_ffn_fc2_weight, L0_ffn_fc2_bias, L0_ffn_norm_weight)
    h = h + _L1_attn_ref(_layernorm(h, axis=-1), L1_attn_Wq, L1_attn_Wk, L1_attn_Wv)
    h = h + _L1_ffn_ref(_layernorm(h, axis=-1), L1_ffn_Wr, L1_ffn_W1, L1_ffn_b1, L1_ffn_W2, L1_ffn_b2)
    return h

_drawn_inputs = setup_inputs


def setup_inputs(seed=0):
    import zlib

    import numpy as np

    out = dict(_drawn_inputs(seed))
    spreads = {'L0_tok_move_bias': (0.0, 0.1),
     'L0_ffn_scale': (1.0, 0.6),
     'L0_ffn_fc1_bias': (0.0, 0.1),
     'L0_ffn_fc2_bias': (0.0, 0.1),
     'L0_ffn_norm_weight': (1.0, 0.2),
     'L1_ffn_b1': (0.0, 0.1),
     'L1_ffn_b2': (0.0, 0.1)}
    factors = {'L0_attn_bk': 8.0, 'L1_attn_Wq': 8.0, 'L1_attn_Wk': 8.0}
    for name, (base, spread) in spreads.items():
        noise = np.random.default_rng([zlib.crc32(name.encode()), seed]).standard_normal(out[name].shape)
        drawn = base * np.exp(spread * noise) if base else spread * noise
        out[name] = jnp.asarray(drawn.astype(out[name].dtype))
    for name, factor in factors.items():
        out[name] = (out[name] * factor).astype(out[name].dtype)
    return out
```

```python
from contextlib import ExitStack

import numpy as np

import concourse.bass as bass
from concourse import mybir

F32 = mybir.dt.float32
BF16 = mybir.dt.bfloat16
ALU = mybir.AluOpType
ACT = mybir.ActivationFunctionType
AX = mybir.AxisListType

B = 32
T_IMG, T_TXT = 64, 32
T = T_IMG + T_TXT
D = 192
HALF = D // 2
PATCH, CIN = 16, 3
KP = CIN * PATCH * PATCH
KC = KP // 128
NH, DH = 12, 16
HH = NH // 2
HPAD = 32
HG = 128 // HPAD
NG = NH // HG
NS = 64
F = 768
FC = F // 128
GS = 4
NGR = NS // GS
W1_DMAS = 3
NE = 8
NTILES = 56
NTOK = B * T
NX = 4
NPAIR = 2 * B
assert NTILES >= (2 * NTOK + NE * 127) // 128 and NTILES % 2 == 0 and 2 * GS == NE
EPS = 1e-5
UNROLL = 4


def item(eng, sem, b, per=1):
    eng.wait_ge(sem, b * per + per)


def reused(eng, sem, b, depth, per=1):
    if not isinstance(b, int) or b >= depth:
        eng.wait_ge(sem, b * per - (depth - 1) * per)


def steps(eng, n, stages, unroll=UNROLL, depth=UNROLL):
    last = max(lag for _, lag in stages)
    first = -(-(last + depth) // unroll) * unroll
    for t in range(first):
        for stage, lag in stages:
            if t >= lag:
                stage(t - lag, (t - lag) % unroll)
    with eng.Fori(first // unroll, n // unroll) as j:
        for u in range(unroll):
            for stage, lag in stages:
                stage(j * unroll + (u - lag), (u - lag) % unroll)
    for t in range(n, n + last):
        for stage, lag in stages:
            if t - lag < n:
                stage(t - lag, (t - lag) % unroll)


class Prog:

    def __init__(self, nc):
        self.nc = nc
        self.live = []

    def phase_sem(self, name):
        s = self.nc.alloc_semaphore(name)
        self.live.append(s)
        return s

    def clear_sems(self):
        self.nc.clear_and_free_semaphores(self.live)
        self.nc.all_engine_barrier()
        self.live = []


def build(nc, A, upto=99):
    with ExitStack() as ctx:
        g = Prog(nc)

        def sem(name):
            return ctx.enter_context(nc.semaphore(name))

        def sb(name, shape, dt=F32):
            return ctx.enter_context(nc.sbuf_tensor(name, shape, dt))

        g.h = sb("h", [T, B, D])
        g.stats = sb("stats", [T, B, 6])
        g.rstd = sb("rstd", [T, B])
        g.nmr = sb("nmr", [T, B])
        g.ident = sb("ident", [128, 128])
        g.lnt = sb("lnt", [T, 4, B])
        g.s_const = sem("s_const")
        w1_flat = sb("w1", [HALF + 1, 4 * GS * F])
        w2_flat = sb("w2", [128, 2 * GS * FC * D])
        g.w1 = w1_flat[:, :].rearrange("p (i k s f) -> p i k s f", i=2, k=2, f=F)
        g.w2 = w2_flat[:, :].rearrange("p (i s n) -> p i s n", i=2, n=FC * D)
        g.e1 = w1_flat[:, :].rearrange("p (k e f) -> p k e f", k=2, f=F)
        g.e2 = w2_flat[:, :].rearrange("p (e n) -> p e n", n=FC * D)
        g.s_e = sem("s_e")
        g.s_x = [sem(f"s_x{i}") for i in range(NX)]
        g.s_add = sem("s_add")
        g.s_w1 = [sem(f"s_w1_{i}") for i in range(2)]
        g.s_w2 = [sem(f"s_w2_{i}") for i in range(2)]
        psum = ctx.enter_context(nc.psum_tensor("psum", [128, 8, 512], F32))
        g.ps = psum
        embed(nc, A, g)
        if upto >= 1:
            attention0(nc, A, g)
        if upto >= 2:
            soft_moe(nc, A, g)
            g.clear_sems()
        if upto >= 3:
            attention1(nc, A, g)
        if upto >= 4:
            routed_moe(nc, A, g)
        else:
            store(nc, A, g)


def layernorm_scale(eng_v, eng_s, g, s):
    st = g.stats
    mean, half_diff, var, sq = (g.lnt[:, i, :] for i in range(4))
    if eng_v is not None:
        v = eng_v
        v.tensor_tensor(mean, st[:, :, 1], st[:, :, 4], ALU.add).then_inc(s, 1)
        v.tensor_tensor(half_diff, st[:, :, 1], st[:, :, 4], ALU.subtract).then_inc(s, 1)
        v.tensor_tensor(var, st[:, :, 2], st[:, :, 5], ALU.add).then_inc(s, 1)
        v.wait_ge(s, 3)
        v.tensor_tensor(half_diff, half_diff, half_diff, ALU.mult).then_inc(s, 1)
        v.tensor_scalar(var, var, 1.0 / D, EPS, ALU.mult, ALU.add).then_inc(s, 1)
        v.wait_ge(s, 5)
        v.scalar_tensor_tensor(var, half_diff, 0.25, var, ALU.mult, ALU.add).then_inc(s, 1)
        v.wait_ge(s, 7)
        v.reciprocal(g.rstd[:, :], sq).then_inc(s, 1)
        v.wait_ge(s, 8)
        v.scalar_tensor_tensor(g.nmr[:, :], mean, -0.5, g.rstd[:, :], ALU.mult, ALU.mult).then_inc(s, 1)
        v.wait_ge(s, 9)
    if eng_s is not None:
        eng_s.wait_ge(s, 6)
        eng_s.activation(sq, var, ACT.Sqrt).then_inc(s, 1)


def load_slots(sp, A, g, gr, i, w1_free=lambda: None, w2_free=lambda: None):
    src = A["fc1_w"][bass.ds(gr * GS, GS), :, :].rearrange("s (k p) n -> k p s n", k=2)
    w1_free()
    for k in range(2):
        sp.dma_start(g.w1[0:HALF, i, k, :, :], src[k]).then_inc(g.s_w1[i], 16)
    sp.dma_start(g.w1[HALF:HALF + 1, i, 1, :, :], A["fc1_b"][bass.ds(gr * GS, GS), :].unsqueeze(0)).then_inc(g.s_w1[i], 16)
    w2_free()
    sp.dma_start(g.w2[:, i, :, :], A["fc2_w"][bass.ds(gr * GS, GS), :, :].rearrange(
        "s (p k) n -> p s (k n)", k=FC)).then_inc(g.s_w2[i], 16)


def embed(nc, A, g):
    NT = B * T_IMG
    CH = 512
    NCH = NT // CH
    TPC = CH // 128
    with ExitStack() as ctx:
        def sem(name):
            return g.phase_sem(name)

        def sb(name, shape, dt=F32):
            return ctx.enter_context(nc.sbuf_tensor(name, shape, dt))

        x_raw = sb("x_raw", [128, NCH, KC, CH])
        x_sign = sb("x_sign", [128, KC, NT], BF16)
        w_raw = sb("w_raw", [128, KC, D])
        w_abs = sb("w_abs", [128, KC, D])
        w_sign = sb("w_sign", [128, KC, D], BF16)
        move = sb("move", [128, KC])
        keep = sb("keep", [128, KC])
        ones = sb("ones_e", [128, 128])
        sf = sb("sf", [128, D])
        s_w, s_txt = sem("e_w"), sem("e_txt")
        s_x = [sem(f"e_x{c}") for c in range(NCH)]
        s_ones, s_wsign, s_wabs, s_sfps, s_sf = (sem(n) for n in ("e_ones", "e_wsign", "e_wabs", "e_sfps", "e_sf"))
        s_sign, s_row, s_edge, s_tile, s_out, s_stats, s_ln = (
            sem(n) for n in ("e_sign", "e_row", "e_edge", "e_tile", "e_out", "e_stats", "e_ln"))
        block = ctx.enter_context(nc.Block())

        @block.sync
        def _(sp):
            sp.dma_start(w_raw[:, :, :], A["tok_w"].rearrange("(k p) e -> p k e", p=128)).then_inc(s_w, 16)
            sp.dma_start(move[:, :], A["tok_move"]).then_inc(s_w, 16)
            sp.dma_start(keep[:, :], A["tok_keep"]).then_inc(s_w, 16)
            for c in range(NCH):
                sp.dma_start(x_raw[:, c, :, :],
                             A["x_patches"][:, :, c * CH:(c + 1) * CH].rearrange("k p n -> p k n")).then_inc(s_x[c], 16)
            sp.dma_start(g.ident[:, :], A["ident"]).then_inc(g.s_const, 16)
            sp.dma_start(g.h[T_IMG:T, :, :], A["txt"].rearrange("b t d -> t b d")).then_inc(s_txt, 16)

        @block.gpsimd
        def _(pool):
            pool.memset(ones[:, :], 1.0 / KP).then_inc(s_ones, 1)

        @block.scalar
        def _(act):
            act.wait_ge(s_w, 48)
            act.activation(w_sign[:, :, :], w_raw[:, :, :], ACT.Sign).then_inc(s_wsign, 1)
            act.activation(w_abs[:, :, :], w_raw[:, :, :], ACT.Abs).then_inc(s_wabs, 1)
            for c in range(NCH):
                act.wait_ge(s_x[c], 16)
                for k in range(KC):
                    act.activation(x_sign[:, k, c * CH:(c + 1) * CH], x_raw[:, c, k, :],
                                   ACT.Sign, bias=move[:, k:k + 1]).then_inc(s_sign, 1)
            layernorm_scale(None, act, g, s_ln)

        @block.tensor
        def _(pe):
            pe.wait_ge(s_ones, 1)
            pe.wait_ge(s_wabs, 1)
            for k in range(KC):
                mm = pe.matmul(g.ps[:, 7, 0:D], ones[:, :], w_abs[:, k, :], start=(k == 0), stop=(k == KC - 1))
            mm.then_inc(s_sfps, 1)
            pe.wait_ge(s_wsign, 1)
            with pe.Fori(0, NCH) as c:
                item(pe, s_edge, c)
                for u in range(TPC):
                    pe.wait_ge(s_out, c * (2 * TPC) + 2 * (u + 1))
                    for k in range(KC):
                        mm = pe.matmul(g.ps[:, u, 0:D], x_sign[:, k, bass.ds(c * CH + u * 128, 128)],
                                       w_sign[:, k, :], start=(k == 0), stop=(k == KC - 1))
                    mm.then_inc(s_tile, 1)

        @block.vector
        def _(v):
            v.sem_inc(s_out, 2 * TPC)
            v.wait_ge(s_sfps, 1)
            v.tensor_copy(sf[:, :], g.ps[:, 7, 0:D]).then_inc(s_sf, 1)
            v.wait_ge(s_sf, 1)

            def edges(c):
                item(v, s_sign, c, KC)
                tok = x_sign[:, :, bass.ds(c * CH, CH)].rearrange("p k (q j) -> p k q j", j=8)[:, :, :, 0]
                row = x_sign[0:CIN * PATCH, 0, bass.ds(c * CH, CH)].rearrange("p (b i j) -> p b i j", i=8, j=8)
                v.tensor_scalar(row[:, :, 0, :], row[:, :, 0, :], 0.0, None, ALU.mult).then_inc(s_row, 1)
                item(v, s_row, c)
                v.tensor_tensor(tok, tok, keep[:, :].unsqueeze(2).broadcast_to([128, KC, CH // 8]),
                                ALU.mult).then_inc(s_edge, 1)

            def scale_tiles(c):
                for u in range(TPC):
                    v.wait_ge(s_tile, c * TPC + u + 1)
                    for i in range(2):
                        b = c * (2 * TPC) + 2 * u + i
                        v.tensor_tensor(g.h[0:T_IMG, bass.ds(b, 1), :],
                                        g.ps[64 * i:64 * i + 64, u, 0:D].unsqueeze(1),
                                        sf[64 * i:64 * i + 64, :].unsqueeze(1), ALU.mult).then_inc(s_out, 1)

            edges(0)
            with v.Fori(1, NCH) as c:
                edges(c)
                scale_tiles(c - 1)
            scale_tiles(NCH - 1)
            v.wait_ge(s_txt, 16)
            v.wait_ge(s_out, 2 * TPC + B)
            with v.Fori(0, B // UNROLL) as j:
                for u in range(UNROLL):
                    b = j * UNROLL
                    v.bn_stats(g.stats[:, bass.ds(b + u, 1), :].rearrange("p a s -> p (a s)"),
                               g.h[:, bass.ds(b + u, 1), :].rearrange("p a d -> p (a d)")).then_inc(s_stats, 1)
            v.wait_ge(s_stats, B)
            layernorm_scale(v, None, g, s_ln)


def attention0(nc, A, g):
    with ExitStack() as ctx:
        def sem(name):
            return g.phase_sem("a_" + name)

        def sb(name, shape, dt=F32):
            return ctx.enter_context(nc.sbuf_tensor("a_" + name, shape, dt))

        wqk = sb("wqk", [HALF + 1, 2, 2 * D])
        wv = sb("wv", [HALF + 1, 2, D])
        wo = sb("wo", [128, NG, D])
        bo = sb("bo", [T, D])
        hmask = sb("hmask", [HALF, HH])
        xn = sb("xn", [T, 2, D])
        xT = sb("xT", [HALF + 1, 2, 2, T])
        qk = sb("qk", [HALF, 2, 4, T])
        kb = sb("kb", [HALF, 2, 2, HH, T])
        vv = sb("vv", [T, 4, NH, HPAD])
        p = sb("p", [T, 2, NH, T])
        pT = sb("pT", [T, NG, HG, T])
        oT = sb("oT", [128, NG, T])
        rw = sb("rw", [T, 2, NH, HPAD])
        rT = sb("rT", [128, NG, T])
        ones = sb("ones", [T, NH])
        mx = sb("mx", [T, 2, NH])
        sm = sb("sm", [T, 2, NH])
        rs = sb("rs", [T, 2, NH])

        s_w, s_set, s_vset, s_ones = sem("w"), sem("set"), sem("vset"), sem("ones")
        s_xn, s_bo, s_xTp, s_xTs, s_qkp, s_vp, s_qks, s_vs, s_kb = (
            sem(n) for n in ("xn", "bo", "xTp", "xTs", "qkp", "vp", "qks", "vs", "kb"))
        s_sc, s_mx, s_sub, s_exp, s_sum, s_rs, s_rw = (sem(n) for n in ("sc", "mx", "sub", "exp", "sum", "rs", "rw"))
        s_pTp, s_pTs, s_rTp, s_rTs, s_oTp, s_oTs, s_op, s_res, s_st, s_ln = (
            sem(n) for n in ("pTp", "pTs", "rTp", "rTs", "oTp", "oTs", "op", "res", "st", "ln"))

        bank_x = g.ps[:, 0, :]
        bank_qk = g.ps[0:HALF, 1, 0:4 * T].rearrange("p (m t) -> p m t", t=T)
        bank_oT = g.ps[:, 2, 0:NG * T].rearrange("p (r t) -> p r t", t=T)
        bank_out = g.ps[0:T, 2, NG * T:NG * T + D]
        scores = g.ps[0:T, 3:6, 0:HG * T].rearrange("p r (h t) -> p r h t", t=T)
        bank_pT = [g.ps[0:T, 6 + r % 2, 0:HG * T] for r in range(NG)]
        bank_rT = g.ps[:, 7, 0:NG * T].rearrange("p (r t) -> p r t", t=T)
        block = ctx.enter_context(nc.Block())

        @block.sync
        def _(sp):
            sp.dma_start(wqk[0:HALF, :, :], A["a0_wqk"][0:D, :].rearrange("(k p) n -> p k n", k=2)).then_inc(s_w, 16)
            sp.dma_start(wqk[HALF:HALF + 1, 1, :], A["a0_wqk"][D:D + 1, :]).then_inc(s_w, 16)
            sp.dma_start(wv[0:HALF, :, :], A["a0_wv"][0:D, :].rearrange("(k p) n -> p k n", k=2)).then_inc(s_w, 16)
            sp.dma_start(wv[HALF:HALF + 1, 1, :], A["a0_wv"][D:D + 1, :]).then_inc(s_w, 16)
            sp.dma_start(wo[:, :, :], A["a0_wo"].rearrange("(r p) n -> p r n", r=NG)).then_inc(s_w, 16)
            sp.dma_start(bo[:, :], A["a0_bo"].unsqueeze(0).broadcast_to([T, D])).then_inc(s_w, 16)
            sp.dma_start(hmask[:, :], A["head_mask"]).then_inc(s_w, 16)
            for gr in range(2):
                load_slots(sp, A, g, gr, gr)

        @block.gpsimd
        def _(pool):
            pool.memset(ones[:, :], 1.0).then_inc(s_ones, 1)
            pool.memset(vv[:, :, :, :], 0.0).then_inc(s_vset, 1)
            pool.wait_ge(s_ones, 1)
            pool.memset(xT[HALF:HALF + 1, :, 1, :], 1.0).then_inc(s_set, 1)
            pool.wait_ge(s_w, 7 * 16)

            def add_bias(b, i):
                item(pool, s_xn, b)
                hb = g.h[:, bass.ds(b, 1), :]
                pool.tensor_tensor(hb, hb, bo[:, :].unsqueeze(1), ALU.add).then_inc(s_bo, 1)

            def block_diagonal(b, i):
                item(pool, s_qks, b)
                reused(pool, s_sc, b, 2)
                k = i % 2
                for hf in range(2):
                    ins = pool.tensor_tensor(
                        kb[:, k, hf, :, :], qk[:, k, 2 + hf, :].unsqueeze(1).broadcast_to([HALF, HH, T]),
                        hmask[:, :].unsqueeze(2).broadcast_to([HALF, HH, T]), ALU.mult)
                ins.then_inc(s_kb, 1)

            def widen(b, i):
                item(pool, s_rs, b)
                reused(pool, s_rTp, b, 2)
                k = i % 2
                pool.tensor_tensor(rw[:, k, :, :], rs[:, k, :].unsqueeze(2).broadcast_to([T, NH, HPAD]),
                                   ones[:, :].unsqueeze(2).broadcast_to([T, NH, HPAD]), ALU.mult).then_inc(s_rw, 1)

            steps(pool, B, [(add_bias, 0), (widen, 3), (block_diagonal, 1)])

        @block.scalar
        def _(act):
            act.wait_ge(s_vset, 1)

            def x_copy(b, i):
                item(act, s_xTp, b)
                reused(act, s_vp, b, 2)
                act.activation(xT[0:HALF, i % 2, :, :],
                               bank_x[0:HALF, 0:2 * T].rearrange("p (k t) -> p k t", k=2), ACT.Copy).then_inc(s_xTs, 1)

            def qk_copy(b, i):
                item(act, s_qkp, b)
                reused(act, s_sc, b, 2)
                reused(act, s_kb, b, 2)
                act.activation(qk[:, i % 2, :, :], bank_qk, ACT.Copy).then_inc(s_qks, 1)

            def v_copy(b, i):
                item(act, s_vp, b)
                reused(act, s_oTp, b, 4)
                act.activation(vv[:, i, :, 0:DH],
                               bank_x[0:T, 2 * T:2 * T + D].rearrange("p (h d) -> p h d", d=DH), ACT.Copy).then_inc(s_vs, 1)

            def exponent(b, i):
                item(act, s_sub, b)
                act.activation(p[:, i % 2, :, :], p[:, i % 2, :, :], ACT.Exp, scale=DH ** -0.5).then_inc(s_exp, 1)

            def p_copy(b, i):
                for r in range(NG):
                    act.wait_ge(s_pTp, b * NG + r + 1)
                    reused(act, s_oTp, b, 1)
                    act.activation(pT[:, r, :, :], bank_pT[r].rearrange("p (h t) -> p h t", t=T),
                                   ACT.Copy).then_inc(s_pTs, 1)

            def r_copy(b, i):
                item(act, s_rTp, b)
                reused(act, s_oTs, b, 1)
                act.activation(rT[:, :, :], bank_rT, ACT.Copy).then_inc(s_rTs, 1)

            steps(act, B, [(exponent, 3), (qk_copy, 1), (v_copy, 1), (p_copy, 3), (x_copy, 0), (r_copy, 3)])
            layernorm_scale(None, act, g, s_ln)

        @block.vector
        def _(v):

            def norm_input(b, i):
                reused(v, s_xTp, b, 2)
                v.tensor_scalar(xn[:, i % 2, :].unsqueeze(1), g.h[:, bass.ds(b, 1), :], g.rstd[:, bass.ds(b, 1)],
                                g.nmr[:, bass.ds(b, 1)], ALU.mult, ALU.add).then_inc(s_xn, 1)

            def residual(b, i):
                item(v, s_op, b)
                item(v, s_bo, b)
                hb = g.h[:, bass.ds(b, 1), :]
                v.tensor_tensor(hb, bank_out.unsqueeze(1), hb, ALU.add).then_inc(s_res, 1)
                v.wait_ge(s_res, b + 1)
                v.bn_stats(g.stats[:, bass.ds(b, 1), :].rearrange("p a s -> p (a s)"),
                           hb.rearrange("p a d -> p (a d)")).then_inc(s_st, 1)

            def maximum(b, i):
                item(v, s_sc, b)
                v.tensor_reduce(mx[:, i % 2, :].rearrange("p (r h) -> p r h", r=NG), scores, AX.X, ALU.max).then_inc(s_mx, 1)

            def subtract(b, i):
                item(v, s_mx, b)
                reused(v, s_pTp, b, 2, NG)
                v.tensor_tensor(p[:, i % 2, :, :].rearrange("p (r h) t -> p r h t", r=NG), scores,
                                mx[:, i % 2, :].rearrange("p (r h) -> p r h", r=NG).unsqueeze(3).broadcast_to([T, NG, HG, T]),
                                ALU.subtract).then_inc(s_sub, 1)

            def row_sum(b, i):
                item(v, s_exp, b)
                v.tensor_reduce(sm[:, i % 2, :], p[:, i % 2, :, :], AX.X, ALU.add).then_inc(s_sum, 1)
                item(v, s_sum, b)
                v.reciprocal(rs[:, i % 2, :], sm[:, i % 2, :]).then_inc(s_rs, 1)

            def divide(b, i):
                item(v, s_oTp, b)
                item(v, s_rTs, b)
                reused(v, s_op, b, 1)
                v.tensor_tensor(oT[:, :, :], bank_oT, rT[:, :, :], ALU.mult).then_inc(s_oTs, 1)

            steps(v, B, [(divide, 4), (row_sum, 3), (residual, 5), (norm_input, 0), (maximum, 2), (subtract, 2)])
            v.wait_ge(s_st, B)
            layernorm_scale(v, None, g, s_ln)

        @block.tensor
        def _(pe):
            pe.wait_ge(g.s_const, 16)
            pe.wait_ge(s_w, 7 * 16)
            pe.wait_ge(s_set, 1)

            def transpose_x(b, i):
                item(pe, s_xn, b)
                reused(pe, s_vs, b, 1)
                for hf in range(2):
                    mm = pe.transpose(bank_x[0:HALF, hf * T:(hf + 1) * T], xn[:, i % 2, hf * HALF:(hf + 1) * HALF],
                                      g.ident[0:T, 0:T])
                mm.then_inc(s_xTp, 1)

            def project(b, i):
                item(pe, s_xTs, b)
                reused(pe, s_qks, b, 1)
                k = i % 2
                for m in range(4):
                    pe.matmul(bank_qk[:, m, :], wqk[0:HALF, 0, m * HALF:(m + 1) * HALF], xT[0:HALF, k, 0, :],
                              start=True, stop=False)
                    mm = pe.matmul(bank_qk[:, m, :], wqk[:, 1, m * HALF:(m + 1) * HALF], xT[:, k, 1, :],
                                   start=False, stop=True)
                mm.then_inc(s_qkp, 1)
                pe.matmul(bank_x[0:T, 2 * T:2 * T + D], xT[0:HALF, k, 0, :], wv[0:HALF, 0, :], start=True, stop=False)
                pe.matmul(bank_x[0:T, 2 * T:2 * T + D], xT[:, k, 1, :], wv[:, 1, :], start=False, stop=True).then_inc(s_vp, 1)

            def score(b, i):
                item(pe, s_kb, b)
                reused(pe, s_sub, b, 1)
                k = i % 2
                q = [qk[:, k, hf, :] for hf in range(2)]
                for hf, h0, n, r, c in ((0, 0, 4, 0, 0), (0, 4, 2, 1, 0), (1, 0, 2, 1, 2), (1, 2, 4, 2, 0)):
                    mm = pe.matmul(g.ps[0:T, 3 + r, c * T:(c + n) * T], q[hf],
                                   kb[:, k, hf, h0:h0 + n, :].rearrange("p h t -> p (h t)"), start=True, stop=True)
                mm.then_inc(s_sc, 1)

            def attend(b, i):
                item(pe, s_exp, b)
                item(pe, s_vs, b)

                def turn(r):
                    if r == 2:
                        pe.wait_ge(s_pTs, b * NG + 1)
                    elif r == 0:
                        reused(pe, s_pTs, b, 1, NG)
                    else:
                        reused(pe, s_rTs, b, 1)
                    for j in range(HG):
                        mm = pe.transpose(bank_pT[r][:, j * T:(j + 1) * T], p[:, i % 2, r * HG + j, :], g.ident[0:T, 0:T])
                    mm.then_inc(s_pTp, 1)

                def values(r):
                    pe.wait_ge(s_pTs, b * NG + r + 1)
                    for j in range(HG):
                        mm = pe.matmul(bank_oT[HPAD * j:HPAD * (j + 1), r, :], vv[:, i, r * HG + j, :], pT[:, r, j, :],
                                       start=True, stop=True, tile_position=(0, HPAD * j))
                    return mm

                turn(0)
                turn(1)
                reused(pe, s_res, b, 2)
                reused(pe, s_oTs, b, 1)
                values(0)
                turn(2)
                pe.wait_ge(s_rw, b + 1)
                pe.wait_ge(s_pTs, b * NG + 2)
                for r in range(NG):
                    mm = pe.transpose(bank_rT[:, r, :], rw[:, i % 2, r * HG:(r + 1) * HG, :].rearrange("p h w -> p (h w)"),
                                      g.ident[0:T, 0:T])
                mm.then_inc(s_rTp, 1)
                values(1)
                values(2).then_inc(s_oTp, 1)

            def output(b, i):
                item(pe, s_oTs, b)
                reused(pe, s_res, b, 1)
                for r in range(NG):
                    mm = pe.matmul(bank_out, oT[:, r, :], wo[:, r, :], start=(r == 0), stop=(r == NG - 1))
                mm.then_inc(s_op, 1)

            steps(pe, B, [(project, 1), (score, 2), (transpose_x, 0), (attend, 3), (output, 4)])


def soft_moe(nc, A, g):
    with ExitStack() as ctx:
        def sb(name, shape, dt=F32):
            return ctx.enter_context(nc.sbuf_tensor("m_" + name, shape, dt))

        g.yT = sb("yT", [HALF, 2, NS, B])
        g.combT = sb("combT", [NS, B, T])
        with ExitStack() as inner:
            g.zw = inner.enter_context(nc.sbuf_tensor("m_zw", [T, B, D], F32))
            g.r1 = inner.enter_context(nc.sbuf_tensor("m_r1", [T, B], F32))
            g.rn = inner.enter_context(nc.sbuf_tensor("m_rn", [T, B], F32))
            g.slT = inner.enter_context(nc.sbuf_tensor("m_slT", [HALF, 2, NS], F32))
            rms_inputs(nc, A, g)
            dispatch(nc, A, g)
        g.y2 = sb("y2", [NS, B, D])
        slot_ffn(nc, A, g)
        combine(nc, A, g)


def rms_inputs(nc, A, g):
    with ExitStack() as ctx:
        def sem(name):
            return g.phase_sem("r_" + name)

        def sb(name, shape, dt=F32):
            return ctx.enter_context(nc.sbuf_tensor("r_" + name, shape, dt))

        nw = sb("nw", [T, D])
        z = sb("z", [T, UNROLL, D])
        junk = sb("junk", [T, UNROLL, D])
        ss = sb("ss", [T, B])
        root = sb("root", [T, 2, B])
        t_ms = sb("t_ms", [T, B])
        sl = sb("sl", [NS, D])
        sl_junk = sb("sl_junk", [NS, D])
        sl_scale = sb("sl_scale", [NS, 1])
        sl_ss = sb("sl_ss", [NS, 4])
        s_w, s_z, s_zw, s_sq, s_ms, s_root, s_c, s_sl, s_slss, s_slroot, s_slT = (
            sem(n) for n in ("w", "z", "zw", "sq", "ms", "root", "c", "sl", "slss", "slroot", "slT"))
        slT_ps = g.ps[0:HALF, 0, 0:2 * NS].rearrange("p (k s) -> p k s", k=2)
        block = ctx.enter_context(nc.Block())

        @block.sync
        def _(sp):
            sp.dma_start(nw[:, :], A["norm_w"].unsqueeze(0).broadcast_to([T, D])).then_inc(s_w, 16)
            sp.dma_start(sl[:, :], A["slots"]).then_inc(s_w, 16)
            sp.dma_start(sl_scale[:, :], A["slot_scale"].unsqueeze(1)).then_inc(s_w, 16)

        @block.vector
        def _(v):
            with v.Fori(0, B // UNROLL) as j:
                for u in range(UNROLL):
                    b = j * UNROLL + u
                    if u == 0:
                        v.wait_ge(s_zw, j * UNROLL + UNROLL)
                    v.tensor_scalar(z[:, u, :].unsqueeze(1), g.h[:, bass.ds(b, 1), :], g.rstd[:, bass.ds(b, 1)],
                                    g.nmr[:, bass.ds(b, 1)], ALU.mult, ALU.add).then_inc(s_z, 1)
            v.tensor_tensor(t_ms[:, :], g.rstd[:, :], g.rstd[:, :], ALU.mult).then_inc(s_c, 1)
            v.wait_ge(s_c, 1)
            v.tensor_scalar(t_ms[:, :], t_ms[:, :], -EPS, 1.0 + EPS, ALU.mult, ALU.add).then_inc(s_ms, 1)
            v.wait_ge(s_slroot, 1)
            v.tensor_scalar(sl_ss[:, 2:3], sl_ss[:, 1:2], EPS, None, ALU.max).then_inc(s_c, 1)
            v.wait_ge(s_c, 2)
            v.reciprocal(sl_ss[:, 3:4], sl_ss[:, 2:3]).then_inc(s_c, 1)
            v.wait_ge(s_c, 3)
            v.tensor_scalar(sl[:, :], sl[:, :], sl_ss[:, 3:4], sl_scale[:, 0:1], ALU.mult, ALU.mult).then_inc(s_sl, 1)
            v.wait_ge(s_root, 2)
            v.reciprocal(g.r1[:, :], root[:, 0, :]).then_inc(s_c, 1)
            v.wait_ge(s_c, 4)
            v.tensor_tensor(ss[:, :], g.r1[:, :], root[:, 1, :], ALU.mult).then_inc(s_c, 1)
            v.wait_ge(s_c, 5)
            v.tensor_scalar(ss[:, :], ss[:, :], EPS, None, ALU.max).then_inc(s_c, 1)
            v.wait_ge(s_c, 6)
            v.reciprocal(g.rn[:, :], ss[:, :])
            v.wait_ge(s_slT, 1)
            v.tensor_copy(g.slT[:, :, :], slT_ps)

        @block.gpsimd
        def _(pool):
            pool.sem_inc(s_zw, UNROLL)
            pool.wait_ge(s_w, 48)
            with pool.Fori(0, B // UNROLL) as j:
                for u in range(UNROLL):
                    b = j * UNROLL + u
                    item(pool, s_z, b)
                    pool.tensor_tensor(g.zw[:, bass.ds(b, 1), :], z[:, u, :].unsqueeze(1),
                                       nw[:, :].unsqueeze(1), ALU.mult).then_inc(s_zw, 1)

        @block.scalar
        def _(act):
            act.wait_ge(s_w, 48)
            act.activation(sl_junk[:, :], sl[:, :], ACT.Square, accum_out=sl_ss[:, 0:1]).then_inc(s_slss, 1)
            act.wait_ge(s_slss, 1)
            act.activation(sl_ss[:, 1:2], sl_ss[:, 0:1], ACT.Sqrt).then_inc(s_slroot, 1)

            def square(b, i):
                act.wait_ge(s_zw, b + 1 + UNROLL)
                reused(act, s_sq, b, UNROLL)
                act.activation(junk[:, i, :].unsqueeze(1), g.zw[:, bass.ds(b, 1), :], ACT.Square,
                               accum_out=ss[:, bass.ds(b, 1)]).then_inc(s_sq, 1)

            steps(act, B, [(square, 0)])
            act.wait_ge(s_sq, B)
            act.wait_ge(s_ms, 1)
            act.activation(root[:, 0, :], t_ms[:, :], ACT.Sqrt).then_inc(s_root, 1)
            act.activation(root[:, 1, :], ss[:, :], ACT.Sqrt).then_inc(s_root, 1)

        @block.tensor
        def _(pe):
            pe.wait_ge(s_sl, 1)
            for k in range(2):
                mm = pe.transpose(slT_ps[:, k, :], sl[:, k * HALF:(k + 1) * HALF], g.ident[0:NS, 0:NS])
            mm.then_inc(s_slT, 1)


def dispatch(nc, A, g):
    NP = B // 2
    with ExitStack() as ctx:
        def sem(name):
            return g.phase_sem("d_" + name)

        def sb(name, shape, dt=F32):
            return ctx.enter_context(nc.sbuf_tensor("d_" + name, shape, dt))

        xn = sb("xn", [T, 4, 2, D])
        xT = sb("xT", [HALF, 2, 2, 2, T])
        lg = sb("lg", [T, 2, 2, NS])
        cm = sb("cm", [T, 4, 2, NS])
        dm = sb("dm", [NS, 4, 2, T])
        dT = sb("dT", [T, 2, 2, NS])
        cs = sb("cs", [T, 2, 3, 2])
        dsm = sb("dsm", [NS, 2, 3, 2])
        (s_xn, s_xTp, s_xTs, s_lgp, s_lg, s_lgT, s_cmx, s_csub, s_cexp, s_csum, s_crs, s_c, s_dmx, s_dsub, s_dexp,
         s_dsum, s_drs, s_d, s_tp, s_dTs, s_cTs, s_yp, s_ys) = (sem(n) for n in (
             "xn", "xTp", "xTs", "lgp", "lg", "lgT", "cmx", "csub", "cexp", "csum", "crs", "c", "dmx", "dsub", "dexp",
             "dsum", "drs", "d", "tp", "dTs", "cTs", "yp", "ys"))
        b_x = g.ps[0:HALF, 0, 0:4 * T].rearrange("p (b k t) -> p b k t", b=2, k=2)
        b_lg = g.ps[0:T, 1, 0:2 * NS].rearrange("p (b s) -> p b s", b=2)
        b_lgT = g.ps[0:NS, 2, 0:2 * T].rearrange("p (b t) -> p b t", b=2)
        b_dT = g.ps[0:T, 3, 0:2 * NS].rearrange("p (b s) -> p b s", b=2)
        b_cT = g.ps[0:NS, 4, 0:2 * T].rearrange("p (b t) -> p b t", b=2)
        b_y = g.ps[0:HALF, 5, 0:4 * NS].rearrange("p (b k s) -> p b k s", b=2, k=2)
        block = ctx.enter_context(nc.Block())

        def wide(small, n):
            return small.unsqueeze(2).broadcast_to([small.shape[0], 2, n])

        @block.vector
        def _(v):
            def scale_x(q, i):
                reused(v, s_yp, q, 4)
                pair = bass.ds(q * 2, 2)
                v.tensor_tensor(xn[:, i, :, :], g.zw[:, pair, :], wide(g.r1[:, pair], D), ALU.mult).then_inc(s_xn, 1)

            def combine_max(q, i):
                k = i % 2
                item(v, s_lgp, q)
                reused(v, s_lgT, q, 2)
                v.tensor_tensor(lg[:, k, :, :], b_lg, wide(g.rn[:, bass.ds(q * 2, 2)], NS), ALU.mult).then_inc(s_lg, 1)
                item(v, s_lg, q)
                v.tensor_reduce(cs[:, k, 0, :], lg[:, k, :, :], AX.X, ALU.max).then_inc(s_cmx, 1)
                item(v, s_cmx, q)
                reused(v, s_tp, q, 4)
                v.tensor_tensor(cm[:, i, :, :], lg[:, k, :, :], wide(cs[:, k, 0, :], NS), ALU.subtract).then_inc(s_csub, 1)

            def dispatch_max(q, i):
                k = i % 2
                item(v, s_lgT, q)
                v.tensor_reduce(dsm[:, k, 0, :], b_lgT, AX.X, ALU.max).then_inc(s_dmx, 1)
                item(v, s_dmx, q)
                reused(v, s_tp, q, 4)
                v.tensor_tensor(dm[:, i, :, :], b_lgT, wide(dsm[:, k, 0, :], T), ALU.subtract).then_inc(s_dsub, 1)

            def combine_sum(q, i):
                k = i % 2
                item(v, s_cexp, q)
                v.tensor_reduce(cs[:, k, 1, :], cm[:, i, :, :], AX.X, ALU.add).then_inc(s_csum, 1)
                item(v, s_csum, q)
                v.reciprocal(cs[:, k, 2, :], cs[:, k, 1, :]).then_inc(s_crs, 1)

            def dispatch_sum(q, i):
                k = i % 2
                item(v, s_dexp, q)
                v.tensor_reduce(dsm[:, k, 1, :], dm[:, i, :, :], AX.X, ALU.add).then_inc(s_dsum, 1)
                item(v, s_dsum, q)
                v.reciprocal(dsm[:, k, 2, :], dsm[:, k, 1, :]).then_inc(s_drs, 1)

            steps(v, NP, [(scale_x, 0), (dispatch_max, 2), (combine_max, 1), (dispatch_sum, 2), (combine_sum, 1)])

        @block.gpsimd
        def _(pool):
            def scale_c(q, i):
                item(pool, s_crs, q)
                pool.tensor_tensor(cm[:, i, :, :], cm[:, i, :, :], wide(cs[:, i % 2, 2, :], NS), ALU.mult).then_inc(s_c, 1)

            def scale_d(q, i):
                item(pool, s_drs, q)
                pool.tensor_tensor(dm[:, i, :, :], dm[:, i, :, :], wide(dsm[:, i % 2, 2, :], T), ALU.mult).then_inc(s_d, 1)

            steps(pool, NP, [(scale_d, 2), (scale_c, 1)])

        @block.scalar
        def _(act):
            def x_copy(q, i):
                item(act, s_xTp, q)
                reused(act, s_lgp, q, 2)
                act.activation(xT[:, i % 2, :, :, :], b_x, ACT.Copy).then_inc(s_xTs, 1)

            def combine_exp(q, i):
                item(act, s_csub, q)
                act.activation(cm[:, i, :, :], cm[:, i, :, :], ACT.Exp).then_inc(s_cexp, 1)

            def dispatch_exp(q, i):
                item(act, s_dsub, q)
                act.activation(dm[:, i, :, :], dm[:, i, :, :], ACT.Exp).then_inc(s_dexp, 1)

            def turn_copy(q, i):
                item(act, s_tp, q)
                reused(act, s_yp, q, 2)
                act.activation(dT[:, i % 2, :, :], b_dT, ACT.Copy).then_inc(s_dTs, 1)
                act.activation(g.combT[:, bass.ds(q * 2, 2), :], b_cT, ACT.Copy).then_inc(s_cTs, 1)

            def y_copy(q, i):
                item(act, s_yp, q)
                act.activation(g.yT[:, :, :, bass.ds(q * 2, 2)].rearrange("p k s b -> p b k s"), b_y,
                               ACT.Copy).then_inc(s_ys, 1)

            steps(act, NP, [(x_copy, 1), (y_copy, 4), (turn_copy, 3), (dispatch_exp, 2), (combine_exp, 1)])

        @block.tensor
        def _(pe):
            def transpose_x(q, i):
                item(pe, s_xn, q)
                reused(pe, s_xTs, q, 1)
                for b in range(2):
                    for k in range(2):
                        mm = pe.transpose(b_x[:, b, k, :], xn[:, i, b, k * HALF:(k + 1) * HALF], g.ident[0:T, 0:T])
                mm.then_inc(s_xTp, 1)

            def logits(q, i):
                item(pe, s_xTs, q)
                reused(pe, s_lg, q, 1)
                for b in range(2):
                    for k in range(2):
                        mm = pe.matmul(b_lg[:, b, :], xT[:, i % 2, b, k, :], g.slT[:, k, :], start=(k == 0), stop=(k == 1))
                mm.then_inc(s_lgp, 1)

            def logits_ready(q, i):
                item(pe, s_lg, q)
                reused(pe, s_dsub, q, 1)

            def transpose_logits(q, i):
                for b in range(2):
                    mm = pe.transpose(b_lgT[:, b, :], lg[:, i % 2, b, :], g.ident[0:T, 0:T])
                mm.then_inc(s_lgT, 1)

            def weights_ready(q, i):
                item(pe, s_c, q)
                item(pe, s_d, q)
                reused(pe, s_dTs, q, 1)
                reused(pe, s_cTs, q, 1)

            def transpose_weights(q, i):
                for b in range(2):
                    pe.transpose(b_dT[:, b, :], dm[:, i, b, :], g.ident[0:NS, 0:NS])
                    mm = pe.transpose(b_cT[:, b, :], cm[:, i, b, :], g.ident[0:T, 0:T])
                mm.then_inc(s_tp, 1)

            def gather(q, i):
                item(pe, s_dTs, q)
                reused(pe, s_ys, q, 1)
                for b in range(2):
                    for k in range(2):
                        mm = pe.matmul(b_y[:, b, k, :], xn[:, i, b, k * HALF:(k + 1) * HALF], dT[:, i % 2, b, :],
                                       start=True, stop=True)
                mm.then_inc(s_yp, 1)

            steps(pe, NP, [(gather, 4), (logits_ready, 2), (transpose_x, 1), (transpose_logits, 2),
                           (weights_ready, 3), (logits, 1), (transpose_weights, 3)])


def slot_ffn(nc, A, g):
    with ExitStack() as ctx:
        def sem(name):
            return g.phase_sem("f_" + name)

        def sb(name, shape, dt=F32):
            return ctx.enter_context(nc.sbuf_tensor("f_" + name, shape, dt))

        yg = sb("yg", [HALF + 1, 2, 2, GS, B])
        hid = sb("hid", [128, 2, F])
        hT = sb("hT", [128, 2, FC, 128])
        b2 = sb("b2", [128, NGR, D])
        y2g = sb("y2g", [128, 2, D])
        s_b2, s_one, s_yg, s_h1, s_gelu, s_hTp, s_hTs, s_y2p, s_y2s = (
            sem(n) for n in ("b2", "one", "yg", "h1", "gelu", "hTp", "hTs", "y2p", "y2s"))
        s_y2 = [sem(f"y2_{i}") for i in range(2)]
        N2 = F // 2
        block = ctx.enter_context(nc.Block())

        @block.sync
        def _(sp):
            bias = A["fc2_b"].rearrange("(g s) d -> s g d", s=GS)
            for s in range(GS):
                sp.dma_start(b2[B * s:B * (s + 1), :, :], bias[s].unsqueeze(0).broadcast_to([B, NGR, D])).then_inc(s_b2, 16)
            with sp.Fori(1, NGR // 2) as j:
                for u in range(2):
                    load_slots(sp, A, g, j * 2 + u, u, lambda: sp.wait_ge(s_h1, j * 2 + (u - 1)),
                               lambda: sp.wait_ge(s_y2p, j * 2 + (u - 1)))

        @block.gpsimd
        def _(pool):
            pool.memset(yg[HALF:HALF + 1, :, 1, :, :], 1.0).then_inc(s_one, 1)

            def pick(gr, i):
                reused(pool, s_h1, gr, 2)
                pool.tensor_copy(yg[0:HALF, i, :, :, :], g.yT[:, :, bass.ds(gr * GS, GS), :]).then_inc(s_yg, 1)

            steps(pool, NGR, [(pick, 0)], unroll=2, depth=2)

        @block.scalar
        def _(act):
            def gelu(gr, i):
                reused(act, s_hTp, gr, 2, 2)
                for n in range(2):
                    act.wait_ge(s_h1, gr + 1)
                    act.activation(hid[:, i, n * N2:(n + 1) * N2], g.ps[:, n, 0:N2], ACT.Gelu).then_inc(s_gelu, 1)

            def put(gr, i):
                item(act, s_y2s, gr)
                act.dma_start(g.y2[gr * GS:(gr + 1) * GS, :, :], y2g[:, i, :]).then_inc(s_y2[i], 16)

            for t in range(NGR + 1):
                if t < NGR:
                    gelu(t, t % 2)
                if t >= 1:
                    put(t - 1, (t - 1) % 2)
            for i in range(2):
                act.wait_ge(s_y2[i], 16 * NGR // 2)

        @block.vector
        def _(v):
            v.wait_ge(s_b2, 16 * GS)

            def turn_copy(gr, i):
                reused(v, s_y2p, gr, 2)
                for n in range(2):
                    v.wait_ge(s_hTp, gr * 2 + n + 1)
                    v.tensor_copy(hT[:, i, 3 * n:3 * n + 3, :], g.ps[:, 2 + n, 0:384].rearrange("p (k m) -> p k m", k=3)).then_inc(s_hTs, 1)

            def add_bias(gr, i):
                item(v, s_y2p, gr)
                if not isinstance(gr, int):
                    v.wait_ge(s_y2[i], (gr - i) * 8)
                elif gr >= 2:
                    v.wait_ge(s_y2[i], 16 * (gr // 2))
                v.tensor_tensor(y2g[:, i, :].unsqueeze(1), g.ps[:, 4, 0:D].unsqueeze(1),
                                b2[:, bass.ds(gr, 1), :], ALU.add).then_inc(s_y2s, 1)

            steps(v, NGR, [(turn_copy, 1), (add_bias, 1)], unroll=2, depth=2)

        @block.tensor
        def _(pe):
            pe.wait_ge(s_one, 1)

            def loaded(sems, gr, i, dmas):
                if isinstance(gr, int):
                    pe.wait_ge(sems[i], 16 * dmas * (gr // 2 + 1))
                else:
                    pe.wait_ge(sems[i], (gr - i) * (8 * dmas) + 16 * dmas)

            def first(gr, i):
                item(pe, s_yg, gr)
                loaded(g.s_w1, gr, i, W1_DMAS)
                reused(pe, s_gelu, gr, 1, 2)
                for n in range(2):
                    for k in range(2):
                        rows = HALF + k
                        for s in range(GS):
                            mm = pe.matmul(g.ps[B * s:B * (s + 1), n, 0:N2], yg[0:rows, i, k, s, :],
                                           g.w1[0:rows, i, k, s, n * N2:(n + 1) * N2],
                                           start=(k == 0), stop=(k == 1), tile_position=(0, B * s))
                mm.then_inc(s_h1, 1)

            def turn(gr, i):
                item(pe, s_gelu, gr, 2)
                for n in range(2):
                    if not isinstance(gr, int) or gr >= 1:
                        pe.wait_ge(s_hTs, gr * 2 + n - 1)
                    for k in range(3):
                        mm = pe.transpose(g.ps[:, 2 + n, 128 * k:128 * (k + 1)], hid[:, i, 3 * n + k:F:FC], g.ident[:, :])
                    mm.then_inc(s_hTp, 1)

            def second(gr, i):
                item(pe, s_hTs, gr, 2)
                loaded(g.s_w2, gr, i, 1)
                reused(pe, s_y2s, gr, 1)
                for k in range(FC):
                    for s in range(GS):
                        mm = pe.matmul(g.ps[B * s:B * (s + 1), 4, 0:D], hT[:, i, k, B * s:B * (s + 1)],
                                       g.w2[:, i, s, k * D:(k + 1) * D], start=(k == 0), stop=(k == FC - 1),
                                       tile_position=(0, B * s))
                mm.then_inc(s_y2p, 1)

            steps(pe, NGR, [(turn, 1), (first, 0), (second, 1)], unroll=2, depth=2)


def combine(nc, A, g):
    with ExitStack() as ctx:
        def sem(name):
            return g.phase_sem("c_" + name)

        cT = ctx.enter_context(nc.sbuf_tensor("c_cT", [NS, UNROLL, T], F32))
        s_cT, s_mm, s_res, s_st, s_ln = (sem(n) for n in ("cT", "mm", "res", "st", "ln"))
        block = ctx.enter_context(nc.Block())

        @block.gpsimd
        def _(pool):
            def pick(b, i):
                reused(pool, s_mm, b, 4)
                pool.tensor_copy(cT[:, i, :].unsqueeze(1), g.combT[:, bass.ds(b, 1), :]).then_inc(s_cT, 1)

            steps(pool, B, [(pick, 0)])

        @block.tensor
        def _(pe):
            def mix(b, i):
                item(pe, s_cT, b)
                reused(pe, s_res, b, 4)
                pe.matmul(g.ps[0:T, i, 0:D], cT[:, i, :], g.y2[:, bass.ds(b, 1), :].rearrange("p a d -> p (a d)"),
                          start=True, stop=True).then_inc(s_mm, 1)

            steps(pe, B, [(mix, 0)])

        @block.vector
        def _(v):
            def residual(b, i):
                item(v, s_mm, b)
                hb = g.h[:, bass.ds(b, 1), :]
                v.tensor_tensor(hb, g.ps[0:T, i, 0:D].unsqueeze(1), hb, ALU.add).then_inc(s_res, 1)

            def statistics(b, i):
                item(v, s_res, b)
                v.bn_stats(g.stats[:, bass.ds(b, 1), :].rearrange("p a s -> p (a s)"),
                           g.h[:, bass.ds(b, 1), :].rearrange("p a d -> p (a d)")).then_inc(s_st, 1)

            steps(v, B, [(residual, 0), (statistics, 1)])
            v.wait_ge(s_st, B)
            layernorm_scale(v, None, g, s_ln)

        @block.scalar
        def _(act):
            layernorm_scale(None, act, g, s_ln)


def attention1(nc, A, g):
    with ExitStack() as ctx:
        def sem(name):
            return g.phase_sem("b_" + name)

        def sb(name, shape, dt=F32):
            return ctx.enter_context(nc.sbuf_tensor("b_" + name, shape, dt))

        wqkv = sb("wqkv", [HALF, 2, 3 * D])
        cos = sb("cos", [T, 2 * D])
        sin = sb("sin", [T, D])
        nsin = sb("nsin", [T, D])
        mask = sb("mask", [T, T])
        xn = sb("xn", [T, 2, D])
        xT = sb("xT", [HALF, 2, 2, T])
        vv = sb("vv", [T, 4, D])
        ra = sb("ra", [T, 2, 2 * D])
        rb = sb("rb", [T, 2, 2 * D])
        qkT = sb("qkT", [HALF, 2, 4, T])
        p = sb("p", [T, 2, T])
        pT = sb("pT", [T, 2, T])
        sc = sb("sc", [T, 4, 4])
        (s_w, s_xn, s_xTp, s_xTs, s_qk, s_v, s_vs, s_ra, s_rot, s_rTp, s_rTs, s_sc, s_msk, s_mx, s_nm, s_exp, s_rs,
         s_pTp, s_pTs, s_o, s_res, s_st, s_ln) = (sem(n) for n in (
             "w", "xn", "xTp", "xTs", "qk", "v", "vs", "ra", "rot", "rTp", "rTs", "sc", "msk", "mx", "nm", "exp", "rs",
             "pTp", "pTs", "o", "res", "st", "ln"))
        b_x = g.ps[0:HALF, 0, 0:2 * T].rearrange("p (k t) -> p k t", k=2)
        b_qk = g.ps[0:T, 1, 0:2 * D]
        b_v = g.ps[0:T, 2, 0:D]
        b_rT = g.ps[0:HALF, 3, 0:4 * T].rearrange("p (m t) -> p m t", m=4)
        b_sc = g.ps[0:T, 4, 0:T]
        b_pT = g.ps[0:T, 5, 0:T]
        b_o = g.ps[0:T, 6, 0:D]
        SCALE = D ** -0.5
        block = ctx.enter_context(nc.Block())

        @block.sync
        def _(sp):
            sp.dma_start(wqkv[:, :, :], A["a1_wqkv"].rearrange("(k p) n -> p k n", k=2)).then_inc(s_w, 16)
            sp.dma_start(cos[:, :], A["rope_cos"]).then_inc(s_w, 16)
            sp.dma_start(sin[:, :], A["rope_sin"]).then_inc(s_w, 16)
            sp.dma_start(nsin[:, :], A["rope_nsin"]).then_inc(s_w, 16)
            sp.dma_start(mask[:, :], A["causal"]).then_inc(s_w, 16)
            for k in range(2):
                sp.dma_start(g.e1[0:HALF, k, :, :], A["moe_w1"][:, k * HALF:(k + 1) * HALF, :].rearrange(
                    "e p n -> p e n")).then_inc(g.s_e, 16)
            sp.dma_start(g.e1[HALF:HALF + 1, 1, :, :], A["moe_b1"].unsqueeze(0)).then_inc(g.s_e, 16)
            sp.dma_start(g.e2[:, :, :], A["moe_w2"].rearrange("e (p k) n -> p e (k n)", k=FC)).then_inc(g.s_e, 16)

        @block.vector
        def _(v):
            v.wait_ge(s_w, 5 * 16)

            def norm_input(b, i):
                reused(v, s_xTp, b, 2)
                v.tensor_scalar(xn[:, i % 2, :].unsqueeze(1), g.h[:, bass.ds(b, 1), :], g.rstd[:, bass.ds(b, 1)],
                                g.nmr[:, bass.ds(b, 1)], ALU.mult, ALU.add).then_inc(s_xn, 1)

            def rotate(b, i):
                k = i % 2
                item(v, s_qk, b)
                reused(v, s_rTp, b, 2)
                pair = b_qk.rearrange("p (n two) -> p n two", two=2)
                out = rb[:, k, :].rearrange("p (n two) -> p n two", two=2)
                v.tensor_tensor(ra[:, k, :], b_qk, cos[:, :], ALU.mult)
                v.tensor_tensor(out[:, :, 0], pair[:, :, 1], nsin[:, :], ALU.mult)
                v.tensor_tensor(out[:, :, 1], pair[:, :, 0], sin[:, :], ALU.mult).then_inc(s_ra, 1)

            def soften(b, i):
                k = i % 2
                item(v, s_sc, b)
                reused(v, s_pTp, b, 2)
                v.tensor_tensor(p[:, k, :], b_sc, mask[:, :], ALU.add).then_inc(s_msk, 1)
                item(v, s_msk, b)
                v.tensor_reduce(sc[:, i, 0:1], p[:, k, :], AX.X, ALU.max).then_inc(s_mx, 1)
                item(v, s_mx, b)
                v.tensor_scalar(sc[:, i, 1:2], sc[:, i, 0:1], -SCALE, None, ALU.mult).then_inc(s_nm, 1)

            def inverse(b, i):
                item(v, s_exp, b)
                v.reciprocal(sc[:, i, 3:4], sc[:, i, 2:3]).then_inc(s_rs, 1)

            def residual(b, i):
                item(v, s_rs, b)
                item(v, s_o, b)
                hb = g.h[:, bass.ds(b, 1), :]
                v.scalar_tensor_tensor(hb, b_o.unsqueeze(1), sc[:, i, 3:4], hb, ALU.mult, ALU.add).then_inc(s_res, 1)

            def statistics(b, i):
                item(v, s_res, b)
                v.bn_stats(g.stats[:, bass.ds(b, 1), :].rearrange("p a s -> p (a s)"),
                           g.h[:, bass.ds(b, 1), :].rearrange("p a d -> p (a d)")).then_inc(s_st, 1)

            steps(v, B, [(inverse, 3), (residual, 4), (norm_input, 0), (statistics, 4), (rotate, 1), (soften, 2)])
            v.wait_ge(s_st, B)
            layernorm_scale(v, None, g, s_ln)

        @block.gpsimd
        def _(pool):
            def add_parts(b, i):
                k = i % 2
                item(pool, s_ra, b)
                pool.tensor_tensor(ra[:, k, :], ra[:, k, :], rb[:, k, :], ALU.add).then_inc(s_rot, 1)

            steps(pool, B, [(add_parts, 1)])

        @block.scalar
        def _(act):
            def x_copy(b, i):
                item(act, s_xTp, b)
                reused(act, s_v, b, 2)
                act.activation(xT[:, i % 2, :, :], b_x, ACT.Copy).then_inc(s_xTs, 1)

            def r_copy(b, i):
                item(act, s_rTp, b)
                reused(act, s_sc, b, 2)
                act.activation(qkT[:, i % 2, :, :], b_rT, ACT.Copy).then_inc(s_rTs, 1)

            def p_copy(b, i):
                item(act, s_pTp, b)
                reused(act, s_o, b, 2)
                act.activation(pT[:, i % 2, :], b_pT, ACT.Copy).then_inc(s_pTs, 1)

            def v_copy(b, i):
                item(act, s_v, b)
                reused(act, s_o, b, 4)
                act.activation(vv[:, i, :], b_v, ACT.Copy).then_inc(s_vs, 1)

            def exponent(b, i):
                item(act, s_nm, b)
                reused(act, s_res, b, 4)
                act.activation(p[:, i % 2, :], p[:, i % 2, :], ACT.Exp, scale=SCALE, bias=sc[:, i, 1:2],
                               accum_out=sc[:, i, 2:3]).then_inc(s_exp, 1)

            steps(act, B, [(x_copy, 1), (r_copy, 2), (p_copy, 3), (v_copy, 1), (exponent, 2)])
            layernorm_scale(None, act, g, s_ln)

        @block.tensor
        def _(pe):
            pe.wait_ge(s_w, 5 * 16)

            def transpose_x(b, i):
                item(pe, s_xn, b)
                reused(pe, s_xTs, b, 1)
                for k in range(2):
                    mm = pe.transpose(b_x[:, k, :], xn[:, i % 2, k * HALF:(k + 1) * HALF], g.ident[0:T, 0:T])
                mm.then_inc(s_xTp, 1)

            def transpose_qk(b, i):
                item(pe, s_rot, b)
                reused(pe, s_rTs, b, 1)
                for m in range(4):
                    mm = pe.transpose(b_rT[:, m, :], ra[:, i % 2, m * HALF:(m + 1) * HALF], g.ident[0:T, 0:T])
                mm.then_inc(s_rTp, 1)

            def transpose_p(b, i):
                item(pe, s_exp, b)
                reused(pe, s_pTs, b, 1)
                pe.transpose(b_pT, p[:, i % 2, :], g.ident[0:T, 0:T]).then_inc(s_pTp, 1)

            def project(b, i):
                item(pe, s_xTs, b)
                reused(pe, s_ra, b, 1)
                reused(pe, s_vs, b, 1)
                for k in range(2):
                    mm = pe.matmul(b_qk, xT[:, i % 2, k, :], wqkv[:, k, 0:2 * D], start=(k == 0), stop=(k == 1))
                mm.then_inc(s_qk, 1)
                for k in range(2):
                    mm = pe.matmul(b_v, xT[:, i % 2, k, :], wqkv[:, k, 2 * D:3 * D], start=(k == 0), stop=(k == 1))
                mm.then_inc(s_v, 1)

            def score(b, i):
                item(pe, s_rTs, b)
                reused(pe, s_msk, b, 1)
                for k in range(2):
                    mm = pe.matmul(b_sc, qkT[:, i % 2, k, :], qkT[:, i % 2, 2 + k, :], start=(k == 0), stop=(k == 1))
                mm.then_inc(s_sc, 1)

            def attend(b, i):
                item(pe, s_pTs, b)
                item(pe, s_vs, b)
                reused(pe, s_res, b, 1)
                pe.matmul(b_o, pT[:, i % 2, :], vv[:, i, :], start=True, stop=True).then_inc(s_o, 1)

            steps(pe, B, [(transpose_x, 1), (transpose_qk, 2), (transpose_p, 3), (project, 1), (score, 2), (attend, 3)])


def routed_moe(nc, A, g):
    with ExitStack() as ctx:
        g.idx = ctx.enter_context(nc.sbuf_tensor("t_idx", [128, NTILES], mybir.dt.uint32))
        g.cw = ctx.enter_context(nc.sbuf_tensor("t_cw", [128, NTILES], F32))
        g.te = ctx.enter_context(nc.sbuf_tensor("t_te", [128, NTILES], mybir.dt.int32))
        with ExitStack() as inner:
            g.lg = inner.enter_context(nc.sbuf_tensor("t_lg", [T, B, NE], F32))
            gate(nc, A, g)
            route(nc, A, g)
        expert_tiles(nc, A, g)


def gate(nc, A, g):
    with ExitStack() as ctx:
        def sem(name):
            return g.phase_sem("g_" + name)

        def sb(name, shape, dt=F32):
            return ctx.enter_context(nc.sbuf_tensor("g_" + name, shape, dt))

        wr = sb("wr", [HALF, 2, NE])
        xn = sb("xn", [T, UNROLL, D])
        xT = sb("xT", [HALF, 2, 2, T])
        zero = sb("zero", [128, D])
        s_w, s_zero, s_tab, s_xn, s_xTp, s_xTs, s_lgp, s_lgs = (
            sem(n) for n in ("w", "zero", "tab", "xn", "xTp", "xTs", "lgp", "lgs"))
        s_put = [sem(f"put{i}") for i in range(UNROLL)]
        b_x = [g.ps[0:HALF, i, 0:2 * T].rearrange("p (k t) -> p k t", k=2) for i in range(2)]
        b_lg = [g.ps[0:T, 2 + i, 0:NE] for i in range(2)]
        block = ctx.enter_context(nc.Block())

        @block.sync
        def _(sp):
            sp.dma_start(wr[:, :, :], A["moe_wr"].rearrange("(k p) e -> p k e", k=2)).then_inc(s_w, 16)
            sp.dma_start(A["out"][0:NTOK, :].rearrange("(b t) d -> t b d", t=T), g.h[:, :, :]).then_inc(s_tab, 16)
            sp.wait_ge(s_zero, 1)
            sp.dma_start(A["out"][NTOK:NTOK + 128, :], zero[:, :]).then_inc(s_tab, 16)
            sp.dma_start(A["xtab"][NTOK:NTOK + 128, :], zero[:, :]).then_inc(s_tab, 16)

            def put(b, i):
                item(sp, s_xn, b)
                sp.dma_start(A["xtab"][bass.ds(b * T, T), :], xn[:, i, :]).then_inc(s_put[i], 16)

            steps(sp, B, [(put, 0)])
            sp.wait_ge(s_tab, 48)
            for i in range(UNROLL):
                sp.wait_ge(s_put[i], 16 * B // UNROLL)

        @block.gpsimd
        def _(pool):
            pool.memset(zero[:, :], 0.0).then_inc(s_zero, 1)

        @block.vector
        def _(v):
            def norm_input(b, i):
                reused(v, s_xTp, b, UNROLL)
                if not isinstance(b, int):
                    v.wait_ge(s_put[i], (b - i) * (16 // UNROLL))
                elif b >= UNROLL:
                    v.wait_ge(s_put[i], 16 * (b // UNROLL))
                v.tensor_scalar(xn[:, i, :].unsqueeze(1), g.h[:, bass.ds(b, 1), :], g.rstd[:, bass.ds(b, 1)],
                                g.nmr[:, bass.ds(b, 1)], ALU.mult, ALU.add).then_inc(s_xn, 1)

            def keep(b, i):
                item(v, s_lgp, b)
                v.tensor_copy(g.lg[:, bass.ds(b, 1), :], b_lg[i % 2].unsqueeze(1)).then_inc(s_lgs, 1)

            steps(v, B, [(norm_input, 0), (keep, 2)])

        @block.scalar
        def _(act):
            def x_copy(b, i):
                item(act, s_xTp, b)
                reused(act, s_lgp, b, 2)
                act.activation(xT[:, i % 2, :, :], b_x[i % 2], ACT.Copy).then_inc(s_xTs, 1)

            steps(act, B, [(x_copy, 0)])

        @block.tensor
        def _(pe):
            pe.wait_ge(s_w, 16)

            def transpose_x(b, i):
                item(pe, s_xn, b)
                reused(pe, s_xTs, b, 2)
                for k in range(2):
                    mm = pe.transpose(b_x[i % 2][:, k, :], xn[:, i, k * HALF:(k + 1) * HALF], g.ident[0:T, 0:T])
                mm.then_inc(s_xTp, 1)

            def logits(b, i):
                item(pe, s_xTs, b)
                reused(pe, s_lgs, b, 2)
                for k in range(2):
                    mm = pe.matmul(b_lg[i % 2], xT[:, i % 2, k, :], wr[:, k, :], start=(k == 0), stop=(k == 1))
                mm.then_inc(s_lgp, 1)

            steps(pe, B, [(transpose_x, 0), (logits, 1)])


def route(nc, A, g):
    with ExitStack() as ctx:
        def sem(name):
            return g.phase_sem("r1_" + name)

        def sb(name, shape, dt=F32):
            return ctx.enter_context(nc.sbuf_tensor("r1_" + name, shape, dt))

        iota = sb("iota", [128, 128])
        padrow = sb("padrow", [128, 2])
        before = sb("before", [T, T])
        tokid = sb("tokid", [T, B])
        ones = sb("ones", [T, 256])
        key = sb("key", [T, B, NE])
        oh = sb("oh", [T, 2, B, NE])
        lg2 = sb("lg2", [T, B, NE])
        both = sb("both", [T, B, NE])
        m = sb("m", [T, 2, B])
        ex = sb("ex", [T, B])
        c = sb("c", [T, 2, B])
        cnt = sb("cnt", [T, NE, B])
        cum = sb("cum", [T, NE, B])
        pos = sb("pos", [T, NE, B])
        e8 = sb("e8", [T, 6, NE])
        place = sb("place", [T, 2, B])
        tile = sb("tile", [T, 2, B])
        row = sb("row", [T, 2, B])
        ohp = sb("ohp", [T, NPAIR, 128])
        info = sb("info", [T, NPAIR, 3, NTILES])
        tge = sb("tge", [T, NTILES, NE])
        tef = sb("tef", [T, NTILES])
        lst = sb("lst", [128, 2, NTILES])
        s_w, s_ones, s_v, s_d, s_ex, s_both, s_pre, s_occ, s_info, s_ohp, s_list = (
            sem(n) for n in ("w", "ones", "v", "d", "ex", "both", "pre", "occ", "info", "ohp", "list"))
        MAGIC = 1.5 * 2 ** 23
        b_intra = g.ps[0:T, 0, 0:256].rearrange("p (e b) -> p e b", e=NE)
        b_cnt = g.ps[0:T, 1, 0:256].rearrange("p (e b) -> p e b", e=NE)
        b_list = g.ps[:, 2, 0:3 * NTILES].rearrange("p (c n) -> p c n", c=3)
        block = ctx.enter_context(nc.Block())

        @block.sync
        def _(sp):
            sp.dma_start(iota[:, :], A["iota"]).then_inc(s_w, 16)
            sp.dma_start(padrow[:, :], A["padrow"]).then_inc(s_w, 16)
            sp.dma_start(before[:, :], A["before"]).then_inc(s_w, 16)
            sp.dma_start(tokid[:, :], A["tokid"]).then_inc(s_w, 16)

        @block.gpsimd
        def _(pool):
            pool.memset(ones[:, :], 1.0).then_inc(s_ones, 1)
            pool.wait_ge(s_occ, 1)
            for k in range(2):
                cols = slice(k * B, (k + 1) * B)
                pool.tensor_tensor(info[:, cols, 1, :], info[:, cols, 0, :],
                                   tokid[:, :].unsqueeze(2).broadcast_to([T, B, NTILES]), ALU.mult).then_inc(s_info, 1)

        @block.scalar
        def _(act):
            act.wait_ge(s_d, 1)
            act.activation(ex[:, :], ex[:, :], ACT.Exp).then_inc(s_ex, 1)

        @block.vector
        def _(v):
            done = [0]

            def link(ins):
                done[0] += 1
                ins.then_inc(s_v, 1)
                v.wait_ge(s_v, done[0])

            def wide(x, n):
                return x.unsqueeze(2).broadcast_to([x.shape[0], x.shape[1], n])

            v.wait_ge(s_w, 64)
            v.wait_ge(s_ones, 1)
            experts = iota[0:T, 0:NE].unsqueeze(1).broadcast_to([T, B, NE])
            for k in range(2):
                src = g.lg if k == 0 else lg2
                link(v.tensor_reduce(m[:, k, :], src[:, :, :], AX.X, ALU.max))
                link(v.tensor_tensor(key[:, :, :], src[:, :, :], wide(m[:, k, :], NE), ALU.is_equal))
                link(v.scalar_tensor_tensor(key[:, :, :], key[:, :, :], -float(NE), experts, ALU.mult, ALU.add))
                link(v.tensor_reduce(place[:, 0, :], key[:, :, :], AX.X, ALU.min))
                link(v.tensor_tensor(oh[:, k, :, :], key[:, :, :], wide(place[:, 0, :], NE), ALU.is_equal))
                if k == 0:
                    link(v.scalar_tensor_tensor(lg2[:, :, :], oh[:, 0, :, :], -1e30, g.lg[:, :, :], ALU.mult, ALU.add))
            v.tensor_tensor(ex[:, :], m[:, 1, :], m[:, 0, :], ALU.subtract).then_inc(s_d, 1)
            v.tensor_tensor(both[:, :, :], oh[:, 0, :, :], oh[:, 1, :, :], ALU.add).then_inc(s_both, 1)
            v.wait_ge(s_ex, 1)
            link(v.tensor_scalar(c[:, 1, :], ex[:, :], 1.0, None, ALU.add))
            link(v.reciprocal(c[:, 0, :], c[:, 1, :]))
            link(v.tensor_tensor(c[:, 1, :], ex[:, :], c[:, 0, :], ALU.mult))
            v.wait_ge(s_pre, 1)
            link(v.tensor_copy(cnt[:, :, :], b_cnt))
            link(v.tensor_tensor_scan(cum[:, :, :].rearrange("p e b -> p (e b)"), ones[:, :],
                                      cnt[:, :, :].rearrange("p e b -> p (e b)"), 0.0, ALU.mult, ALU.add))
            upto_, n_, tiles, ctiles, shift = (e8[:, i, :] for i in range(5))
            start = e8[:, 5, :]
            link(v.tensor_copy(upto_, cum[:, :, B - 1]))
            link(v.memset(start, 0.0))
            link(v.tensor_copy(e8[:, 5, 1:NE], e8[:, 0, 0:NE - 1]))
            link(v.tensor_tensor(n_, upto_, start, ALU.subtract))
            link(v.tensor_scalar(tiles, n_, 1.0 / 128, 127.0 / 128 - 0.5 + 1.0 / 256, ALU.mult, ALU.add))
            link(v.tensor_scalar(tiles, tiles, MAGIC, None, ALU.add))
            link(v.tensor_scalar(tiles, tiles, -MAGIC, None, ALU.add))
            link(v.tensor_tensor_scan(ctiles, ones[:, 0:NE], tiles, 0.0, ALU.mult, ALU.add))
            link(v.tensor_tensor(shift, ctiles, tiles, ALU.subtract))
            link(v.scalar_tensor_tensor(shift, shift, 128.0, start, ALU.mult, ALU.subtract))
            link(v.tensor_tensor(pos[:, :, :], cum[:, :, :], cnt[:, :, :], ALU.subtract))
            link(v.tensor_tensor(pos[:, :, :], b_intra, pos[:, :, :], ALU.add))
            link(v.tensor_tensor(pos[:, :, :], pos[:, :, :], wide(shift, B), ALU.add))
            for k in range(2):
                link(v.tensor_tensor(key[:, :, :], pos[:, :, :].rearrange("p e b -> p b e"), oh[:, k, :, :], ALU.mult))
                link(v.tensor_reduce(place[:, k, :], key[:, :, :], AX.X, ALU.add))
            link(v.tensor_scalar(tile[:, :, :], place[:, :, :], 1.0 / 128, -0.5 + 1.0 / 256, ALU.mult, ALU.add))
            link(v.tensor_scalar(tile[:, :, :], tile[:, :, :], MAGIC, None, ALU.add))
            link(v.tensor_scalar(tile[:, :, :], tile[:, :, :], -MAGIC, None, ALU.add))
            link(v.scalar_tensor_tensor(row[:, :, :], tile[:, :, :], -128.0, place[:, :, :], ALU.mult, ALU.add))
            flat = lambda x: x[:, :, :].rearrange("p k b -> p (k b)")
            v.tensor_tensor(info[:, :, 0, :], iota[0:T, 0:NTILES].unsqueeze(1).broadcast_to([T, NPAIR, NTILES]),
                            wide(flat(tile), NTILES), ALU.is_equal).then_inc(s_occ, 1)
            v.wait_ge(s_occ, 1)
            v.tensor_tensor(info[:, :, 2, :], info[:, :, 0, :], wide(flat(c), NTILES), ALU.mult).then_inc(s_info, 1)
            for q in range(4):
                cols = slice(16 * q, 16 * q + 16)
                v.tensor_tensor(ohp[:, cols, :], iota[0:T, :].unsqueeze(1).broadcast_to([T, 16, 128]),
                                wide(flat(row)[:, cols], 128), ALU.is_equal).then_inc(s_ohp, 1)
            link(v.tensor_tensor(tge[:, :, :], wide(iota[0:T, 0:NTILES], NE),
                                 ctiles.unsqueeze(1).broadcast_to([T, NTILES, NE]), ALU.is_ge))
            link(v.tensor_reduce(tef[:, :], tge[:, :, :], AX.X, ALU.add))
            link(v.tensor_scalar(g.te[0:T, :], tef[:, :], float(NE - 1), None, ALU.min))
            v.wait_ge(s_list, 1)
            link(v.tensor_copy(lst[:, 0, :], b_list[:, 0, :]))
            link(v.scalar_tensor_tensor(lst[:, 1, :], lst[:, 0, :], padrow[:, 1:2], b_list[:, 1, :], ALU.mult, ALU.add))
            link(v.tensor_scalar(g.idx[:, :], lst[:, 1, :], padrow[:, 0:1], None, ALU.add))
            link(v.tensor_copy(g.cw[:, :], b_list[:, 2, :]))

        @block.tensor
        def _(pe):
            pe.wait_ge(s_both, 1)
            flat = both[:, :, :].rearrange("p b e -> p e b")
            pe.matmul(b_intra, before[:, :], flat, start=True, stop=True)
            pe.matmul(b_cnt, ones[:, 0:T], flat, start=True, stop=True).then_inc(s_pre, 1)
            pe.wait_ge(s_info, 3)
            for j in range(NPAIR):
                if j % 16 == 0:
                    pe.wait_ge(s_ohp, j // 16 + 1)
                mm = pe.matmul(b_list, ohp[:, j, :], info[:, j, :, :], start=(j == 0), stop=(j == NPAIR - 1))
            mm.then_inc(s_list, 1)


def expert_tiles(nc, A, g):
    with ExitStack() as ctx:
        def sem(name):
            return g.phase_sem("x_" + name)

        def sb(name, shape, dt=F32):
            return ctx.enter_context(nc.sbuf_tensor("x_" + name, shape, dt))

        xg = sb("xg", [128, NX, D])
        xT = sb("xT", [HALF + 1, 2, 2, 128])
        hid = sb("hid", [128, 2, F])
        hT = sb("hT", [128, 2, FC, 128])
        b2 = sb("b2", [128, NE, D])
        ya = sb("ya", [128, 2, D])
        ys = sb("ys", [128, 2, D])
        s_b2, s_one, s_xTp, s_xTs, s_h1, s_relu, s_hTp, s_hTs, s_y, s_ya, s_ys = (
            sem(n) for n in ("b2", "one", "xTp", "xTs", "h1", "relu", "hTp", "hTs", "y", "ya", "ys"))
        s_x, s_add = g.s_x, g.s_add
        N2 = F // 2
        b_x = g.ps[0:HALF, 0, 0:256].rearrange("p (k t) -> p k t", k=2)
        block = ctx.enter_context(nc.Block())

        @block.sync
        def _(sp):
            sp.dma_start(b2[:, :, :], A["moe_b2"].unsqueeze(0).broadcast_to([128, NE, D])).then_inc(s_b2, 16)

        @block.gpsimd
        def _(pool):
            pool.memset(xT[HALF:HALF + 1, :, 1, :], 1.0).then_inc(s_one, 1)
            for t in range(NTILES + 3):
                if t < NTILES:
                    if t >= NX:
                        pool.wait_ge(s_xTp, t - NX + 1)
                    pool.indirect_dma_start(out=xg[:, t % NX, :], out_offset=None, in_=A["xtab"][:, :],
                                            in_offset=bass.IndirectOffsetOnAxis(ap=g.idx[:, t:t + 1], axis=0)
                                            ).then_inc(s_x[t % NX], 16)
                i = t - 3
                if i >= 0:
                    pool.wait_ge(s_ys, i + 1)
                    if i >= 1:
                        pool.wait_ge(s_add, 16 * i)
                    pool.indirect_dma_start(out=A["out"][:, :],
                                            out_offset=bass.IndirectOffsetOnAxis(ap=g.idx[:, i:i + 1], axis=0),
                                            in_=ys[:, i % 2, :], in_offset=None, compute_op=ALU.add).then_inc(s_add, 16)
            pool.wait_ge(s_add, 16 * NTILES)

        @block.scalar
        def _(act):
            def x_copy(i, u):
                item(act, s_xTp, i)
                reused(act, s_h1, i, 2, 2)
                act.activation(xT[0:HALF, u % 2, :, :], b_x, ACT.Copy).then_inc(s_xTs, 1)

            def relu(i, u):
                reused(act, s_hTp, i, 2, 2)
                for n in range(2):
                    act.wait_ge(s_h1, i * 2 + n + 1)
                    act.activation(hid[:, u % 2, n * N2:(n + 1) * N2], g.ps[:, 1 + n, 0:N2], ACT.Relu).then_inc(s_relu, 1)

            def weigh(i, u):
                item(act, s_ya, i)
                if not isinstance(i, int) or i >= 2:
                    act.wait_ge(s_add, i * 16 - 16)
                act.activation(ys[:, u % 2, :], ya[:, u % 2, :], ACT.Copy,
                               scale=g.cw[:, bass.ds(i, 1)]).then_inc(s_ys, 1)

            steps(act, NTILES, [(x_copy, 0), (relu, 0), (weigh, 2)], unroll=4, depth=4)

        @block.vector
        def _(v):
            v.wait_ge(s_b2, 16)

            def turn_copy(i, u):
                reused(v, s_y, i, 2)
                for n in range(2):
                    v.wait_ge(s_hTp, i * 2 + n + 1)
                    v.tensor_copy(hT[:, u % 2, 3 * n:3 * n + 3, :],
                                  g.ps[:, 3 + n, 0:384].rearrange("p (k m) -> p k m", k=3)).then_inc(s_hTs, 1)

            def add_bias(i, u):
                e = v.value_load(g.te[0:1, bass.ds(i, 1)], min_val=0, max_val=NE - 1)
                item(v, s_y, i)
                reused(v, s_ys, i, 2)
                v.tensor_tensor(ya[:, u % 2, :].unsqueeze(1), g.ps[:, 5, 0:D].unsqueeze(1), b2[:, bass.ds(e, 1), :],
                                ALU.add).then_inc(s_ya, 1)

            steps(v, NTILES, [(turn_copy, 1), (add_bias, 1)], unroll=4, depth=4)

        @block.tensor
        def _(pe):
            pe.wait_ge(s_one, 1)
            pe.wait_ge(g.s_e, 64)

            def transpose_x(i, u):
                if isinstance(i, int):
                    pe.wait_ge(s_x[u], 16 * (i // NX + 1))
                else:
                    pe.wait_ge(s_x[u], (i - u) * (16 // NX) + 16)
                reused(pe, s_xTs, i, 1)
                for k in range(2):
                    mm = pe.transpose(b_x[:, k, :], xg[:, u, k * HALF:(k + 1) * HALF], g.ident[:, :])
                mm.then_inc(s_xTp, 1)

            def first(i, u):
                e = pe.value_load(g.te[0:1, bass.ds(i, 1)], min_val=0, max_val=NE - 1)
                item(pe, s_xTs, i)
                for n in range(2):
                    if not isinstance(i, int) or i >= 1:
                        pe.wait_ge(s_relu, i * 2 + n - 1)
                    for k in range(2):
                        mm = pe.matmul(g.ps[:, 1 + n, 0:N2], xT[0:HALF + k, u % 2, k, :],
                                       g.e1[0:HALF + k, k, bass.ds(e, 1), n * N2:(n + 1) * N2].rearrange("p a f -> p (a f)"),
                                       start=(k == 0), stop=(k == 1))
                    mm.then_inc(s_h1, 1)

            def turn(i, u):
                for n in range(2):
                    pe.wait_ge(s_relu, i * 2 + 2)
                    if not isinstance(i, int) or i >= 1:
                        pe.wait_ge(s_hTs, i * 2 + n - 1)
                    for k in range(3):
                        mm = pe.transpose(g.ps[:, 3 + n, 128 * k:128 * (k + 1)], hid[:, u % 2, 3 * n + k:F:FC], g.ident[:, :])
                    mm.then_inc(s_hTp, 1)

            def second(i, u):
                e = pe.value_load(g.te[0:1, bass.ds(i, 1)], min_val=0, max_val=NE - 1)
                reused(pe, s_ya, i, 1)
                for k in range(FC):
                    if k % 3 == 0:
                        pe.wait_ge(s_hTs, i * 2 + k // 3 + 1)
                    mm = pe.matmul(g.ps[:, 5, 0:D], hT[:, u % 2, k, :],
                                   g.e2[:, bass.ds(e, 1), k * D:(k + 1) * D].rearrange("p a d -> p (a d)"),
                                   start=(k == 0), stop=(k == FC - 1))
                mm.then_inc(s_y, 1)

            steps(pe, NTILES, [(transpose_x, 0), (turn, 1), (first, 0), (second, 1)], unroll=4, depth=4)


def store(nc, A, g):
    with ExitStack() as ctx:
        s_out = ctx.enter_context(nc.semaphore("o_out"))
        block = ctx.enter_context(nc.Block())

        @block.sync
        def _(sp):
            sp.dma_start(A["out"][0:NTOK, :].rearrange("(b t) d -> t b d", t=T), g.h[:, :, :]).then_inc(s_out, 16)
            sp.wait_ge(s_out, 16)


def lay_out(i):
    a = {k: np.asarray(v) for k, v in i.items()}
    x = a["x"]
    xs = np.zeros_like(x)
    xs[:, :, 1:, 1:] = x[:, :, :-1, :-1]
    n = 128 // PATCH
    xs = xs.reshape(B, CIN, n, PATCH, n, PATCH).transpose(3, 5, 1, 0, 2, 4).reshape(KC, 128, B * n * n)
    w = a["L0_tok_weight"].transpose(2, 3, 1, 0).reshape(KP, D)
    kw = (np.arange(KP) // CIN) % PATCH
    q = {
        "x_patches": xs,
        "txt": a["txt"],
        "tok_w": w,
        "tok_move": np.tile(a["L0_tok_move_bias"], KP // CIN).reshape(KC, 128).T,
        "tok_keep": (kw != 0).astype(np.float32).reshape(KC, 128).T,
        "ident": np.eye(128, dtype=np.float32),
        "head_mask": np.kron(np.eye(HH), np.ones((DH, 1))).astype(np.float32),
        "a0_wqk": np.concatenate([np.concatenate([a["L0_attn_Wq"], a["L0_attn_Wk"]], 1),
                                  np.concatenate([a["L0_attn_bq"], a["L0_attn_bk"]])[None]], 0),
        "a0_wv": np.concatenate([a["L0_attn_Wv"], a["L0_attn_bv"][None]], 0),
        "a0_bo": a["L0_attn_bo"],
    }
    q.update({"norm_w": a["L0_ffn_norm_weight"], "slots": a["L0_ffn_slots"], "slot_scale": a["L0_ffn_scale"],
              "fc1_w": a["L0_ffn_fc1_weight"], "fc1_b": a["L0_ffn_fc1_bias"],
              "fc2_w": a["L0_ffn_fc2_weight"], "fc2_b": a["L0_ffn_fc2_bias"]})
    theta = np.float32(10000.0) ** (-2.0 * np.arange(D // 2, dtype=np.float32) / np.float32(D))
    angle = np.arange(T, dtype=np.float32)[:, None] * theta[None, :].astype(np.float32)
    cos, sin = np.cos(angle).astype(np.float32), np.sin(angle).astype(np.float32)
    q["rope_cos"] = np.tile(np.repeat(cos, 2, axis=1), (1, 2))
    q["rope_sin"] = np.tile(sin, (1, 2))
    q["rope_nsin"] = -q["rope_sin"]
    q["causal"] = np.where(np.tril(np.ones((T, T), bool)), 0.0, -1e30).astype(np.float32)
    q["a1_wqkv"] = np.concatenate([a["L1_attn_Wq"], a["L1_attn_Wk"], a["L1_attn_Wv"]], 1)
    q.update({"moe_wr": a["L1_ffn_Wr"], "moe_w1": a["L1_ffn_W1"], "moe_b1": a["L1_ffn_b1"],
              "moe_w2": a["L1_ffn_W2"], "moe_b2": a["L1_ffn_b2"]})
    q["iota"] = np.tile(np.arange(128, dtype=np.float32), (128, 1))
    pad = NTOK + np.arange(128, dtype=np.float32)
    q["padrow"] = np.stack([pad, -pad], 1)
    q["before"] = np.triu(np.ones((T, T), np.float32), 1)
    q["tokid"] = (np.arange(T)[:, None] + T * np.arange(B)[None, :]).astype(np.float32)
    wo = np.zeros((NH, HPAD, D), np.float32)
    wo[:, :DH] = a["L0_attn_Wo"].reshape(NH, DH, D)
    q["a0_wo"] = wo.reshape(NH * HPAD, D)
    return {k: np.ascontiguousarray(v) for k, v in q.items()}


def declare(nc, arrays):
    A = {k: nc.dram_tensor(f"in_{k}", v.shape, mybir.dt.from_np(v.dtype), kind="ExternalInput").ap()
         for k, v in arrays.items()}
    A["out"] = nc.dram_tensor("out_h", (NTOK + 128, D), F32, kind="ExternalOutput").ap()
    A["xtab"] = nc.dram_tensor("xtab", (NTOK + 128, D), F32, kind="Internal").ap()
    return A


def kernel(**inputs):
    import concourse.bacc as bacc
    from concourse.bass_utils import run_bass_kernel_spmd as run
    arrays = lay_out(inputs)
    nc = bacc.Bacc("TRN2", target_bir_lowering=False, num_devices=1)
    build(nc, declare(nc, arrays))
    r = run(nc, [{f"in_{k}": v for k, v in arrays.items()}], core_ids=[0])
    return r.results[0]["out_h"][:NTOK].reshape(B, T, D)
```

```python
from contextlib import ExitStack

import numpy as np

import concourse.bass as bass
from concourse import mybir

F32 = mybir.dt.float32
BF16 = mybir.dt.bfloat16
F32R = mybir.dt.float32r
ALU = mybir.AluOpType
ACT = mybir.ActivationFunctionType
AX = mybir.AxisListType

B = 32
T_IMG, T_TXT = 64, 32
T = T_IMG + T_TXT
D = 192
HALF = D // 2
PATCH, CIN = 16, 3
KP = CIN * PATCH * PATCH
KC = KP // 128
NH, DH = 12, 16
HH = NH // 2
HPAD = 32
HG = 128 // HPAD
NG = NH // HG
NS = 64
F = 768
FC = F // 128
GS = 4
NGR = NS // GS
W1_DMAS = 3
NE = 8
NTILES = 56
NTOK = B * T
NX = 4
NPAIR = 2 * B
assert NTILES >= (2 * NTOK + NE * 127) // 128 and NTILES % 2 == 0 and 2 * GS == NE
EPS = 1e-5
UNROLL = 4


def item(eng, sem, b, per=1):
    eng.wait_ge(sem, b * per + per)


def reused(eng, sem, b, depth, per=1):
    if not isinstance(b, int) or b >= depth:
        eng.wait_ge(sem, b * per - (depth - 1) * per)


def steps(eng, n, stages, unroll=UNROLL, depth=UNROLL):
    last = max(lag for _, lag in stages)
    first = -(-(last + depth) // unroll) * unroll
    for t in range(first):
        for stage, lag in stages:
            if t >= lag:
                stage(t - lag, (t - lag) % unroll)
    with eng.Fori(first // unroll, n // unroll) as j:
        for u in range(unroll):
            for stage, lag in stages:
                stage(j * unroll + (u - lag), (u - lag) % unroll)
    for t in range(n, n + last):
        for stage, lag in stages:
            if t - lag < n:
                stage(t - lag, (t - lag) % unroll)


def few_steps(n, stages):
    for t in range(n + max(lag for _, lag in stages)):
        for stage, lag in stages:
            if 0 <= t - lag < n:
                stage(t - lag, (t - lag) % 2)


class Prog:

    def __init__(self, nc):
        self.nc = nc
        self.live = []

    def phase_sem(self, name):
        s = self.nc.alloc_semaphore(name)
        self.live.append(s)
        return s

    def clear_sems(self):
        self.nc.clear_and_free_semaphores(self.live)
        self.nc.all_engine_barrier()
        self.live = []


def build(nc, A):
    with ExitStack() as ctx:
        g = Prog(nc)

        def sem(name):
            return ctx.enter_context(nc.semaphore(name))

        def sb(name, shape, dt=F32):
            return ctx.enter_context(nc.sbuf_tensor(name, shape, dt))

        g.ident = sb("ident", [128, 128])
        g.idx = sb("idx", [128, NTILES], mybir.dt.uint32)
        g.cw = sb("cw", [128, NTILES])
        g.te = sb("te", [128, NTILES], mybir.dt.int32)
        g.s_const = sem("s_const")
        n1, n2, nh = 4 * GS * F, 2 * GS * FC * D, B * D
        held = ExitStack()
        g.flat = held.enter_context(nc.sbuf_tensor("flat", [128, n1 + n2 + nh], F32))
        w1_flat, w2_flat = g.flat[0:HALF + 1, 0:n1], g.flat[:, n1:n1 + n2]
        g.h = g.flat[0:T, n1 + n2:].rearrange("p (b d) -> p b d", d=D)
        g.w1 = w1_flat.rearrange("p (i k s f) -> p i k s f", i=2, k=2, f=F)
        g.w2 = w2_flat.rearrange("p (i s n) -> p i s n", i=2, n=FC * D)
        g.e1 = w1_flat.rearrange("p (k e f) -> p k e f", k=2, f=F)
        g.e2 = w2_flat.rearrange("p (k e d) -> p k e d", k=FC, d=D)
        g.s_e = sem("s_e")
        g.s_x = [sem(f"s_x{i}") for i in range(NX)]
        g.s_add = sem("s_add")
        g.s_w1 = [sem(f"s_w1_{i}") for i in range(2)]
        g.s_w2 = [sem(f"s_w2_{i}") for i in range(2)]
        psum = ctx.enter_context(nc.psum_tensor("psum", [128, 8, 512], F32))
        g.ps = psum
        with ExitStack() as norms:
            def small(name, shape):
                return norms.enter_context(nc.sbuf_tensor(name, shape, F32))

            g.stats = small("stats", [T, B, 6])
            g.rstd = small("rstd", [T, B])
            g.nmr = small("nmr", [T, B])
            g.lnt = small("lnt", [T, 4, B])
            embed(nc, A, g)
            with ExitStack() as inner:
                g.nw = inner.enter_context(nc.sbuf_tensor("nw", [T, D], F32))
                g.slT = inner.enter_context(nc.sbuf_tensor("slT", [HALF, 2, NS], F32))
                attention0(nc, A, g)
                soft_moe(nc, A, g)
            g.clear_sems()
            attention1(nc, A, g)
            with ExitStack() as inner:
                g.lg = inner.enter_context(nc.sbuf_tensor("t_lg", [T, B, NE], F32))
                gate(nc, A, g)
                route(nc, A, g)
        held.close()
        expert_tiles(nc, A, g)


def layernorm_scale(eng_v, eng_s, g, s):
    st = g.stats
    mean, half_diff, var, sq = (g.lnt[:, i, :] for i in range(4))
    if eng_v is not None:
        v = eng_v
        v.tensor_tensor(mean, st[:, :, 1], st[:, :, 4], ALU.add).then_inc(s, 1)
        v.tensor_tensor(half_diff, st[:, :, 1], st[:, :, 4], ALU.subtract).then_inc(s, 1)
        v.tensor_tensor(var, st[:, :, 2], st[:, :, 5], ALU.add).then_inc(s, 1)
        v.wait_ge(s, 3)
        v.tensor_tensor(half_diff, half_diff, half_diff, ALU.mult).then_inc(s, 1)
        v.tensor_scalar(var, var, 1.0 / D, EPS, ALU.mult, ALU.add).then_inc(s, 1)
        v.wait_ge(s, 5)
        v.scalar_tensor_tensor(var, half_diff, 0.25, var, ALU.mult, ALU.add).then_inc(s, 1)
        v.wait_ge(s, 7)
        v.reciprocal(g.rstd[:, :], sq).then_inc(s, 1)
        v.wait_ge(s, 8)
        v.scalar_tensor_tensor(g.nmr[:, :], mean, -0.5, g.rstd[:, :], ALU.mult, ALU.mult).then_inc(s, 1)
        v.wait_ge(s, 9)
    if eng_s is not None:
        eng_s.wait_ge(s, 6)
        eng_s.activation(sq, var, ACT.Sqrt).then_inc(s, 1)


def load_slots(sp, A, g, gr, i, w1_free=lambda: None, w2_free=lambda: None):
    src = A["fc1_w"][bass.ds(gr * GS, GS), :, :].rearrange("s (k p) n -> k p s n", k=2)
    w1_free()
    for k in range(2):
        sp.dma_start(g.w1[0:HALF, i, k, :, :], src[k]).then_inc(g.s_w1[i], 16)
    sp.dma_start(g.w1[HALF:HALF + 1, i, 1, :, :], A["fc1_b"][bass.ds(gr * GS, GS), :].unsqueeze(0)).then_inc(g.s_w1[i], 16)
    w2_free()
    sp.dma_start(g.w2[:, i, :, :], A["fc2_w"][bass.ds(gr * GS, GS), :, :].rearrange(
        "s (p k) n -> p s (k n)", k=FC)).then_inc(g.s_w2[i], 16)


def embed(nc, A, g):
    NT = B * T_IMG
    CH = 512
    NCH = NT // CH
    TPC = CH // 128
    with ExitStack() as ctx:
        def sem(name):
            return g.phase_sem(name)

        def sb(name, shape, dt=F32):
            return ctx.enter_context(nc.sbuf_tensor(name, shape, dt))

        x_raw = sb("x_raw", [128, NCH, KC, CH])
        x_sign = sb("x_sign", [128, KC, NT], BF16)
        w_raw = sb("w_raw", [128, KC, D])
        w_abs = sb("w_abs", [128, KC, D])
        w_sign = sb("w_sign", [128, KC, D], BF16)
        move = sb("move", [128, KC])
        keep = sb("keep", [128, KC])
        ones = sb("ones_e", [128, 128])
        sf = sb("sf", [128, D])
        s_w, s_txt = sem("e_w"), sem("e_txt")
        s_x = [sem(f"e_x{c}") for c in range(NCH)]
        s_ones, s_wsign, s_wabs, s_sfps, s_sf = (sem(n) for n in ("e_ones", "e_wsign", "e_wabs", "e_sfps", "e_sf"))
        s_sign, s_row, s_edge, s_tile, s_out, s_stats, s_ln = (
            sem(n) for n in ("e_sign", "e_row", "e_edge", "e_tile", "e_out", "e_stats", "e_ln"))
        block = ctx.enter_context(nc.Block())

        @block.sync
        def _(sp):
            sp.dma_start(w_raw[:, :, :], A["tok_w"].rearrange("(k p) e -> p k e", p=128)).then_inc(s_w, 16)
            sp.dma_start(move[:, :], A["tok_move"]).then_inc(s_w, 16)
            sp.dma_start(keep[:, :], A["tok_keep"]).then_inc(s_w, 16)
            for c in range(NCH):
                sp.dma_start(x_raw[:, c, :, :],
                             A["x_patches"][:, :, c * CH:(c + 1) * CH].rearrange("k p n -> p k n")).then_inc(s_x[c], 16)
            sp.dma_start(g.ident[:, :], A["ident"]).then_inc(g.s_const, 16)
            sp.dma_start(g.h[T_IMG:T, :, :], A["txt"].rearrange("b t d -> t b d")).then_inc(s_txt, 16)

        @block.gpsimd
        def _(pool):
            pool.memset(ones[:, :], 1.0 / KP).then_inc(s_ones, 1)

        @block.scalar
        def _(act):
            act.wait_ge(s_w, 48)
            act.activation(w_sign[:, :, :], w_raw[:, :, :], ACT.Sign).then_inc(s_wsign, 1)
            act.activation(w_abs[:, :, :], w_raw[:, :, :], ACT.Abs).then_inc(s_wabs, 1)
            for c in range(NCH):
                act.wait_ge(s_x[c], 16)
                for k in range(KC):
                    act.activation(x_sign[:, k, c * CH:(c + 1) * CH], x_raw[:, c, k, :],
                                   ACT.Sign, bias=move[:, k:k + 1]).then_inc(s_sign, 1)
            layernorm_scale(None, act, g, s_ln)

        @block.tensor
        def _(pe):
            pe.wait_ge(s_ones, 1)
            pe.wait_ge(s_wabs, 1)
            for k in range(KC):
                mm = pe.matmul(g.ps[:, 7, 0:D], ones[:, :], w_abs[:, k, :], start=(k == 0), stop=(k == KC - 1))
            mm.then_inc(s_sfps, 1)
            pe.wait_ge(s_wsign, 1)
            with pe.Fori(0, NCH) as c:
                item(pe, s_edge, c)
                for u in range(TPC):
                    pe.wait_ge(s_out, c * (2 * TPC) + 2 * (u + 1))
                    for k in range(KC):
                        mm = pe.matmul(g.ps[:, u, 0:D], x_sign[:, k, bass.ds(c * CH + u * 128, 128)],
                                       w_sign[:, k, :], start=(k == 0), stop=(k == KC - 1))
                    mm.then_inc(s_tile, 1)

        @block.vector
        def _(v):
            v.sem_inc(s_out, 2 * TPC)
            v.wait_ge(s_sfps, 1)
            v.tensor_copy(sf[:, :], g.ps[:, 7, 0:D]).then_inc(s_sf, 1)
            v.wait_ge(s_sf, 1)

            def edges(c):
                item(v, s_sign, c, KC)
                tok = x_sign[:, :, bass.ds(c * CH, CH)].rearrange("p k (q j) -> p k q j", j=8)[:, :, :, 0]
                row = x_sign[0:CIN * PATCH, 0, bass.ds(c * CH, CH)].rearrange("p (b i j) -> p b i j", i=8, j=8)
                v.tensor_scalar(row[:, :, 0, :], row[:, :, 0, :], 0.0, None, ALU.mult).then_inc(s_row, 1)
                item(v, s_row, c)
                v.tensor_tensor(tok, tok, keep[:, :].unsqueeze(2).broadcast_to([128, KC, CH // 8]),
                                ALU.mult).then_inc(s_edge, 1)

            def scale_tiles(c):
                for u in range(TPC):
                    v.wait_ge(s_tile, c * TPC + u + 1)
                    for i in range(2):
                        b = c * (2 * TPC) + 2 * u + i
                        v.tensor_tensor(g.h[0:T_IMG, bass.ds(b, 1), :],
                                        g.ps[64 * i:64 * i + 64, u, 0:D].unsqueeze(1),
                                        sf[64 * i:64 * i + 64, :].unsqueeze(1), ALU.mult).then_inc(s_out, 1)

            edges(0)
            with v.Fori(1, NCH) as c:
                edges(c)
                scale_tiles(c - 1)
            scale_tiles(NCH - 1)
            v.wait_ge(s_txt, 16)
            v.wait_ge(s_out, 2 * TPC + B)
            with v.Fori(0, B // UNROLL) as j:
                for u in range(UNROLL):
                    b = j * UNROLL
                    v.bn_stats(g.stats[:, bass.ds(b + u, 1), :].rearrange("p a s -> p (a s)"),
                               g.h[:, bass.ds(b + u, 1), :].rearrange("p a d -> p (a d)")).then_inc(s_stats, 1)
            v.wait_ge(s_stats, B)
            layernorm_scale(v, None, g, s_ln)


def attention0(nc, A, g):
    with ExitStack() as ctx:
        def sem(name):
            return g.phase_sem("a_" + name)

        def sb(name, shape, dt=F32):
            return ctx.enter_context(nc.sbuf_tensor("a_" + name, shape, dt))

        wqk = sb("wqk", [HALF + 1, 2, 2 * D])
        wv = sb("wv", [HALF + 1, 2, D])
        wo = sb("wo", [128, NG, D])
        bo = sb("bo", [T, D])
        hmask = sb("hmask", [HALF, HH])
        xn = sb("xn", [T, 2, D])
        xT = sb("xT", [HALF + 1, 2, 2, T])
        qk = sb("qk", [HALF, 2, 4, T])
        kb = sb("kb", [HALF, 2, 2, HH, T])
        vv = sb("vv", [T, 4, NH, HPAD])
        p = sb("p", [T, 2, NH, T])
        pT = sb("pT", [T, NG, HG, T])
        oT = sb("oT", [128, NG, T])
        rw = sb("rw", [T, 2, NH, HPAD])
        rT = sb("rT", [128, NG, T])
        ones = sb("ones", [T, NH])
        sl = sb("sl", [NS, D])
        sl_junk = sb("sl_junk", [NS, D])
        sl_scale = sb("sl_scale", [NS, 1])
        sl_n = sb("sl_n", [NS, 4])
        mx = sb("mx", [T, 2, NH])
        sm = sb("sm", [T, 2, NH])
        rs = sb("rs", [T, 2, NH])

        s_w, s_set, s_vset, s_ones = sem("w"), sem("set"), sem("vset"), sem("ones")
        s_xn, s_bo, s_xTp, s_xTs, s_qkp, s_vp, s_qks, s_vs, s_kb = (
            sem(n) for n in ("xn", "bo", "xTp", "xTs", "qkp", "vp", "qks", "vs", "kb"))
        s_sc, s_mx, s_sub, s_exp, s_sum, s_rs, s_rw = (sem(n) for n in ("sc", "mx", "sub", "exp", "sum", "rs", "rw"))
        s_pTp, s_pTs, s_rTp, s_rTs, s_oTp, s_oTs, s_op, s_res, s_st, s_ln = (
            sem(n) for n in ("pTp", "pTs", "rTp", "rTs", "oTp", "oTs", "op", "res", "st", "ln"))

        s_slw, s_sl, s_slroot, s_slT = (sem(n) for n in ("slw", "sl", "slroot", "slT"))
        slT_ps = g.ps[0:HALF, 7, 0:2 * NS].rearrange("p (k s) -> p k s", k=2)
        bank_x = g.ps[:, 0, :]
        bank_qk = g.ps[0:HALF, 1, 0:4 * T].rearrange("p (m t) -> p m t", t=T)
        bank_oT = g.ps[:, 2, 0:NG * T].rearrange("p (r t) -> p r t", t=T)
        bank_out = g.ps[0:T, 2, NG * T:NG * T + D]
        scores = g.ps[0:T, 3:6, 0:HG * T].rearrange("p r (h t) -> p r h t", t=T)
        bank_pT = [g.ps[0:T, 6 + r % 2, 0:HG * T] for r in range(NG)]
        bank_rT = g.ps[:, 7, 0:NG * T].rearrange("p (r t) -> p r t", t=T)
        block = ctx.enter_context(nc.Block())

        @block.sync
        def _(sp):
            sp.dma_start(wqk[0:HALF, :, :], A["a0_wqk"][0:D, :].rearrange("(k p) n -> p k n", k=2)).then_inc(s_w, 16)
            sp.dma_start(wqk[HALF:HALF + 1, 1, :], A["a0_wqk"][D:D + 1, :]).then_inc(s_w, 16)
            sp.dma_start(wv[0:HALF, :, :], A["a0_wv"][0:D, :].rearrange("(k p) n -> p k n", k=2)).then_inc(s_w, 16)
            sp.dma_start(wv[HALF:HALF + 1, 1, :], A["a0_wv"][D:D + 1, :]).then_inc(s_w, 16)
            sp.dma_start(wo[:, :, :], A["a0_wo"].rearrange("(r p) n -> p r n", r=NG)).then_inc(s_w, 16)
            sp.dma_start(bo[:, :], A["a0_bo"].unsqueeze(0).broadcast_to([T, D])).then_inc(s_w, 16)
            sp.dma_start(hmask[:, :], A["head_mask"]).then_inc(s_w, 16)
            sp.dma_start(sl[:, :], A["slots"]).then_inc(s_slw, 16)
            sp.dma_start(sl_scale[:, :], A["slot_scale"].unsqueeze(1)).then_inc(s_slw, 16)
            sp.dma_start(g.nw[:, :], A["norm_w"].unsqueeze(0).broadcast_to([T, D])).then_inc(s_slw, 16)
            for gr in range(2):
                load_slots(sp, A, g, gr, gr)

        @block.gpsimd
        def _(pool):
            pool.memset(ones[:, :], 1.0).then_inc(s_ones, 1)
            pool.memset(vv[:, :, :, :], 0.0).then_inc(s_vset, 1)
            pool.wait_ge(s_ones, 1)
            pool.memset(xT[HALF:HALF + 1, :, 1, :], 1.0).then_inc(s_set, 1)
            pool.wait_ge(s_w, 7 * 16)

            def add_bias(b, i):
                item(pool, s_xn, b)
                hb = g.h[:, bass.ds(b, 1), :]
                pool.tensor_tensor(hb, hb, bo[:, :].unsqueeze(1), ALU.add).then_inc(s_bo, 1)

            def block_diagonal(b, i):
                item(pool, s_qks, b)
                reused(pool, s_sc, b, 2)
                k = i % 2
                for hf in range(2):
                    ins = pool.tensor_tensor(
                        kb[:, k, hf, :, :], qk[:, k, 2 + hf, :].unsqueeze(1).broadcast_to([HALF, HH, T]),
                        hmask[:, :].unsqueeze(2).broadcast_to([HALF, HH, T]), ALU.mult)
                ins.then_inc(s_kb, 1)

            def widen(b, i):
                item(pool, s_rs, b)
                reused(pool, s_rTp, b, 2)
                k = i % 2
                pool.tensor_tensor(rw[:, k, :, :], rs[:, k, :].unsqueeze(2).broadcast_to([T, NH, HPAD]),
                                   ones[:, :].unsqueeze(2).broadcast_to([T, NH, HPAD]), ALU.mult).then_inc(s_rw, 1)

            steps(pool, B, [(add_bias, 0), (widen, 3), (block_diagonal, 1)])

        @block.scalar
        def _(act):
            act.wait_ge(s_slw, 48)
            act.activation(sl_junk[:, :], sl[:, :], ACT.Square, accum_out=sl_n[:, 0:1]).then_inc(s_sl, 1)
            act.wait_ge(s_sl, 1)
            act.activation(sl_n[:, 1:2], sl_n[:, 0:1], ACT.Sqrt).then_inc(s_slroot, 1)
            act.wait_ge(s_vset, 1)

            def x_copy(b, i):
                item(act, s_xTp, b)
                reused(act, s_vp, b, 2)
                act.activation(xT[0:HALF, i % 2, :, :],
                               bank_x[0:HALF, 0:2 * T].rearrange("p (k t) -> p k t", k=2), ACT.Copy).then_inc(s_xTs, 1)

            def qk_copy(b, i):
                item(act, s_qkp, b)
                reused(act, s_sc, b, 2)
                reused(act, s_kb, b, 2)
                act.activation(qk[:, i % 2, :, :], bank_qk, ACT.Copy).then_inc(s_qks, 1)

            def v_copy(b, i):
                item(act, s_vp, b)
                reused(act, s_oTp, b, 4)
                act.activation(vv[:, i, :, 0:DH],
                               bank_x[0:T, 2 * T:2 * T + D].rearrange("p (h d) -> p h d", d=DH), ACT.Copy).then_inc(s_vs, 1)

            def exponent(b, i):
                item(act, s_sub, b)
                act.activation(p[:, i % 2, :, :], p[:, i % 2, :, :], ACT.Exp, scale=DH ** -0.5).then_inc(s_exp, 1)

            def p_copy(b, i):
                for r in range(NG):
                    act.wait_ge(s_pTp, b * NG + r + 1)
                    reused(act, s_oTp, b, 1)
                    act.activation(pT[:, r, :, :], bank_pT[r].rearrange("p (h t) -> p h t", t=T),
                                   ACT.Copy).then_inc(s_pTs, 1)

            def r_copy(b, i):
                item(act, s_rTp, b)
                reused(act, s_oTs, b, 1)
                act.activation(rT[:, :, :], bank_rT, ACT.Copy).then_inc(s_rTs, 1)

            steps(act, B, [(exponent, 3), (qk_copy, 1), (v_copy, 1), (p_copy, 3), (x_copy, 0), (r_copy, 3)])
            layernorm_scale(None, act, g, s_ln)

        @block.vector
        def _(v):

            def norm_input(b, i):
                reused(v, s_xTp, b, 2)
                v.tensor_scalar(xn[:, i % 2, :].unsqueeze(1), g.h[:, bass.ds(b, 1), :], g.rstd[:, bass.ds(b, 1)],
                                g.nmr[:, bass.ds(b, 1)], ALU.mult, ALU.add).then_inc(s_xn, 1)

            def residual(b, i):
                item(v, s_op, b)
                item(v, s_bo, b)
                hb = g.h[:, bass.ds(b, 1), :]
                v.tensor_tensor(hb, bank_out.unsqueeze(1), hb, ALU.add).then_inc(s_res, 1)
                v.wait_ge(s_res, b + 1)
                v.bn_stats(g.stats[:, bass.ds(b, 1), :].rearrange("p a s -> p (a s)"),
                           hb.rearrange("p a d -> p (a d)")).then_inc(s_st, 1)

            def maximum(b, i):
                item(v, s_sc, b)
                v.tensor_reduce(mx[:, i % 2, :].rearrange("p (r h) -> p r h", r=NG), scores, AX.X, ALU.max).then_inc(s_mx, 1)

            def subtract(b, i):
                item(v, s_mx, b)
                reused(v, s_pTp, b, 2, NG)
                v.tensor_tensor(p[:, i % 2, :, :].rearrange("p (r h) t -> p r h t", r=NG), scores,
                                mx[:, i % 2, :].rearrange("p (r h) -> p r h", r=NG).unsqueeze(3).broadcast_to([T, NG, HG, T]),
                                ALU.subtract).then_inc(s_sub, 1)

            def row_sum(b, i):
                item(v, s_exp, b)
                v.tensor_reduce(sm[:, i % 2, :], p[:, i % 2, :, :], AX.X, ALU.add).then_inc(s_sum, 1)
                item(v, s_sum, b)
                v.reciprocal(rs[:, i % 2, :], sm[:, i % 2, :]).then_inc(s_rs, 1)

            def divide(b, i):
                item(v, s_oTp, b)
                item(v, s_rTs, b)
                reused(v, s_op, b, 1)
                v.tensor_tensor(oT[:, :, :], bank_oT, rT[:, :, :], ALU.mult).then_inc(s_oTs, 1)

            v.wait_ge(s_slroot, 1)
            v.tensor_scalar(sl_n[:, 2:3], sl_n[:, 1:2], EPS, None, ALU.max).then_inc(s_sl, 1)
            v.wait_ge(s_sl, 2)
            v.reciprocal(sl_n[:, 3:4], sl_n[:, 2:3]).then_inc(s_sl, 1)
            v.wait_ge(s_sl, 3)
            v.tensor_scalar(sl[:, :], sl[:, :], sl_n[:, 3:4], sl_scale[:, 0:1], ALU.mult, ALU.mult).then_inc(s_sl, 1)
            v.wait_ge(s_slT, 1)
            v.tensor_copy(g.slT[:, :, :], slT_ps).then_inc(s_sl, 1)
            steps(v, B, [(divide, 4), (row_sum, 3), (residual, 5), (norm_input, 0), (maximum, 2), (subtract, 2)])
            v.wait_ge(s_st, B)
            layernorm_scale(v, None, g, s_ln)

        @block.tensor
        def _(pe):
            pe.wait_ge(g.s_const, 16)
            pe.wait_ge(s_sl, 4)
            for k in range(2):
                mm = pe.transpose(slT_ps[:, k, :], sl[:, k * HALF:(k + 1) * HALF], g.ident[0:NS, 0:NS])
            mm.then_inc(s_slT, 1)
            pe.wait_ge(s_w, 7 * 16)
            pe.wait_ge(s_set, 1)
            pe.wait_ge(s_sl, 5)

            def transpose_x(b, i):
                item(pe, s_xn, b)
                reused(pe, s_vs, b, 1)
                for hf in range(2):
                    mm = pe.transpose(bank_x[0:HALF, hf * T:(hf + 1) * T], xn[:, i % 2, hf * HALF:(hf + 1) * HALF],
                                      g.ident[0:T, 0:T])
                mm.then_inc(s_xTp, 1)

            def project(b, i):
                item(pe, s_xTs, b)
                reused(pe, s_qks, b, 1)
                k = i % 2
                for m in range(4):
                    pe.matmul(bank_qk[:, m, :], wqk[0:HALF, 0, m * HALF:(m + 1) * HALF], xT[0:HALF, k, 0, :],
                              start=True, stop=False)
                    mm = pe.matmul(bank_qk[:, m, :], wqk[:, 1, m * HALF:(m + 1) * HALF], xT[:, k, 1, :],
                                   start=False, stop=True)
                mm.then_inc(s_qkp, 1)
                pe.matmul(bank_x[0:T, 2 * T:2 * T + D], xT[0:HALF, k, 0, :], wv[0:HALF, 0, :], start=True, stop=False)
                pe.matmul(bank_x[0:T, 2 * T:2 * T + D], xT[:, k, 1, :], wv[:, 1, :], start=False, stop=True).then_inc(s_vp, 1)

            def score(b, i):
                item(pe, s_kb, b)
                reused(pe, s_sub, b, 1)
                k = i % 2
                q = [qk[:, k, hf, :] for hf in range(2)]
                for hf, h0, n, r, c in ((0, 0, 4, 0, 0), (0, 4, 2, 1, 0), (1, 0, 2, 1, 2), (1, 2, 4, 2, 0)):
                    mm = pe.matmul(g.ps[0:T, 3 + r, c * T:(c + n) * T], q[hf],
                                   kb[:, k, hf, h0:h0 + n, :].rearrange("p h t -> p (h t)"), start=True, stop=True)
                mm.then_inc(s_sc, 1)

            def attend(b, i):
                item(pe, s_exp, b)
                item(pe, s_vs, b)

                def turn(r):
                    if r == 2:
                        pe.wait_ge(s_pTs, b * NG + 1)
                    elif r == 0:
                        reused(pe, s_pTs, b, 1, NG)
                    else:
                        reused(pe, s_rTs, b, 1)
                    for j in range(HG):
                        mm = pe.transpose(bank_pT[r][:, j * T:(j + 1) * T], p[:, i % 2, r * HG + j, :], g.ident[0:T, 0:T])
                    mm.then_inc(s_pTp, 1)

                def values(r):
                    pe.wait_ge(s_pTs, b * NG + r + 1)
                    for j in range(HG):
                        mm = pe.matmul(bank_oT[HPAD * j:HPAD * (j + 1), r, :], vv[:, i, r * HG + j, :], pT[:, r, j, :],
                                       start=True, stop=True, tile_position=(0, HPAD * j))
                    return mm

                turn(0)
                turn(1)
                reused(pe, s_res, b, 2)
                reused(pe, s_oTs, b, 1)
                values(0)
                turn(2)
                pe.wait_ge(s_rw, b + 1)
                pe.wait_ge(s_pTs, b * NG + 2)
                for r in range(NG):
                    mm = pe.transpose(bank_rT[:, r, :], rw[:, i % 2, r * HG:(r + 1) * HG, :].rearrange("p h w -> p (h w)"),
                                      g.ident[0:T, 0:T])
                mm.then_inc(s_rTp, 1)
                values(1)
                values(2).then_inc(s_oTp, 1)

            def output(b, i):
                item(pe, s_oTs, b)
                reused(pe, s_res, b, 1)
                for r in range(NG):
                    mm = pe.matmul(bank_out, oT[:, r, :], wo[:, r, :], start=(r == 0), stop=(r == NG - 1))
                mm.then_inc(s_op, 1)

            steps(pe, B, [(project, 1), (score, 2), (transpose_x, 0), (attend, 3), (output, 4)])


def soft_moe(nc, A, g):
    with ExitStack() as ctx:
        def sb(name, shape, dt=F32):
            return ctx.enter_context(nc.sbuf_tensor("m_" + name, shape, dt))

        g.yT = sb("yT", [HALF, 2, NS, B])
        g.combT = sb("combT", [NS, B, T])
        dispatch(nc, A, g)
        g.y2 = sb("y2", [NS, B, D])
        slot_ffn(nc, A, g)
        combine(nc, A, g)


def dispatch(nc, A, g):
    NP = B // 2
    CH = 4
    NQ = B // CH
    with ExitStack() as ctx:
        def sem(name):
            return g.phase_sem("d_" + name)

        def sb(name, shape, dt=F32):
            return ctx.enter_context(nc.sbuf_tensor("d_" + name, shape, dt))

        u = sb("u", [T, B, D])
        junk = sb("junk", [T, D])
        xT = sb("xT", [HALF, 2, 2, 2, T])
        lg = sb("lg", [T, B, NS])
        dm = sb("dm", [NS, 2, CH, T])
        dT = sb("dT", [T, 2, CH, NS])
        cs = sb("cs", [T, 2, 3, CH])
        dsm = sb("dsm", [NS, 2, 3, CH])
        neg_mean = sb("neg_mean", [T, B])
        in_scale = sb("in_scale", [T, B])
        lg_scale = sb("lg_scale", [T, B])
        ss = sb("ss", [T, B])
        root = sb("root", [T, 2, B])
        t_ms = sb("t_ms", [T, B])
        (s_neg, s_u, s_sq, s_xTp, s_xTs, s_raw, s_ms, s_root, s_chain, s_scales, s_lg, s_lgT, s_cmx, s_csub, s_cexp,
         s_csum, s_crs, s_c, s_dmx, s_dsub, s_dexp, s_dsum, s_drs, s_d, s_dTp, s_cTp, s_dTs, s_cTs, s_yp, s_ys) = (
             sem(n) for n in ("neg", "u", "sq", "xTp", "xTs", "raw", "ms", "root", "chain", "scales", "lg", "lgT",
                              "cmx", "csub", "cexp", "csum", "crs", "c", "dmx", "dsub", "dexp", "dsum", "drs", "d",
                              "dTp", "cTp", "dTs", "cTs", "yp", "ys"))
        b_x = [g.ps[0:HALF, i, 0:4 * T].rearrange("p (b k t) -> p b k t", b=2, k=2) for i in range(2)]
        raw = g.ps[0:T, 4:8, :].rearrange("p n (b s) -> p (n b) s", s=NS)
        b_lgT = g.ps[0:NS, 0, 0:CH * T].rearrange("p (b t) -> p b t", b=CH)
        b_dT = g.ps[0:T, 1, 0:CH * NS].rearrange("p (b s) -> p b s", b=CH)
        b_cT = g.ps[0:NS, 2, 0:CH * T].rearrange("p (b t) -> p b t", b=CH)
        b_y = g.ps[0:HALF, 3, 0:2 * CH * NS].rearrange("p (b k s) -> p b k s", b=CH, k=2)
        block = ctx.enter_context(nc.Block())

        def wide(small, n):
            return small.unsqueeze(2).broadcast_to([small.shape[0], small.shape[1], n])

        def chunk(q):
            return slice(q * CH, (q + 1) * CH)

        @block.vector
        def _(v):
            v.tensor_scalar(neg_mean[:, :], g.lnt[:, 0, :], -0.5, None, ALU.mult).then_inc(s_neg, 1)
            v.tensor_tensor(t_ms[:, :], g.rstd[:, :], g.rstd[:, :], ALU.mult).then_inc(s_chain, 1)
            v.wait_ge(s_chain, 1)
            v.tensor_scalar(t_ms[:, :], t_ms[:, :], -EPS, 1.0 + EPS, ALU.mult, ALU.add).then_inc(s_ms, 1)
            v.wait_ge(s_neg, 1)
            with v.Fori(0, B // UNROLL) as j:
                for i in range(UNROLL):
                    b = j * UNROLL + i
                    v.scalar_tensor_tensor(u[:, bass.ds(b, 1), :], g.h[:, bass.ds(b, 1), :], neg_mean[:, bass.ds(b, 1)],
                                           g.nw[:, :].unsqueeze(1), ALU.add, ALU.mult).then_inc(s_u, 1)
            v.wait_ge(s_root, 1)
            v.reciprocal(in_scale[:, :], root[:, 0, :]).then_inc(s_chain, 1)
            v.wait_ge(s_chain, 2)
            v.tensor_tensor(in_scale[:, :], in_scale[:, :], g.rstd[:, :], ALU.mult).then_inc(s_chain, 1)
            v.wait_ge(s_chain, 3)
            v.wait_ge(s_root, 2)
            v.tensor_tensor(ss[:, :], in_scale[:, :], root[:, 1, :], ALU.mult).then_inc(s_chain, 1)
            v.wait_ge(s_chain, 4)
            v.tensor_scalar(ss[:, :], ss[:, :], EPS, None, ALU.max).then_inc(s_chain, 1)
            v.wait_ge(s_chain, 5)
            v.reciprocal(lg_scale[:, :], ss[:, :]).then_inc(s_chain, 1)
            v.wait_ge(s_chain, 6)
            v.tensor_tensor(lg_scale[:, :], lg_scale[:, :], in_scale[:, :], ALU.mult).then_inc(s_scales, 1)
            v.wait_ge(s_scales, 1)
            v.wait_ge(s_raw, NP)

            def logits(q, i):
                v.tensor_tensor(lg[:, chunk(q), :], raw[:, chunk(q), :], wide(lg_scale[:, chunk(q)], NS),
                                ALU.mult).then_inc(s_lg, 1)
                item(v, s_lg, q)
                reused(v, s_csub, q, 2)
                v.tensor_reduce(cs[:, i, 0, :], lg[:, chunk(q), :], AX.X, ALU.max).then_inc(s_cmx, 1)

            def dispatch_max(q, i):
                item(v, s_lgT, q)
                v.tensor_reduce(dsm[:, i, 0, :], b_lgT, AX.X, ALU.max).then_inc(s_dmx, 1)
                item(v, s_dmx, q)
                reused(v, s_dTp, q, 2)
                v.tensor_tensor(dm[:, i, :, :], b_lgT, wide(dsm[:, i, 0, :], T), ALU.subtract).then_inc(s_dsub, 1)

            def combine_sum(q, i):
                item(v, s_cexp, q)
                v.tensor_reduce(cs[:, i, 1, :], lg[:, chunk(q), :], AX.X, ALU.add).then_inc(s_csum, 1)
                item(v, s_csum, q)
                reused(v, s_c, q, 2)
                v.reciprocal(cs[:, i, 2, :], cs[:, i, 1, :]).then_inc(s_crs, 1)

            def dispatch_sum(q, i):
                item(v, s_dexp, q)
                v.tensor_reduce(dsm[:, i, 1, :], dm[:, i, :, :], AX.X, ALU.add).then_inc(s_dsum, 1)
                item(v, s_dsum, q)
                reused(v, s_d, q, 2)
                v.reciprocal(dsm[:, i, 2, :], dsm[:, i, 1, :]).then_inc(s_drs, 1)

            def scale_turned(q, i):
                item(v, s_dTp, q)
                reused(v, s_yp, q, 2)
                v.tensor_tensor(dT[:, i, :, :], b_dT, wide(in_scale[:, chunk(q)], NS), ALU.mult).then_inc(s_dTs, 1)

            few_steps(NQ, [(dispatch_max, 1), (logits, 0), (scale_turned, 2), (dispatch_sum, 1), (combine_sum, 1)])

        @block.gpsimd
        def _(pool):
            def combine_sub(q, i):
                item(pool, s_cmx, q)
                item(pool, s_lgT, q)
                pool.tensor_tensor(lg[:, chunk(q), :], lg[:, chunk(q), :], wide(cs[:, i, 0, :], NS),
                                   ALU.subtract).then_inc(s_csub, 1)

            def scale_c(q, i):
                item(pool, s_crs, q)
                pool.tensor_tensor(lg[:, chunk(q), :], lg[:, chunk(q), :], wide(cs[:, i, 2, :], NS),
                                   ALU.mult).then_inc(s_c, 1)

            def scale_d(q, i):
                item(pool, s_drs, q)
                pool.tensor_tensor(dm[:, i, :, :], dm[:, i, :, :], wide(dsm[:, i, 2, :], T), ALU.mult).then_inc(s_d, 1)

            few_steps(NQ, [(combine_sub, 0), (scale_d, 1), (scale_c, 1)])

        @block.scalar
        def _(act):
            act.wait_ge(s_ms, 1)
            act.activation(root[:, 0, :], t_ms[:, :], ACT.Sqrt).then_inc(s_root, 1)

            def x_copy(q, i):
                item(act, s_xTp, q)
                reused(act, s_raw, q, 2)
                act.activation(xT[:, i % 2, :, :, :], b_x[i % 2], ACT.Copy).then_inc(s_xTs, 1)

            def square(q, i):
                for b in range(2):
                    act.wait_ge(s_u, q * 2 + b + 1)
                    reused(act, s_sq, q, 1, 2)
                    act.activation(junk[:, :].unsqueeze(1), u[:, bass.ds(q * 2 + b, 1), :], ACT.Square,
                                   accum_out=ss[:, bass.ds(q * 2 + b, 1)]).then_inc(s_sq, 1)
                    act.wait_ge(s_sq, q * 2 + b + 1)

            steps(act, NP, [(x_copy, 1), (square, 0)])
            act.activation(root[:, 1, :], ss[:, :], ACT.Sqrt).then_inc(s_root, 1)

            def combine_exp(q, i):
                item(act, s_csub, q)
                act.activation(lg[:, chunk(q), :], lg[:, chunk(q), :], ACT.Exp).then_inc(s_cexp, 1)

            def dispatch_exp(q, i):
                item(act, s_dsub, q)
                act.activation(dm[:, i, :, :], dm[:, i, :, :], ACT.Exp).then_inc(s_dexp, 1)

            def turned_copy(q, i):
                item(act, s_cTp, q)
                act.activation(g.combT[:, chunk(q), :], b_cT, ACT.Copy).then_inc(s_cTs, 1)

            def y_copy(q, i):
                item(act, s_yp, q)
                act.activation(g.yT[:, :, :, chunk(q)].rearrange("p k s b -> p b k s"), b_y,
                               ACT.Copy).then_inc(s_ys, 1)

            few_steps(NQ, [(dispatch_exp, 1), (combine_exp, 1), (turned_copy, 2), (y_copy, 3)])

        @block.tensor
        def _(pe):
            def transpose_x(q, i):
                item(pe, s_u, q, 2)
                reused(pe, s_xTs, q, 2)
                for b in range(2):
                    for k in range(2):
                        mm = pe.transpose(b_x[i % 2][:, b, k, :], u[:, q * 2 + b, k * HALF:(k + 1) * HALF],
                                          g.ident[0:T, 0:T])
                mm.then_inc(s_xTp, 1)

            def products(q, i):
                item(pe, s_xTs, q)
                for b in range(2):
                    for k in range(2):
                        mm = pe.matmul(raw[:, q * 2 + b, :], xT[:, i % 2, b, k, :], g.slT[:, k, :], start=(k == 0), stop=(k == 1))
                mm.then_inc(s_raw, 1)

            def transpose_logits(q, i):
                item(pe, s_lg, q)
                reused(pe, s_dsub, q, 1)
                for b in range(CH):
                    mm = pe.transpose(b_lgT[:, b, :], lg[:, q * CH + b, :],
                                      g.ident[0:T, 0:T])
                mm.then_inc(s_lgT, 1)

            def transpose_weights(q, i):
                item(pe, s_d, q)
                reused(pe, s_dTs, q, 1)
                for b in range(CH):
                    mm = pe.transpose(b_dT[:, b, :], dm[:, i, b, :], g.ident[0:NS, 0:NS])
                mm.then_inc(s_dTp, 1)
                item(pe, s_c, q)
                reused(pe, s_cTs, q, 1)
                for b in range(CH):
                    mm = pe.transpose(b_cT[:, b, :], lg[:, q * CH + b, :],
                                      g.ident[0:T, 0:T])
                mm.then_inc(s_cTp, 1)

            def gather(q, i):
                item(pe, s_dTs, q)
                reused(pe, s_ys, q, 1)
                for b in range(CH):
                    for k in range(2):
                        mm = pe.matmul(b_y[:, b, k, :], u[:, q * CH + b, k * HALF:(k + 1) * HALF], dT[:, i, b, :],
                                       start=True, stop=True)
                mm.then_inc(s_yp, 1)

            few_steps(NP, [(transpose_x, 0), (products, 1)])
            few_steps(NQ, [(transpose_logits, 0), (transpose_weights, 2), (gather, 3)])


def slot_ffn(nc, A, g):
    with ExitStack() as ctx:
        def sem(name):
            return g.phase_sem("f_" + name)

        def sb(name, shape, dt=F32):
            return ctx.enter_context(nc.sbuf_tensor("f_" + name, shape, dt))

        yg = sb("yg", [HALF + 1, 2, 2, GS, B])
        hid = sb("hid", [128, 2, F])
        hT = sb("hT", [128, 2, FC, 128])
        b2 = sb("b2", [128, NGR, D])
        y2g = sb("y2g", [128, 2, D])
        s_b2, s_one, s_yg, s_h1, s_gelu, s_hTp, s_hTs, s_y2p, s_y2s = (
            sem(n) for n in ("b2", "one", "yg", "h1", "gelu", "hTp", "hTs", "y2p", "y2s"))
        s_y2 = [sem(f"y2_{i}") for i in range(2)]
        N2 = F // 2
        block = ctx.enter_context(nc.Block())

        @block.sync
        def _(sp):
            bias = A["fc2_b"].rearrange("(g s) d -> s g d", s=GS)
            for s in range(GS):
                sp.dma_start(b2[B * s:B * (s + 1), :, :], bias[s].unsqueeze(0).broadcast_to([B, NGR, D])).then_inc(s_b2, 16)
            with sp.Fori(1, NGR // 2) as j:
                for u in range(2):
                    load_slots(sp, A, g, j * 2 + u, u, lambda: sp.wait_ge(s_h1, j * 2 + (u - 1)),
                               lambda: sp.wait_ge(s_y2p, j * 2 + (u - 1)))

        @block.gpsimd
        def _(pool):
            pool.memset(yg[HALF:HALF + 1, :, 1, :, :], 1.0).then_inc(s_one, 1)

            def pick(gr, i):
                reused(pool, s_h1, gr, 2)
                pool.tensor_copy(yg[0:HALF, i, :, :, :], g.yT[:, :, bass.ds(gr * GS, GS), :]).then_inc(s_yg, 1)

            steps(pool, NGR, [(pick, 0)], unroll=2, depth=2)

        @block.scalar
        def _(act):
            def gelu(gr, i):
                reused(act, s_hTp, gr, 2, 2)
                for n in range(2):
                    act.wait_ge(s_h1, gr + 1)
                    act.activation(hid[:, i, n * N2:(n + 1) * N2], g.ps[:, n, 0:N2], ACT.Gelu).then_inc(s_gelu, 1)

            def put(gr, i):
                item(act, s_y2s, gr)
                act.dma_start(g.y2[gr * GS:(gr + 1) * GS, :, :], y2g[:, i, :]).then_inc(s_y2[i], 16)

            for t in range(NGR + 1):
                if t < NGR:
                    gelu(t, t % 2)
                if t >= 1:
                    put(t - 1, (t - 1) % 2)
            for i in range(2):
                act.wait_ge(s_y2[i], 16 * NGR // 2)

        @block.vector
        def _(v):
            v.wait_ge(s_b2, 16 * GS)

            def turn_copy(gr, i):
                reused(v, s_y2p, gr, 2)
                for n in range(2):
                    v.wait_ge(s_hTp, gr * 2 + n + 1)
                    v.tensor_copy(hT[:, i, 3 * n:3 * n + 3, :], g.ps[:, 2 + n, 0:384].rearrange("p (k m) -> p k m", k=3)).then_inc(s_hTs, 1)

            def add_bias(gr, i):
                item(v, s_y2p, gr)
                if not isinstance(gr, int):
                    v.wait_ge(s_y2[i], (gr - i) * 8)
                elif gr >= 2:
                    v.wait_ge(s_y2[i], 16 * (gr // 2))
                v.tensor_tensor(y2g[:, i, :].unsqueeze(1), g.ps[:, 4, 0:D].unsqueeze(1),
                                b2[:, bass.ds(gr, 1), :], ALU.add).then_inc(s_y2s, 1)

            steps(v, NGR, [(turn_copy, 1), (add_bias, 1)], unroll=2, depth=2)

        @block.tensor
        def _(pe):
            pe.wait_ge(s_one, 1)

            def loaded(sems, gr, i, dmas):
                if isinstance(gr, int):
                    pe.wait_ge(sems[i], 16 * dmas * (gr // 2 + 1))
                else:
                    pe.wait_ge(sems[i], (gr - i) * (8 * dmas) + 16 * dmas)

            def first(gr, i):
                item(pe, s_yg, gr)
                loaded(g.s_w1, gr, i, W1_DMAS)
                reused(pe, s_gelu, gr, 1, 2)
                for n in range(2):
                    for k in range(2):
                        rows = HALF + k
                        for s in range(GS):
                            mm = pe.matmul(g.ps[B * s:B * (s + 1), n, 0:N2], yg[0:rows, i, k, s, :],
                                           g.w1[0:rows, i, k, s, n * N2:(n + 1) * N2],
                                           start=(k == 0), stop=(k == 1), tile_position=(0, B * s))
                mm.then_inc(s_h1, 1)

            def turn(gr, i):
                item(pe, s_gelu, gr, 2)
                for n in range(2):
                    if not isinstance(gr, int) or gr >= 1:
                        pe.wait_ge(s_hTs, gr * 2 + n - 1)
                    for k in range(3):
                        mm = pe.transpose(g.ps[:, 2 + n, 128 * k:128 * (k + 1)], hid[:, i, 3 * n + k:F:FC], g.ident[:, :])
                    mm.then_inc(s_hTp, 1)

            def second(gr, i):
                item(pe, s_hTs, gr, 2)
                loaded(g.s_w2, gr, i, 1)
                reused(pe, s_y2s, gr, 1)
                for k in range(FC):
                    for s in range(GS):
                        mm = pe.matmul(g.ps[B * s:B * (s + 1), 4, 0:D], hT[:, i, k, B * s:B * (s + 1)],
                                       g.w2[:, i, s, k * D:(k + 1) * D], start=(k == 0), stop=(k == FC - 1),
                                       tile_position=(0, B * s))
                mm.then_inc(s_y2p, 1)

            steps(pe, NGR, [(turn, 1), (first, 0), (second, 1)], unroll=2, depth=2)


def combine(nc, A, g):
    with ExitStack() as ctx:
        def sem(name):
            return g.phase_sem("c_" + name)

        cT = ctx.enter_context(nc.sbuf_tensor("c_cT", [NS, UNROLL, T], F32))
        s_cT, s_mm, s_res, s_st, s_ln = (sem(n) for n in ("cT", "mm", "res", "st", "ln"))
        block = ctx.enter_context(nc.Block())

        @block.gpsimd
        def _(pool):
            def pick(b, i):
                reused(pool, s_mm, b, 4)
                pool.tensor_copy(cT[:, i, :].unsqueeze(1), g.combT[:, bass.ds(b, 1), :]).then_inc(s_cT, 1)

            steps(pool, B, [(pick, 0)])

        @block.tensor
        def _(pe):
            def mix(b, i):
                item(pe, s_cT, b)
                reused(pe, s_res, b, 4)
                pe.matmul(g.ps[0:T, i, 0:D], cT[:, i, :], g.y2[:, bass.ds(b, 1), :].rearrange("p a d -> p (a d)"),
                          start=True, stop=True).then_inc(s_mm, 1)

            steps(pe, B, [(mix, 0)])

        @block.vector
        def _(v):
            def residual(b, i):
                item(v, s_mm, b)
                hb = g.h[:, bass.ds(b, 1), :]
                v.tensor_tensor(hb, g.ps[0:T, i, 0:D].unsqueeze(1), hb, ALU.add).then_inc(s_res, 1)

            def statistics(b, i):
                item(v, s_res, b)
                v.bn_stats(g.stats[:, bass.ds(b, 1), :].rearrange("p a s -> p (a s)"),
                           g.h[:, bass.ds(b, 1), :].rearrange("p a d -> p (a d)")).then_inc(s_st, 1)

            steps(v, B, [(residual, 0), (statistics, 1)])
            v.wait_ge(s_st, B)
            layernorm_scale(v, None, g, s_ln)

        @block.scalar
        def _(act):
            layernorm_scale(None, act, g, s_ln)


def attention1(nc, A, g):
    with ExitStack() as ctx:
        def sem(name):
            return g.phase_sem("b_" + name)

        def sb(name, shape, dt=F32):
            return ctx.enter_context(nc.sbuf_tensor("b_" + name, shape, dt))

        wqkv = sb("wqkv", [HALF, 2, 3 * D])
        cos = sb("cos", [T, 2 * D])
        sin = sb("sin", [T, D])
        nsin = sb("nsin", [T, D])
        mask = sb("mask", [T, T])
        xn = sb("xn", [T, 2, D])
        xT = sb("xT", [HALF, 2, 2, T])
        vv = sb("vv", [T, 4, D])
        ra = sb("ra", [T, 2, 2 * D])
        rb = sb("rb", [T, 2, 2 * D])
        qkT = sb("qkT", [HALF, 2, 4, T])
        p = sb("p", [T, 2, T])
        pT = sb("pT", [T, 2, T])
        sc = sb("sc", [T, 4, 4])
        (s_w, s_xn, s_xTp, s_xTs, s_qk, s_v, s_vs, s_ra, s_rot, s_rTp, s_rTs, s_sc, s_msk, s_mx, s_nm, s_exp, s_rs,
         s_pTp, s_pTs, s_o, s_res, s_st, s_ln) = (sem(n) for n in (
             "w", "xn", "xTp", "xTs", "qk", "v", "vs", "ra", "rot", "rTp", "rTs", "sc", "msk", "mx", "nm", "exp", "rs",
             "pTp", "pTs", "o", "res", "st", "ln"))
        b_x = g.ps[0:HALF, 0, 0:2 * T].rearrange("p (k t) -> p k t", k=2)
        b_qk = g.ps[0:T, 1, 0:2 * D]
        b_v = g.ps[0:T, 2, 0:D]
        b_rT = g.ps[0:HALF, 3, 0:4 * T].rearrange("p (m t) -> p m t", m=4)
        b_sc = g.ps[0:T, 4, 0:T]
        b_pT = g.ps[0:T, 5, 0:T]
        b_o = g.ps[0:T, 6, 0:D]
        SCALE = D ** -0.5
        block = ctx.enter_context(nc.Block())

        @block.sync
        def _(sp):
            sp.dma_start(wqkv[:, :, :], A["a1_wqkv"].rearrange("(k p) n -> p k n", k=2)).then_inc(s_w, 16)
            sp.dma_start(cos[:, :], A["rope_cos"]).then_inc(s_w, 16)
            sp.dma_start(sin[:, :], A["rope_sin"]).then_inc(s_w, 16)
            sp.dma_start(nsin[:, :], A["rope_nsin"]).then_inc(s_w, 16)
            sp.dma_start(mask[:, :], A["causal"]).then_inc(s_w, 16)
            for k in range(2):
                sp.dma_start(g.e1[0:HALF, k, :, :], A["moe_w1"][:, k * HALF:(k + 1) * HALF, :].rearrange(
                    "e p n -> p e n")).then_inc(g.s_e, 16)
            sp.dma_start(g.e1[HALF:HALF + 1, 1, :, :], A["moe_b1"].unsqueeze(0)).then_inc(g.s_e, 16)
            for k in range(FC):
                sp.dma_start(g.e2[:, k, :, :], A["moe_w2"][:, k * 128:(k + 1) * 128, :].rearrange(
                    "e p n -> p e n")).then_inc(g.s_e, 16)

        @block.vector
        def _(v):
            v.wait_ge(s_w, 5 * 16)

            def norm_input(b, i):
                reused(v, s_xTp, b, 2)
                v.tensor_scalar(xn[:, i % 2, :].unsqueeze(1), g.h[:, bass.ds(b, 1), :], g.rstd[:, bass.ds(b, 1)],
                                g.nmr[:, bass.ds(b, 1)], ALU.mult, ALU.add).then_inc(s_xn, 1)

            def rotate(b, i):
                k = i % 2
                item(v, s_qk, b)
                reused(v, s_rTp, b, 2)
                pair = b_qk.rearrange("p (n two) -> p n two", two=2)
                out = rb[:, k, :].rearrange("p (n two) -> p n two", two=2)
                v.tensor_tensor(ra[:, k, :], b_qk, cos[:, :], ALU.mult)
                v.tensor_tensor(out[:, :, 0], pair[:, :, 1], nsin[:, :], ALU.mult)
                v.tensor_tensor(out[:, :, 1], pair[:, :, 0], sin[:, :], ALU.mult).then_inc(s_ra, 1)

            def soften(b, i):
                k = i % 2
                item(v, s_sc, b)
                reused(v, s_pTp, b, 2)
                v.tensor_tensor(p[:, k, :], b_sc, mask[:, :], ALU.add).then_inc(s_msk, 1)
                item(v, s_msk, b)
                v.tensor_reduce(sc[:, i, 0:1], p[:, k, :], AX.X, ALU.max).then_inc(s_mx, 1)
                item(v, s_mx, b)
                v.tensor_scalar(sc[:, i, 1:2], sc[:, i, 0:1], -SCALE, None, ALU.mult).then_inc(s_nm, 1)

            def inverse(b, i):
                item(v, s_exp, b)
                v.reciprocal(sc[:, i, 3:4], sc[:, i, 2:3]).then_inc(s_rs, 1)

            def residual(b, i):
                item(v, s_rs, b)
                item(v, s_o, b)
                hb = g.h[:, bass.ds(b, 1), :]
                v.scalar_tensor_tensor(hb, b_o.unsqueeze(1), sc[:, i, 3:4], hb, ALU.mult, ALU.add).then_inc(s_res, 1)

            def statistics(b, i):
                item(v, s_res, b)
                v.bn_stats(g.stats[:, bass.ds(b, 1), :].rearrange("p a s -> p (a s)"),
                           g.h[:, bass.ds(b, 1), :].rearrange("p a d -> p (a d)")).then_inc(s_st, 1)

            steps(v, B, [(inverse, 3), (residual, 4), (norm_input, 0), (statistics, 4), (rotate, 1), (soften, 2)])
            v.wait_ge(s_st, B)
            layernorm_scale(v, None, g, s_ln)

        @block.gpsimd
        def _(pool):
            def add_parts(b, i):
                k = i % 2
                item(pool, s_ra, b)
                pool.tensor_tensor(ra[:, k, :], ra[:, k, :], rb[:, k, :], ALU.add).then_inc(s_rot, 1)

            steps(pool, B, [(add_parts, 1)])

        @block.scalar
        def _(act):
            def x_copy(b, i):
                item(act, s_xTp, b)
                reused(act, s_v, b, 2)
                act.activation(xT[:, i % 2, :, :], b_x, ACT.Copy).then_inc(s_xTs, 1)

            def r_copy(b, i):
                item(act, s_rTp, b)
                reused(act, s_sc, b, 2)
                act.activation(qkT[:, i % 2, :, :], b_rT, ACT.Copy).then_inc(s_rTs, 1)

            def p_copy(b, i):
                item(act, s_pTp, b)
                reused(act, s_o, b, 2)
                act.activation(pT[:, i % 2, :], b_pT, ACT.Copy).then_inc(s_pTs, 1)

            def v_copy(b, i):
                item(act, s_v, b)
                reused(act, s_o, b, 4)
                act.activation(vv[:, i, :], b_v, ACT.Copy).then_inc(s_vs, 1)

            def exponent(b, i):
                item(act, s_nm, b)
                reused(act, s_res, b, 4)
                act.activation(p[:, i % 2, :], p[:, i % 2, :], ACT.Exp, scale=SCALE, bias=sc[:, i, 1:2],
                               accum_out=sc[:, i, 2:3]).then_inc(s_exp, 1)

            steps(act, B, [(x_copy, 1), (r_copy, 2), (p_copy, 3), (v_copy, 1), (exponent, 2)])
            layernorm_scale(None, act, g, s_ln)

        @block.tensor
        def _(pe):
            pe.wait_ge(s_w, 5 * 16)

            def transpose_x(b, i):
                item(pe, s_xn, b)
                reused(pe, s_xTs, b, 1)
                for k in range(2):
                    mm = pe.transpose(b_x[:, k, :], xn[:, i % 2, k * HALF:(k + 1) * HALF], g.ident[0:T, 0:T])
                mm.then_inc(s_xTp, 1)

            def transpose_qk(b, i):
                item(pe, s_rot, b)
                reused(pe, s_rTs, b, 1)
                for m in range(4):
                    mm = pe.transpose(b_rT[:, m, :], ra[:, i % 2, m * HALF:(m + 1) * HALF], g.ident[0:T, 0:T])
                mm.then_inc(s_rTp, 1)

            def transpose_p(b, i):
                item(pe, s_exp, b)
                reused(pe, s_pTs, b, 1)
                pe.transpose(b_pT, p[:, i % 2, :], g.ident[0:T, 0:T]).then_inc(s_pTp, 1)

            def project(b, i):
                item(pe, s_xTs, b)
                reused(pe, s_ra, b, 1)
                reused(pe, s_vs, b, 1)
                for k in range(2):
                    mm = pe.matmul(b_qk, xT[:, i % 2, k, :], wqkv[:, k, 0:2 * D], start=(k == 0), stop=(k == 1))
                mm.then_inc(s_qk, 1)
                for k in range(2):
                    mm = pe.matmul(b_v, xT[:, i % 2, k, :], wqkv[:, k, 2 * D:3 * D], start=(k == 0), stop=(k == 1))
                mm.then_inc(s_v, 1)

            def score(b, i):
                item(pe, s_rTs, b)
                reused(pe, s_msk, b, 1)
                for k in range(2):
                    mm = pe.matmul(b_sc, qkT[:, i % 2, k, :], qkT[:, i % 2, 2 + k, :], start=(k == 0), stop=(k == 1))
                mm.then_inc(s_sc, 1)

            def attend(b, i):
                item(pe, s_pTs, b)
                item(pe, s_vs, b)
                reused(pe, s_res, b, 1)
                pe.matmul(b_o, pT[:, i % 2, :], vv[:, i, :], start=True, stop=True).then_inc(s_o, 1)

            steps(pe, B, [(transpose_x, 1), (transpose_qk, 2), (transpose_p, 3), (project, 1), (score, 2), (attend, 3)])


def gate(nc, A, g):
    with ExitStack() as ctx:
        def sem(name):
            return g.phase_sem("g_" + name)

        def sb(name, shape, dt=F32):
            return ctx.enter_context(nc.sbuf_tensor("g_" + name, shape, dt))

        wr = sb("wr", [HALF, 2, NE])
        xn = sb("xn", [T, UNROLL, D])
        xT = sb("xT", [HALF, 2, 2, T])
        zero = sb("zero", [128, D])
        s_w, s_zero, s_tab, s_xn, s_xTp, s_xTs, s_lgp, s_lgs = (
            sem(n) for n in ("w", "zero", "tab", "xn", "xTp", "xTs", "lgp", "lgs"))
        s_put = [sem(f"put{i}") for i in range(UNROLL)]
        b_x = [g.ps[0:HALF, i, 0:2 * T].rearrange("p (k t) -> p k t", k=2) for i in range(2)]
        b_lg = [g.ps[0:T, 2 + i, 0:NE] for i in range(2)]
        block = ctx.enter_context(nc.Block())

        @block.sync
        def _(sp):
            sp.dma_start(wr[:, :, :], A["moe_wr"].rearrange("(k p) e -> p k e", k=2)).then_inc(s_w, 16)
            sp.dma_start(A["out"][0:NTOK, :].rearrange("(b t) d -> t b d", t=T), g.h[:, :, :]).then_inc(s_tab, 16)
            sp.wait_ge(s_zero, 1)
            sp.dma_start(A["out"][NTOK:NTOK + 128, :], zero[:, :]).then_inc(s_tab, 16)
            sp.dma_start(A["xtab"][NTOK:NTOK + 128, :], zero[:, :]).then_inc(s_tab, 16)

            def put(b, i):
                item(sp, s_xn, b)
                sp.dma_start(A["xtab"][bass.ds(b * T, T), :], xn[:, i, :]).then_inc(s_put[i], 16)

            steps(sp, B, [(put, 0)])
            sp.wait_ge(s_tab, 48)
            for i in range(UNROLL):
                sp.wait_ge(s_put[i], 16 * B // UNROLL)

        @block.gpsimd
        def _(pool):
            pool.memset(zero[:, :], 0.0).then_inc(s_zero, 1)

        @block.vector
        def _(v):
            def norm_input(b, i):
                reused(v, s_xTp, b, UNROLL)
                if not isinstance(b, int):
                    v.wait_ge(s_put[i], (b - i) * (16 // UNROLL))
                elif b >= UNROLL:
                    v.wait_ge(s_put[i], 16 * (b // UNROLL))
                v.tensor_scalar(xn[:, i, :].unsqueeze(1), g.h[:, bass.ds(b, 1), :], g.rstd[:, bass.ds(b, 1)],
                                g.nmr[:, bass.ds(b, 1)], ALU.mult, ALU.add).then_inc(s_xn, 1)

            def keep(b, i):
                item(v, s_lgp, b)
                v.tensor_copy(g.lg[:, bass.ds(b, 1), :], b_lg[i % 2].unsqueeze(1)).then_inc(s_lgs, 1)

            steps(v, B, [(norm_input, 0), (keep, 2)])

        @block.scalar
        def _(act):
            def x_copy(b, i):
                item(act, s_xTp, b)
                reused(act, s_lgp, b, 2)
                act.activation(xT[:, i % 2, :, :], b_x[i % 2], ACT.Copy).then_inc(s_xTs, 1)

            steps(act, B, [(x_copy, 0)])

        @block.tensor
        def _(pe):
            pe.wait_ge(s_w, 16)

            def transpose_x(b, i):
                item(pe, s_xn, b)
                reused(pe, s_xTs, b, 2)
                for k in range(2):
                    mm = pe.transpose(b_x[i % 2][:, k, :], xn[:, i, k * HALF:(k + 1) * HALF], g.ident[0:T, 0:T])
                mm.then_inc(s_xTp, 1)

            def logits(b, i):
                item(pe, s_xTs, b)
                reused(pe, s_lgs, b, 2)
                for k in range(2):
                    mm = pe.matmul(b_lg[i % 2], xT[:, i % 2, k, :], wr[:, k, :], start=(k == 0), stop=(k == 1))
                mm.then_inc(s_lgp, 1)

            steps(pe, B, [(transpose_x, 0), (logits, 1)])


def route(nc, A, g):
    with ExitStack() as ctx:
        def sem(name):
            return g.phase_sem("r1_" + name)

        def sb(name, shape, dt=F32):
            return ctx.enter_context(nc.sbuf_tensor("r1_" + name, shape, dt))

        iota = sb("iota", [128, 128])
        padrow = sb("padrow", [128, 2])
        before = sb("before", [T, T])
        tokid = sb("tokid", [T, B])
        ones = sb("ones", [T, 256])
        key = sb("key", [T, B, NE])
        oh = sb("oh", [T, 2, B, NE])
        lg2 = sb("lg2", [T, B, NE])
        both = sb("both", [T, B, NE])
        m = sb("m", [T, 2, B])
        ex = sb("ex", [T, B])
        c = sb("c", [T, 2, B])
        cnt = sb("cnt", [T, NE, B])
        cum = sb("cum", [T, NE, B])
        pos = sb("pos", [T, NE, B])
        e8 = sb("e8", [T, 6, NE])
        place = sb("place", [T, 2, B])
        tile = sb("tile", [T, 2, B])
        row = sb("row", [T, 2, B])
        ohp = sb("ohp", [T, NPAIR, 128])
        info = sb("info", [T, NPAIR, 3, NTILES])
        tge = sb("tge", [T, NTILES, NE])
        tef = sb("tef", [T, NTILES])
        lst = sb("lst", [128, 2, NTILES])
        s_w, s_ones, s_v, s_d, s_ex, s_both, s_pre, s_occ, s_info, s_ohp, s_list = (
            sem(n) for n in ("w", "ones", "v", "d", "ex", "both", "pre", "occ", "info", "ohp", "list"))
        MAGIC = 1.5 * 2 ** 23
        b_intra = g.ps[0:T, 0, 0:256].rearrange("p (e b) -> p e b", e=NE)
        b_cnt = g.ps[0:T, 1, 0:256].rearrange("p (e b) -> p e b", e=NE)
        b_list = g.ps[:, 2, 0:3 * NTILES].rearrange("p (c n) -> p c n", c=3)
        block = ctx.enter_context(nc.Block())

        @block.sync
        def _(sp):
            sp.dma_start(iota[:, :], A["iota"]).then_inc(s_w, 16)
            sp.dma_start(padrow[:, :], A["padrow"]).then_inc(s_w, 16)
            sp.dma_start(before[:, :], A["before"]).then_inc(s_w, 16)
            sp.dma_start(tokid[:, :], A["tokid"]).then_inc(s_w, 16)

        @block.gpsimd
        def _(pool):
            pool.memset(ones[:, :], 1.0).then_inc(s_ones, 1)
            pool.wait_ge(s_occ, 1)
            for k in range(2):
                cols = slice(k * B, (k + 1) * B)
                pool.tensor_tensor(info[:, cols, 1, :], info[:, cols, 0, :],
                                   tokid[:, :].unsqueeze(2).broadcast_to([T, B, NTILES]), ALU.mult).then_inc(s_info, 1)

        @block.scalar
        def _(act):
            act.wait_ge(s_d, 1)
            act.activation(ex[:, :], ex[:, :], ACT.Exp).then_inc(s_ex, 1)

        @block.vector
        def _(v):
            done = [0]

            def link(ins):
                done[0] += 1
                ins.then_inc(s_v, 1)
                v.wait_ge(s_v, done[0])

            def wide(x, n):
                return x.unsqueeze(2).broadcast_to([x.shape[0], x.shape[1], n])

            v.wait_ge(s_w, 64)
            v.wait_ge(s_ones, 1)
            experts = iota[0:T, 0:NE].unsqueeze(1).broadcast_to([T, B, NE])
            for k in range(2):
                src = g.lg if k == 0 else lg2
                link(v.tensor_reduce(m[:, k, :], src[:, :, :], AX.X, ALU.max))
                link(v.tensor_tensor(key[:, :, :], src[:, :, :], wide(m[:, k, :], NE), ALU.is_equal))
                link(v.scalar_tensor_tensor(key[:, :, :], key[:, :, :], -float(NE), experts, ALU.mult, ALU.add))
                link(v.tensor_reduce(place[:, 0, :], key[:, :, :], AX.X, ALU.min))
                link(v.tensor_tensor(oh[:, k, :, :], key[:, :, :], wide(place[:, 0, :], NE), ALU.is_equal))
                if k == 0:
                    link(v.scalar_tensor_tensor(lg2[:, :, :], oh[:, 0, :, :], -1e30, g.lg[:, :, :], ALU.mult, ALU.add))
            v.tensor_tensor(ex[:, :], m[:, 1, :], m[:, 0, :], ALU.subtract).then_inc(s_d, 1)
            v.tensor_tensor(both[:, :, :], oh[:, 0, :, :], oh[:, 1, :, :], ALU.add).then_inc(s_both, 1)
            v.wait_ge(s_ex, 1)
            link(v.tensor_scalar(c[:, 1, :], ex[:, :], 1.0, None, ALU.add))
            link(v.reciprocal(c[:, 0, :], c[:, 1, :]))
            link(v.tensor_tensor(c[:, 1, :], ex[:, :], c[:, 0, :], ALU.mult))
            v.wait_ge(s_pre, 1)
            link(v.tensor_copy(cnt[:, :, :], b_cnt))
            link(v.tensor_tensor_scan(cum[:, :, :].rearrange("p e b -> p (e b)"), ones[:, :],
                                      cnt[:, :, :].rearrange("p e b -> p (e b)"), 0.0, ALU.mult, ALU.add))
            upto_, n_, tiles, ctiles, shift = (e8[:, i, :] for i in range(5))
            start = e8[:, 5, :]
            link(v.tensor_copy(upto_, cum[:, :, B - 1]))
            link(v.memset(start, 0.0))
            link(v.tensor_copy(e8[:, 5, 1:NE], e8[:, 0, 0:NE - 1]))
            link(v.tensor_tensor(n_, upto_, start, ALU.subtract))
            link(v.tensor_scalar(tiles, n_, 1.0 / 128, 127.0 / 128 - 0.5 + 1.0 / 256, ALU.mult, ALU.add))
            link(v.tensor_scalar(tiles, tiles, MAGIC, None, ALU.add))
            link(v.tensor_scalar(tiles, tiles, -MAGIC, None, ALU.add))
            link(v.tensor_tensor_scan(ctiles, ones[:, 0:NE], tiles, 0.0, ALU.mult, ALU.add))
            link(v.tensor_tensor(shift, ctiles, tiles, ALU.subtract))
            link(v.scalar_tensor_tensor(shift, shift, 128.0, start, ALU.mult, ALU.subtract))
            link(v.tensor_tensor(pos[:, :, :], cum[:, :, :], cnt[:, :, :], ALU.subtract))
            link(v.tensor_tensor(pos[:, :, :], b_intra, pos[:, :, :], ALU.add))
            link(v.tensor_tensor(pos[:, :, :], pos[:, :, :], wide(shift, B), ALU.add))
            for k in range(2):
                link(v.tensor_tensor(key[:, :, :], pos[:, :, :].rearrange("p e b -> p b e"), oh[:, k, :, :], ALU.mult))
                link(v.tensor_reduce(place[:, k, :], key[:, :, :], AX.X, ALU.add))
            link(v.tensor_scalar(tile[:, :, :], place[:, :, :], 1.0 / 128, -0.5 + 1.0 / 256, ALU.mult, ALU.add))
            link(v.tensor_scalar(tile[:, :, :], tile[:, :, :], MAGIC, None, ALU.add))
            link(v.tensor_scalar(tile[:, :, :], tile[:, :, :], -MAGIC, None, ALU.add))
            link(v.scalar_tensor_tensor(row[:, :, :], tile[:, :, :], -128.0, place[:, :, :], ALU.mult, ALU.add))
            flat = lambda x: x[:, :, :].rearrange("p k b -> p (k b)")
            v.tensor_tensor(info[:, :, 0, :], iota[0:T, 0:NTILES].unsqueeze(1).broadcast_to([T, NPAIR, NTILES]),
                            wide(flat(tile), NTILES), ALU.is_equal).then_inc(s_occ, 1)
            v.wait_ge(s_occ, 1)
            v.tensor_tensor(info[:, :, 2, :], info[:, :, 0, :], wide(flat(c), NTILES), ALU.mult).then_inc(s_info, 1)
            for q in range(4):
                cols = slice(16 * q, 16 * q + 16)
                v.tensor_tensor(ohp[:, cols, :], iota[0:T, :].unsqueeze(1).broadcast_to([T, 16, 128]),
                                wide(flat(row)[:, cols], 128), ALU.is_equal).then_inc(s_ohp, 1)
            link(v.tensor_tensor(tge[:, :, :], wide(iota[0:T, 0:NTILES], NE),
                                 ctiles.unsqueeze(1).broadcast_to([T, NTILES, NE]), ALU.is_ge))
            link(v.tensor_reduce(tef[:, :], tge[:, :, :], AX.X, ALU.add))
            link(v.tensor_scalar(g.te[0:T, :], tef[:, :], float(NE - 1), None, ALU.min))
            v.wait_ge(s_list, 1)
            link(v.tensor_copy(lst[:, 0, :], b_list[:, 0, :]))
            link(v.scalar_tensor_tensor(lst[:, 1, :], lst[:, 0, :], padrow[:, 1:2], b_list[:, 1, :], ALU.mult, ALU.add))
            link(v.tensor_scalar(g.idx[:, :], lst[:, 1, :], padrow[:, 0:1], None, ALU.add))
            link(v.tensor_copy(g.cw[:, :], b_list[:, 2, :]))

        @block.tensor
        def _(pe):
            pe.wait_ge(s_both, 1)
            flat = both[:, :, :].rearrange("p b e -> p e b")
            pe.matmul(b_intra, before[:, :], flat, start=True, stop=True)
            pe.matmul(b_cnt, ones[:, 0:T], flat, start=True, stop=True).then_inc(s_pre, 1)
            pe.wait_ge(s_info, 3)
            for j in range(NPAIR):
                if j % 16 == 0:
                    pe.wait_ge(s_ohp, j // 16 + 1)
                mm = pe.matmul(b_list, ohp[:, j, :], info[:, j, :, :], start=(j == 0), stop=(j == NPAIR - 1))
            mm.then_inc(s_list, 1)


def expert_tiles(nc, A, g):
    NCOL = NE // 4 * F
    with ExitStack() as ctx:
        def sem(name):
            return g.phase_sem("x_" + name)

        def sb(name, shape, dt=F32):
            return ctx.enter_context(nc.sbuf_tensor("x_" + name, shape, dt))

        e1_lo = sb("e1_lo", [128, 2, NE, F], F32R)
        pairs = sb("pairs", [128, 2, FC - 1, NE, D], F32R)
        e1_hi = sb("e1_hi", [HALF + 1, 2, NE, F], F32R)
        last = sb("last", [128, 2, NE, D], F32R)
        e2 = [pairs[:, :, k, :, :] for k in range(FC - 1)] + [last[:, :, :, :]]
        pieces = [(g.e2[:, k, :, :], e2[k][:, 1], e2[k][:, 0]) for k in range(FC)]
        pieces = [pieces[-1]] + [(g.e1[0:HALF + k, k, q:q + 2, :], e1_hi[0:HALF + k, k, q:q + 2, :],
                                  e1_lo[0:HALF + k, k, q:q + 2, :])
                                 for k in range(2) for q in range(0, NE, 2)] + pieces[:-1]
        xg = sb("xg", [128, NX, D])
        x_hi = sb("x_hi", [HALF + 1, 2, 128], F32R)
        x_lo = sb("x_lo", [HALF, 2, 128], F32R)
        hid = sb("hid", [128, F])
        h_hi = sb("h_hi", [128, FC, 128], F32R)
        h_lo = sb("h_lo", [128, FC, 128], F32R)
        b2 = sb("b2", [128, NE, D])
        ys = sb("ys", [128, 2, D])
        s_sum = sem("sum")
        s_b2, s_mem, s_one, s_hi, s_lo_v, s_lo_p, s_xTp, s_xh, s_xl, s_h1, s_r0, s_r1, s_hTp, s_hh, s_hl, s_y, s_ya, s_ys = (
            sem(n) for n in ("b2", "mem", "one", "hi", "lo_v", "lo_p", "xTp", "xh", "xl", "h1", "r0", "r1", "hTp", "hh",
                             "hl", "y", "ya", "ys"))
        N2 = F // 2
        s_x, s_add = g.s_x, g.s_add
        b_x = g.ps[0:HALF, 0, 0:256].rearrange("p (k t) -> p k t", k=2)
        b_h = [g.ps[:, 1 + n, 0:N2] for n in range(2)]
        b_hT = [g.ps[:, 3 + n, 0:3 * 128].rearrange("p (k t) -> p k t", k=3) for n in range(2)]
        b_y = [g.ps[:, 5 + i, 0:2 * D].rearrange("p (two d) -> p two d", two=2) for i in range(2)]
        on_pool = [n for n in range(len(pieces)) if n % 3 == 2]
        on_vector = [n for n in range(len(pieces)) if n % 3 != 2]
        block = ctx.enter_context(nc.Block())

        @block.sync
        def _(sp):
            sp.dma_start(b2[:, :, :], A["moe_b2"].unsqueeze(0).broadcast_to([128, NE, D])).then_inc(s_b2, 16)

        @block.gpsimd
        def _(pool):
            pool.memset(hid[HALF:HALF + 1, 0:128], 1.0).then_inc(s_mem, 1)
            pool.wait_ge(s_mem, 1)
            pool.tensor_copy(x_hi[HALF:HALF + 1, 1, :], hid[HALF:HALF + 1, 0:128]).then_inc(s_one, 1)
            pool.wait_ge(s_one, 1)
            for t in range(NTILES + 4):
                if t < NTILES:
                    if t >= NX:
                        pool.wait_ge(s_xTp, t - NX + 1)
                    pool.indirect_dma_start(out=xg[:, t % NX, :], out_offset=None, in_=A["xtab"][:, :],
                                            in_offset=bass.IndirectOffsetOnAxis(ap=g.idx[:, t:t + 1], axis=0)
                                            ).then_inc(s_x[t % NX], 16)
                if t == NX - 1:
                    for n in on_pool:
                        pool.wait_ge(s_hi, n + 1)
                        full, hi, lo = pieces[n]
                        pool.tensor_tensor(lo, full, hi.bitcast(F32), ALU.subtract).then_inc(s_lo_p, 1)
                i = t - 4
                if i >= 0:
                    pool.wait_ge(s_ys, i + 1)
                    if i >= 1:
                        pool.wait_ge(s_add, 16 * i)
                    pool.indirect_dma_start(out=A["out"][:, :],
                                            out_offset=bass.IndirectOffsetOnAxis(ap=g.idx[:, i:i + 1], axis=0),
                                            in_=ys[:, i % 2, :], in_offset=None, compute_op=ALU.add).then_inc(s_add, 16)
            pool.wait_ge(s_add, 16 * NTILES)

        @block.scalar
        def _(act):
            act.wait_ge(g.s_e, 16 * 9)
            for n, (full, hi, _) in enumerate(pieces):
                if n == 9:
                    act.wait_ge(s_lo_v, 1)
                act.activation(hi, full, ACT.Copy).then_inc(s_hi, 1)

            def x_copy(i, u):
                item(act, s_xTp, i)
                reused(act, s_h1, i, 1, 2)
                act.activation(x_hi[0:HALF, :, :], b_x, ACT.Copy).then_inc(s_xh, 1)

            def relu(i, u):
                reused(act, s_hTp, i, 1, 2)
                act.wait_ge(s_h1, i * 2 + 1)
                act.activation(hid[:, 0:N2], b_h[0], ACT.Relu).then_inc(s_r0, 1)

            def turn_copy(i, u):
                reused(act, s_y, i, 1)
                for n in range(2):
                    act.wait_ge(s_hTp, i * 2 + n + 1)
                    act.activation(h_hi[:, 3 * n:3 * n + 3, :], b_hT[n], ACT.Copy).then_inc(s_hh, 1)

            def weigh(i, u):
                item(act, s_ya, i)
                act.activation(ys[:, u % 2, :], ys[:, u % 2, :], ACT.Copy,
                               scale=g.cw[:, bass.ds(i, 1)]).then_inc(s_ys, 1)

            steps(act, NTILES, [(relu, 1), (x_copy, 0), (turn_copy, 1), (weigh, 2)])

        @block.vector
        def _(v):
            for n in on_vector:
                v.wait_ge(s_hi, n + 1)
                full, hi, lo = pieces[n]
                v.tensor_tensor(lo, full, hi.bitcast(F32), ALU.subtract).then_inc(s_lo_v, 1)
            v.wait_ge(s_b2, 16)
            v.wait_ge(s_one, 1)

            def x_rest(i, u):
                item(v, s_xh, i)
                v.tensor_tensor(x_lo[:, :, :], b_x, x_hi[0:HALF, :, :].bitcast(F32), ALU.subtract).then_inc(s_xl, 1)

            def relu(i, u):
                reused(v, s_hTp, i, 1, 2)
                v.wait_ge(s_h1, i * 2 + 2)
                v.tensor_scalar(hid[:, N2:F], b_h[1], 0.0, None, ALU.max).then_inc(s_r1, 1)

            def turn_rest(i, u):
                for n in range(2):
                    v.wait_ge(s_hh, i * 2 + n + 1)
                    v.tensor_tensor(h_lo[:, 3 * n:3 * n + 3, :], b_hT[n], h_hi[:, 3 * n:3 * n + 3, :].bitcast(F32),
                                    ALU.subtract).then_inc(s_hl, 1)

            def add_bias(i, u):
                e = v.value_load(g.te[0:1, bass.ds(i, 1)], min_val=0, max_val=NE - 1)
                item(v, s_y, i)
                if not isinstance(i, int) or i >= 2:
                    v.wait_ge(s_add, i * 16 - 16)
                v.tensor_tensor(ys[:, u % 2, :].unsqueeze(1), b_y[u % 2][:, 0, :].unsqueeze(1), b2[:, bass.ds(e, 1), :],
                                ALU.add).then_inc(s_sum, 1)
                item(v, s_sum, i)
                v.tensor_tensor(ys[:, u % 2, :], b_y[u % 2][:, 1, :], ys[:, u % 2, :], ALU.add).then_inc(s_ya, 1)

            steps(v, NTILES, [(relu, 1), (x_rest, 0), (turn_rest, 1), (add_bias, 2)])

        @block.tensor
        def _(pe):
            pe.wait_ge(s_one, 1)
            pe.wait_ge(s_lo_v, len(on_vector))
            pe.wait_ge(s_lo_p, len(on_pool))

            regs = [pe.alloc_register(f"tile_expert{u}") for u in range(UNROLL)]

            def pick(i, u):
                pe.reg_load(regs[u], g.te[0:1, bass.ds(i, 1)])

            def expert(u):
                return pe.snap(regs[u], min_val=0, max_val=NE - 1)

            def transpose_x(i, u):
                if isinstance(i, int):
                    pe.wait_ge(s_x[u], 16 * (i // NX + 1))
                else:
                    pe.wait_ge(s_x[u], (i - u) * (16 // NX) + 16)
                reused(pe, s_xl, i, 1)
                for k in range(2):
                    mm = pe.transpose(b_x[:, k, :], xg[:, u, k * HALF:(k + 1) * HALF], g.ident[:, :])
                mm.then_inc(s_xTp, 1)

            def first(i, u):
                e = expert(u)
                item(pe, s_xl, i)
                for n in range(2):
                    m = 0
                    for k in range(2):
                        for x, w, rows in ((x_lo, e1_hi, HALF), (x_hi, e1_lo, HALF + k), (x_hi, e1_hi, HALF + k)):
                            mm = pe.matmul(b_h[n], x[0:rows, k, :],
                                           w[0:rows, k, bass.ds(e, 1), n * N2:(n + 1) * N2].rearrange("p a f -> p (a f)"),
                                           start=(m == 0), stop=(m == 5))
                            m += 1
                    mm.then_inc(s_h1, 1)

            def turn(i, u):
                item(pe, s_r0, i)
                item(pe, s_r1, i)
                reused(pe, s_hl, i, 1, 2)
                for n in range(2):
                    for k in range(3):
                        c = 3 * n + k
                        mm = pe.transpose(b_hT[n][:, k, :], hid[:, c * 128:(c + 1) * 128], g.ident[:, :])
                    mm.then_inc(s_hTp, 1)

            def second(i, u):
                e = expert(u)
                reused(pe, s_ya, i, 2)
                for k in range(FC):
                    pe.wait_ge(s_hl, i * 2 + k // 3 + 1)
                    pe.matmul(b_y[u % 2], h_hi[:, k, :], e2[k][:, :, bass.ds(e, 1), :].rearrange("p two a d -> p two (a d)"),
                              start=(k == 0), stop=False)
                    mm = pe.matmul(b_y[u % 2][:, 1, :], h_lo[:, k, :], e2[k][:, 1, bass.ds(e, 1), :].rearrange("p a d -> p (a d)"),
                                   start=False, stop=(k == FC - 1))
                mm.then_inc(s_y, 1)

            steps(pe, NTILES, [(pick, 0), (transpose_x, 0), (second, 2), (turn, 1), (first, 0)])


def lay_out(i):
    a = {k: np.asarray(v) for k, v in i.items()}
    x = a["x"]
    xs = np.zeros_like(x)
    xs[:, :, 1:, 1:] = x[:, :, :-1, :-1]
    n = 128 // PATCH
    xs = xs.reshape(B, CIN, n, PATCH, n, PATCH).transpose(3, 5, 1, 0, 2, 4).reshape(KC, 128, B * n * n)
    w = a["L0_tok_weight"].transpose(2, 3, 1, 0).reshape(KP, D)
    kw = (np.arange(KP) // CIN) % PATCH
    q = {
        "x_patches": xs,
        "txt": a["txt"],
        "tok_w": w,
        "tok_move": np.tile(a["L0_tok_move_bias"], KP // CIN).reshape(KC, 128).T,
        "tok_keep": (kw != 0).astype(np.float32).reshape(KC, 128).T,
        "ident": np.eye(128, dtype=np.float32),
        "head_mask": np.kron(np.eye(HH), np.ones((DH, 1))).astype(np.float32),
        "a0_wqk": np.concatenate([np.concatenate([a["L0_attn_Wq"], a["L0_attn_Wk"]], 1),
                                  np.concatenate([a["L0_attn_bq"], a["L0_attn_bk"]])[None]], 0),
        "a0_wv": np.concatenate([a["L0_attn_Wv"], a["L0_attn_bv"][None]], 0),
        "a0_bo": a["L0_attn_bo"],
    }
    q.update({"norm_w": a["L0_ffn_norm_weight"], "slots": a["L0_ffn_slots"], "slot_scale": a["L0_ffn_scale"],
              "fc1_w": a["L0_ffn_fc1_weight"], "fc1_b": a["L0_ffn_fc1_bias"],
              "fc2_w": a["L0_ffn_fc2_weight"], "fc2_b": a["L0_ffn_fc2_bias"]})
    theta = np.float32(10000.0) ** (-2.0 * np.arange(D // 2, dtype=np.float32) / np.float32(D))
    angle = np.arange(T, dtype=np.float32)[:, None] * theta[None, :].astype(np.float32)
    cos, sin = np.cos(angle).astype(np.float32), np.sin(angle).astype(np.float32)
    q["rope_cos"] = np.tile(np.repeat(cos, 2, axis=1), (1, 2))
    q["rope_sin"] = np.tile(sin, (1, 2))
    q["rope_nsin"] = -q["rope_sin"]
    q["causal"] = np.where(np.tril(np.ones((T, T), bool)), 0.0, -1e30).astype(np.float32)
    q["a1_wqkv"] = np.concatenate([a["L1_attn_Wq"], a["L1_attn_Wk"], a["L1_attn_Wv"]], 1)
    q.update({"moe_wr": a["L1_ffn_Wr"], "moe_w1": a["L1_ffn_W1"], "moe_b1": a["L1_ffn_b1"],
              "moe_w2": a["L1_ffn_W2"], "moe_b2": a["L1_ffn_b2"]})
    q["iota"] = np.tile(np.arange(128, dtype=np.float32), (128, 1))
    pad = NTOK + np.arange(128, dtype=np.float32)
    q["padrow"] = np.stack([pad, -pad], 1)
    q["before"] = np.triu(np.ones((T, T), np.float32), 1)
    q["tokid"] = (np.arange(T)[:, None] + T * np.arange(B)[None, :]).astype(np.float32)
    wo = np.zeros((NH, HPAD, D), np.float32)
    wo[:, :DH] = a["L0_attn_Wo"].reshape(NH, DH, D)
    q["a0_wo"] = wo.reshape(NH * HPAD, D)
    return {k: np.ascontiguousarray(v) for k, v in q.items()}


def declare(nc, arrays):
    A = {k: nc.dram_tensor(f"in_{k}", v.shape, mybir.dt.from_np(v.dtype), kind="ExternalInput").ap()
         for k, v in arrays.items()}
    A["out"] = nc.dram_tensor("out_h", (NTOK + 128, D), F32, kind="ExternalOutput").ap()
    A["xtab"] = nc.dram_tensor("xtab", (NTOK + 128, D), F32, kind="Internal").ap()
    return A


def kernel(**inputs):
    import concourse.bacc as bacc
    from concourse.bass_utils import run_bass_kernel_spmd as run
    arrays = lay_out(inputs)
    nc = bacc.Bacc("TRN2", target_bir_lowering=False, num_devices=1)
    build(nc, declare(nc, arrays))
    r = run(nc, [{f"in_{k}": v for k, v in arrays.items()}], core_ids=[0])
    return r.results[0]["out_h"][:NTOK].reshape(B, T, D)
```

```python
from contextlib import ExitStack

import numpy as np

import concourse.bass as bass
from concourse import mybir

F32 = mybir.dt.float32
BF16 = mybir.dt.bfloat16
F32R = mybir.dt.float32r
ALU = mybir.AluOpType
ACT = mybir.ActivationFunctionType
AX = mybir.AxisListType

B = 32
T_IMG, T_TXT = 64, 32
T = T_IMG + T_TXT
D = 192
HALF = D // 2
PATCH, CIN = 16, 3
KP = CIN * PATCH * PATCH
KC = KP // 128
NH, DH = 12, 16
HH = NH // 2
HPAD = 32
HG = 128 // HPAD
NG = NH // HG
NS = 64
F = 768
FC = F // 128
GS = 4
NGR = NS // GS
W1_DMAS = 3
NE = 8
NTILES = 55
NTOK = B * T
NX = 4
NPAIR = 2 * B
assert NTILES >= (2 * NTOK + NE * 127) // 128 and 2 * GS == NE
EPS = 1e-5
UNROLL = 4


def item(eng, sem, b, per=1):
    eng.wait_ge(sem, b * per + per)


def reused(eng, sem, b, depth, per=1):
    if not isinstance(b, int) or b >= depth:
        eng.wait_ge(sem, b * per - (depth - 1) * per)


def steps(eng, n, stages, unroll=UNROLL, depth=UNROLL):
    last = max(lag for _, lag in stages)
    first = -(-(last + depth) // unroll) * unroll
    for t in range(first):
        for stage, lag in stages:
            if t >= lag:
                stage(t - lag, (t - lag) % unroll)
    end = n // unroll
    with eng.Fori(first // unroll, end) as j:
        for u in range(unroll):
            for stage, lag in stages:
                stage(j * unroll + (u - lag), (u - lag) % unroll)
    for t in range(end * unroll, n + last):
        for stage, lag in stages:
            if t - lag < n:
                stage(t - lag, (t - lag) % unroll)


def few_steps(n, stages):
    for t in range(n + max(lag for _, lag in stages)):
        for stage, lag in stages:
            if 0 <= t - lag < n:
                stage(t - lag, (t - lag) % 2)


class Prog:

    def __init__(self, nc):
        self.nc = nc
        self.live = []

    def phase_sem(self, name):
        s = self.nc.alloc_semaphore(name)
        self.live.append(s)
        return s

    def clear_sems(self):
        self.nc.clear_and_free_semaphores(self.live)
        self.nc.all_engine_barrier()
        self.live = []


def build(nc, A):
    with ExitStack() as ctx:
        g = Prog(nc)

        def sem(name):
            return ctx.enter_context(nc.semaphore(name))

        def sb(name, shape, dt=F32):
            return ctx.enter_context(nc.sbuf_tensor(name, shape, dt))

        g.ident = sb("ident", [128, 128])
        g.idx = sb("idx", [128, NTILES], mybir.dt.uint32)
        g.cw = sb("cw", [128, NTILES])
        g.te = sb("te", [128, NTILES], mybir.dt.int32)
        g.s_const = sem("s_const")
        n1, n2, nh = 4 * GS * F, 2 * GS * FC * D, B * D
        held = ExitStack()
        g.flat = held.enter_context(nc.sbuf_tensor("flat", [128, n1 + n2 + nh], F32))
        w1_flat, w2_flat = g.flat[0:HALF + 1, 0:n1], g.flat[:, n1:n1 + n2]
        g.h = g.flat[0:T, n1 + n2:].rearrange("p (b d) -> p b d", d=D)
        g.w1 = w1_flat.rearrange("p (i k s f) -> p i k s f", i=2, k=2, f=F)
        g.w2 = w2_flat.rearrange("p (i s n) -> p i s n", i=2, n=FC * D)
        g.e1 = w1_flat.rearrange("p (k e f) -> p k e f", k=2, f=F)
        g.e2 = w2_flat.rearrange("p (k e d) -> p k e d", k=FC, d=D)
        g.s_e = sem("s_e")
        g.s_x = [sem(f"s_x{i}") for i in range(NX)]
        g.s_add = sem("s_add")
        g.s_w1 = [sem(f"s_w1_{i}") for i in range(2)]
        g.s_w2 = [sem(f"s_w2_{i}") for i in range(2)]
        psum = ctx.enter_context(nc.psum_tensor("psum", [128, 8, 512], F32))
        g.ps = psum
        with ExitStack() as norms:
            def small(name, shape):
                return norms.enter_context(nc.sbuf_tensor(name, shape, F32))

            g.stats = small("stats", [T, B, 6])
            g.rstd = small("rstd", [T, B])
            g.nmr = small("nmr", [T, B])
            g.lnt = small("lnt", [T, 4, B])
            with ExitStack() as layer0:
                def small0(name, shape):
                    return layer0.enter_context(nc.sbuf_tensor(name, shape, F32))

                g.nw = small0("nw", [T, D])
                g.slT = small0("slT", [HALF, 2, NS])
                with ExitStack() as weights:
                    def weight(name, shape):
                        return weights.enter_context(nc.sbuf_tensor("a_" + name, shape, F32))

                    g.a0 = dict(wqk=weight("wqk", [HALF + 1, 2, 2 * D]), wv=weight("wv", [HALF + 1, 2, D]),
                                wo=weight("wo", [128, NG, D]), bo=weight("bo", [T, D]), hmask=weight("hmask", [HALF, HH]),
                                sl=weight("sl", [NS, D]), sl_scale=weight("sl_scale", [NS, 1]))
                    g.s_w0, g.s_slw = g.phase_sem("a_w"), g.phase_sem("a_slw")
                    embed(nc, A, g)
                    attention0(nc, A, g)
                soft_moe(nc, A, g)
            g.clear_sems()
            g.lg = small("t_lg", [T, B, NE])
            g.colsum = small("t_colsum", [T, NE])
            g.iota, g.padrow = small("iota", [128, 128]), small("padrow", [128, 2])
            g.before, g.tokid = small("before", [T, T]), small("tokid", [T, B])
            g.s_rw = g.phase_sem("s_rw")
            attention1(nc, A, g)
            route(nc, A, g)
        held.close()
        expert_tiles(nc, A, g)


def layernorm_scale(eng_v, eng_s, g, s):
    st = g.stats
    mean, half_diff, var, sq = (g.lnt[:, i, :] for i in range(4))
    if eng_v is not None:
        v = eng_v
        v.tensor_tensor(mean, st[:, :, 1], st[:, :, 4], ALU.add).then_inc(s, 1)
        v.tensor_tensor(half_diff, st[:, :, 1], st[:, :, 4], ALU.subtract).then_inc(s, 1)
        v.tensor_tensor(var, st[:, :, 2], st[:, :, 5], ALU.add).then_inc(s, 1)
        v.wait_ge(s, 3)
        v.tensor_tensor(half_diff, half_diff, half_diff, ALU.mult).then_inc(s, 1)
        v.tensor_scalar(var, var, 1.0 / D, EPS, ALU.mult, ALU.add).then_inc(s, 1)
        v.wait_ge(s, 5)
        v.scalar_tensor_tensor(var, half_diff, 0.25, var, ALU.mult, ALU.add).then_inc(s, 1)
        v.wait_ge(s, 7)
        v.reciprocal(g.rstd[:, :], sq).then_inc(s, 1)
        v.wait_ge(s, 8)
        v.scalar_tensor_tensor(g.nmr[:, :], mean, -0.5, g.rstd[:, :], ALU.mult, ALU.mult).then_inc(s, 1)
        v.wait_ge(s, 9)
    if eng_s is not None:
        eng_s.wait_ge(s, 6)
        eng_s.activation(sq, var, ACT.Sqrt).then_inc(s, 1)


def load_slots(sp, A, g, gr, i, w1_free=lambda: None, w2_free=lambda: None):
    src = A["fc1_w"][bass.ds(gr * GS, GS), :, :].rearrange("s (k p) n -> k p s n", k=2)
    w1_free()
    for k in range(2):
        sp.dma_start(g.w1[0:HALF, i, k, :, :], src[k]).then_inc(g.s_w1[i], 16)
    sp.dma_start(g.w1[HALF:HALF + 1, i, 1, :, :], A["fc1_b"][bass.ds(gr * GS, GS), :].unsqueeze(0)).then_inc(g.s_w1[i], 16)
    w2_free()
    sp.dma_start(g.w2[:, i, :, :], A["fc2_w"][bass.ds(gr * GS, GS), :, :].rearrange(
        "s (p k) n -> p s (k n)", k=FC)).then_inc(g.s_w2[i], 16)


def load_attention0(sp, A, g):
    w = g.a0
    sp.dma_start(w["sl"][:, :], A["slots"]).then_inc(g.s_slw, 16)
    sp.dma_start(w["sl_scale"][:, :], A["slot_scale"].unsqueeze(1)).then_inc(g.s_slw, 16)
    sp.dma_start(g.nw[:, :], A["norm_w"].unsqueeze(0).broadcast_to([T, D])).then_inc(g.s_slw, 16)
    sp.dma_start(w["wqk"][0:HALF, :, :], A["a0_wqk"][0:D, :].rearrange("(k p) n -> p k n", k=2)).then_inc(g.s_w0, 16)
    sp.dma_start(w["wqk"][HALF:HALF + 1, 1, :], A["a0_wqk"][D:D + 1, :]).then_inc(g.s_w0, 16)
    sp.dma_start(w["wv"][0:HALF, :, :], A["a0_wv"][0:D, :].rearrange("(k p) n -> p k n", k=2)).then_inc(g.s_w0, 16)
    sp.dma_start(w["wv"][HALF:HALF + 1, 1, :], A["a0_wv"][D:D + 1, :]).then_inc(g.s_w0, 16)
    sp.dma_start(w["wo"][:, :, :], A["a0_wo"].rearrange("(r p) n -> p r n", r=NG)).then_inc(g.s_w0, 16)
    sp.dma_start(w["bo"][:, :], A["a0_bo"].unsqueeze(0).broadcast_to([T, D])).then_inc(g.s_w0, 16)
    sp.dma_start(w["hmask"][:, :], A["head_mask"]).then_inc(g.s_w0, 16)


def embed(nc, A, g):
    NT = B * T_IMG
    CH = 512
    NCH = NT // CH
    TPC = CH // 128
    SPC = CH // T_IMG
    NRAW = 3
    with ExitStack() as ctx:
        def sem(name):
            return g.phase_sem(name)

        def sb(name, shape, dt=F32):
            return ctx.enter_context(nc.sbuf_tensor(name, shape, dt))

        x_raw = sb("x_raw", [128, NRAW, KC, CH])
        x_sign = sb("x_sign", [128, KC, NT], BF16)
        w_raw = sb("w_raw", [128, KC, D])
        w_sign = sb("w_sign", [128, KC, D], BF16)
        move = sb("move", [128, KC])
        keep = sb("keep", [128, KC])
        ones = sb("ones_e", [128, 128])
        sf = sb("sf", [128, D])
        s_w, s_txt = sem("e_w"), sem("e_txt")
        s_x = [sem(f"e_x{c}") for c in range(NCH)]
        s_ones, s_wsign, s_wabs, s_sfps, s_sf = (sem(n) for n in ("e_ones", "e_wsign", "e_wabs", "e_sfps", "e_sf"))
        s_sign, s_row, s_edge, s_tile, s_out, s_stats, s_ln = (
            sem(n) for n in ("e_sign", "e_row", "e_edge", "e_tile", "e_out", "e_stats", "e_ln"))
        block = ctx.enter_context(nc.Block())

        @block.sync
        def _(sp):
            sp.dma_start(w_raw[:, :, :], A["tok_w"].rearrange("(k p) e -> p k e", p=128)).then_inc(s_w, 16)
            sp.dma_start(move[:, :], A["tok_move"]).then_inc(s_w, 16)
            sp.dma_start(keep[:, :], A["tok_keep"]).then_inc(s_w, 16)
            for c in range(NCH):
                if c >= NRAW:
                    sp.wait_ge(s_sign, KC * (c - NRAW + 1))
                sp.dma_start(x_raw[:, c % NRAW, :, :],
                             A["x_patches"][:, :, c * CH:(c + 1) * CH].rearrange("k p n -> p k n")).then_inc(s_x[c], 16)
                if c == 0:
                    sp.dma_start(g.h[T_IMG:T, :, :], A["txt"].rearrange("b t d -> t b d")).then_inc(s_txt, 16)
            sp.dma_start(g.ident[:, :], A["ident"]).then_inc(g.s_const, 16)
            load_attention0(sp, A, g)

        @block.gpsimd
        def _(pool):
            pool.memset(ones[:, :], 1.0 / KP).then_inc(s_ones, 1)
            pool.wait_ge(s_w, 48)
            for c in range(NCH):
                item(pool, s_sign, c, KC)
                tok = x_sign[:, :, c * CH:(c + 1) * CH].rearrange("p k (q j) -> p k q j", j=8)[:, :, :, 0]
                row = x_sign[0:CIN * PATCH, 0, c * CH:(c + 1) * CH].rearrange("p (b i j) -> p b i j", i=8, j=8)
                pool.tensor_scalar(row[:, :, 0, :], row[:, :, 0, :], 0.0, None, ALU.mult).then_inc(s_row, 1)
                item(pool, s_row, c)
                pool.tensor_tensor(tok, tok, keep[:, :].unsqueeze(2).broadcast_to([128, KC, CH // 8]),
                                   ALU.mult).then_inc(s_edge, 1)

        @block.scalar
        def _(act):
            act.wait_ge(s_w, 48)
            act.activation(w_sign[:, :, :], w_raw[:, :, :], ACT.Sign).then_inc(s_wsign, 1)
            act.wait_ge(s_wsign, 1)
            act.activation(w_raw[:, :, :], w_raw[:, :, :], ACT.Abs).then_inc(s_wabs, 1)
            for c in range(NCH):
                act.wait_ge(s_x[c], 16)
                for k in range(KC):
                    act.activation(x_sign[:, k, c * CH:(c + 1) * CH], x_raw[:, c % NRAW, k, :],
                                   ACT.Sign, bias=move[:, k:k + 1]).then_inc(s_sign, 1)
            layernorm_scale(None, act, g, s_ln)

        @block.tensor
        def _(pe):
            pe.wait_ge(s_ones, 1)
            pe.wait_ge(s_wabs, 1)
            for k in range(KC):
                mm = pe.matmul(g.ps[:, 7, 0:D], ones[:, :], w_raw[:, k, :], start=(k == 0), stop=(k == KC - 1))
            mm.then_inc(s_sfps, 1)
            pe.wait_ge(s_wsign, 1)
            with pe.Fori(0, NCH) as c:
                item(pe, s_edge, c)
                for u in range(TPC):
                    pe.wait_ge(s_out, c * (2 * TPC) + 2 * (u + 1))
                    for k in range(KC):
                        mm = pe.matmul(g.ps[:, u, 0:D], x_sign[:, k, bass.ds(c * CH + u * 128, 128)],
                                       w_sign[:, k, :], start=(k == 0), stop=(k == KC - 1))
                    mm.then_inc(s_tile, 1)

        @block.vector
        def _(v):
            v.sem_inc(s_out, 2 * TPC)
            v.wait_ge(s_sfps, 1)
            v.tensor_copy(sf[:, :], g.ps[:, 7, 0:D]).then_inc(s_sf, 1)
            v.wait_ge(s_sf, 1)

            def scale_tiles(c):
                for u in range(TPC):
                    v.wait_ge(s_tile, c * TPC + u + 1)
                    for i in range(2):
                        b = c * (2 * TPC) + 2 * u + i
                        v.tensor_tensor(g.h[0:T_IMG, bass.ds(b, 1), :],
                                        g.ps[64 * i:64 * i + 64, u, 0:D].unsqueeze(1),
                                        sf[64 * i:64 * i + 64, :].unsqueeze(1), ALU.mult).then_inc(s_out, 1)

            v.wait_ge(s_txt, 16)
            with v.Fori(0, NCH) as c:
                scale_tiles(c)
                v.wait_ge(s_out, c * SPC + (SPC + 2 * TPC))
                for i in range(SPC):
                    v.bn_stats(g.stats[:, bass.ds(c * SPC + i, 1), :].rearrange("p a s -> p (a s)"),
                               g.h[:, bass.ds(c * SPC + i, 1), :].rearrange("p a d -> p (a d)")).then_inc(s_stats, 1)
            v.wait_ge(s_stats, B)
            layernorm_scale(v, None, g, s_ln)


def attention0(nc, A, g):
    with ExitStack() as ctx:
        def sem(name):
            return g.phase_sem("a_" + name)

        def sb(name, shape, dt=F32):
            return ctx.enter_context(nc.sbuf_tensor("a_" + name, shape, dt))

        wqk, wv, wo, bo, hmask, sl, sl_scale = (
            g.a0[n] for n in ("wqk", "wv", "wo", "bo", "hmask", "sl", "sl_scale"))
        xn = sb("xn", [T, 2, D])
        xT = sb("xT", [HALF + 1, 2, 2, T])
        qk = sb("qk", [HALF, 2, 4, T])
        kb = sb("kb", [HALF, 2, 2, HH, T])
        vv = sb("vv", [T, 4, NH, HPAD])
        p = sb("p", [T, 2, NH, T])
        pT = sb("pT", [T, NG, HG, T])
        oT = sb("oT", [128, NG, T])
        rw = sb("rw", [T, 2, NH, HPAD])
        rT = sb("rT", [128, NG, T])
        ones = sb("ones", [T, NH])
        sl_junk = sb("sl_junk", [NS, D])
        sl_n = sb("sl_n", [NS, 4])
        mx = sb("mx", [T, 2, NH])
        sm = sb("sm", [T, 2, NH])
        rs = sb("rs", [T, 2, NH])

        s_w, s_slw = g.s_w0, g.s_slw
        s_set, s_vset, s_ones = sem("set"), sem("vset"), sem("ones")
        s_xn, s_bo, s_xTp, s_xTs, s_qkp, s_vp, s_qks, s_vs, s_kb = (
            sem(n) for n in ("xn", "bo", "xTp", "xTs", "qkp", "vp", "qks", "vs", "kb"))
        s_sc, s_mx, s_sub, s_exp, s_sum, s_rs, s_rw = (sem(n) for n in ("sc", "mx", "sub", "exp", "sum", "rs", "rw"))
        s_pTp, s_pTs, s_rTp, s_rTs, s_oTp, s_oTs, s_op, s_res, s_st, s_ln = (
            sem(n) for n in ("pTp", "pTs", "rTp", "rTs", "oTp", "oTs", "op", "res", "st", "ln"))

        s_sl, s_slroot, s_slT = (sem(n) for n in ("sl", "slroot", "slT"))
        slT_ps = g.ps[0:HALF, 7, 0:2 * NS].rearrange("p (k s) -> p k s", k=2)
        bank_x = g.ps[:, 0, :]
        bank_qk = g.ps[0:HALF, 1, 0:4 * T].rearrange("p (m t) -> p m t", t=T)
        bank_oT = g.ps[:, 2, 0:NG * T].rearrange("p (r t) -> p r t", t=T)
        bank_out = g.ps[0:T, 2, NG * T:NG * T + D]
        scores = g.ps[0:T, 3:6, 0:HG * T].rearrange("p r (h t) -> p r h t", t=T)
        bank_pT = [g.ps[0:T, 6 + r % 2, 0:HG * T] for r in range(NG)]
        bank_rT = g.ps[:, 7, 0:NG * T].rearrange("p (r t) -> p r t", t=T)
        block = ctx.enter_context(nc.Block())

        @block.sync
        def _(sp):
            for gr in range(2):
                load_slots(sp, A, g, gr, gr)

        @block.gpsimd
        def _(pool):
            pool.memset(ones[:, :], 1.0).then_inc(s_ones, 1)
            pool.memset(vv[:, :, :, :], 0.0).then_inc(s_vset, 1)
            pool.wait_ge(s_ones, 1)
            pool.memset(xT[HALF:HALF + 1, :, 1, :], 1.0).then_inc(s_set, 1)
            pool.wait_ge(s_w, 7 * 16)

            def add_bias(b, i):
                item(pool, s_xn, b)
                hb = g.h[:, bass.ds(b, 1), :]
                pool.tensor_tensor(hb, hb, bo[:, :].unsqueeze(1), ALU.add).then_inc(s_bo, 1)

            def block_diagonal(b, i):
                item(pool, s_qks, b)
                reused(pool, s_sc, b, 2)
                k = i % 2
                for hf in range(2):
                    ins = pool.tensor_tensor(
                        kb[:, k, hf, :, :], qk[:, k, 2 + hf, :].unsqueeze(1).broadcast_to([HALF, HH, T]),
                        hmask[:, :].unsqueeze(2).broadcast_to([HALF, HH, T]), ALU.mult)
                ins.then_inc(s_kb, 1)

            def widen(b, i):
                item(pool, s_rs, b)
                reused(pool, s_rTp, b, 2)
                k = i % 2
                pool.tensor_tensor(rw[:, k, :, :], rs[:, k, :].unsqueeze(2).broadcast_to([T, NH, HPAD]),
                                   ones[:, :].unsqueeze(2).broadcast_to([T, NH, HPAD]), ALU.mult).then_inc(s_rw, 1)

            steps(pool, B, [(add_bias, 0), (widen, 3), (block_diagonal, 1)])

        @block.scalar
        def _(act):
            act.wait_ge(s_slw, 48)
            act.activation(sl_junk[:, :], sl[:, :], ACT.Square, accum_out=sl_n[:, 0:1]).then_inc(s_sl, 1)
            act.wait_ge(s_sl, 1)
            act.activation(sl_n[:, 1:2], sl_n[:, 0:1], ACT.Sqrt).then_inc(s_slroot, 1)
            act.wait_ge(s_vset, 1)

            def x_copy(b, i):
                item(act, s_xTp, b)
                reused(act, s_vp, b, 2)
                act.activation(xT[0:HALF, i % 2, :, :],
                               bank_x[0:HALF, 0:2 * T].rearrange("p (k t) -> p k t", k=2), ACT.Copy).then_inc(s_xTs, 1)

            def qk_copy(b, i):
                item(act, s_qkp, b)
                reused(act, s_sc, b, 2)
                reused(act, s_kb, b, 2)
                act.activation(qk[:, i % 2, :, :], bank_qk, ACT.Copy).then_inc(s_qks, 1)

            def v_copy(b, i):
                item(act, s_vp, b)
                reused(act, s_oTp, b, 4)
                act.activation(vv[:, i, :, 0:DH],
                               bank_x[0:T, 2 * T:2 * T + D].rearrange("p (h d) -> p h d", d=DH), ACT.Copy).then_inc(s_vs, 1)

            def exponent(b, i):
                item(act, s_sub, b)
                act.activation(p[:, i % 2, :, :], p[:, i % 2, :, :], ACT.Exp, scale=DH ** -0.5).then_inc(s_exp, 1)

            def p_copy(b, rounds):
                for r in rounds:
                    act.wait_ge(s_pTp, b * NG + r + 1)
                    reused(act, s_oTp, b, 1)
                    act.activation(pT[:, r, :, :], bank_pT[r].rearrange("p (h t) -> p h t", t=T),
                                   ACT.Copy).then_inc(s_pTs, 1)

            def p_copy_first(b, i):
                p_copy(b, (0, 1))

            def p_copy_last(b, i):
                p_copy(b, (2,))

            def r_copy(b, i):
                item(act, s_rTp, b)
                reused(act, s_oTs, b, 1)
                act.activation(rT[:, :, :], bank_rT, ACT.Copy).then_inc(s_rTs, 1)

            steps(act, B, [(exponent, 3), (qk_copy, 1), (v_copy, 1), (p_copy_first, 3), (x_copy, 0), (p_copy_last, 3),
                           (r_copy, 3)])
            layernorm_scale(None, act, g, s_ln)

        @block.vector
        def _(v):

            def norm_input(b, i):
                reused(v, s_xTp, b, 2)
                v.tensor_scalar(xn[:, i % 2, :].unsqueeze(1), g.h[:, bass.ds(b, 1), :], g.rstd[:, bass.ds(b, 1)],
                                g.nmr[:, bass.ds(b, 1)], ALU.mult, ALU.add).then_inc(s_xn, 1)

            def residual(b, i):
                item(v, s_op, b)
                item(v, s_bo, b)
                hb = g.h[:, bass.ds(b, 1), :]
                v.tensor_tensor(hb, bank_out.unsqueeze(1), hb, ALU.add).then_inc(s_res, 1)
                v.wait_ge(s_res, b + 1)
                v.bn_stats(g.stats[:, bass.ds(b, 1), :].rearrange("p a s -> p (a s)"),
                           hb.rearrange("p a d -> p (a d)")).then_inc(s_st, 1)

            def maximum(b, i):
                item(v, s_sc, b)
                v.tensor_reduce(mx[:, i % 2, :].rearrange("p (r h) -> p r h", r=NG), scores, AX.X, ALU.max).then_inc(s_mx, 1)

            def subtract(b, i):
                item(v, s_mx, b)
                reused(v, s_pTp, b, 2, NG)
                v.tensor_tensor(p[:, i % 2, :, :].rearrange("p (r h) t -> p r h t", r=NG), scores,
                                mx[:, i % 2, :].rearrange("p (r h) -> p r h", r=NG).unsqueeze(3).broadcast_to([T, NG, HG, T]),
                                ALU.subtract).then_inc(s_sub, 1)

            def row_sum(b, i):
                item(v, s_exp, b)
                v.tensor_reduce(sm[:, i % 2, :], p[:, i % 2, :, :], AX.X, ALU.add).then_inc(s_sum, 1)
                item(v, s_sum, b)
                v.reciprocal(rs[:, i % 2, :], sm[:, i % 2, :]).then_inc(s_rs, 1)

            def divide(b, i):
                item(v, s_oTp, b)
                item(v, s_rTs, b)
                reused(v, s_op, b, 1)
                v.tensor_tensor(oT[:, :, :], bank_oT, rT[:, :, :], ALU.mult).then_inc(s_oTs, 1)

            v.wait_ge(s_slroot, 1)
            v.tensor_scalar(sl_n[:, 2:3], sl_n[:, 1:2], EPS, None, ALU.max).then_inc(s_sl, 1)
            v.wait_ge(s_sl, 2)
            v.reciprocal(sl_n[:, 3:4], sl_n[:, 2:3]).then_inc(s_sl, 1)
            v.wait_ge(s_sl, 3)
            v.tensor_scalar(sl[:, :], sl[:, :], sl_n[:, 3:4], sl_scale[:, 0:1], ALU.mult, ALU.mult).then_inc(s_sl, 1)
            v.wait_ge(s_slT, 1)
            v.tensor_copy(g.slT[:, :, :], slT_ps).then_inc(s_sl, 1)
            steps(v, B, [(divide, 4), (row_sum, 3), (residual, 5), (norm_input, 0), (maximum, 2), (subtract, 2)])
            v.wait_ge(s_st, B)
            layernorm_scale(v, None, g, s_ln)

        @block.tensor
        def _(pe):
            pe.wait_ge(g.s_const, 16)
            pe.wait_ge(s_sl, 4)
            for k in range(2):
                mm = pe.transpose(slT_ps[:, k, :], sl[:, k * HALF:(k + 1) * HALF], g.ident[0:NS, 0:NS])
            mm.then_inc(s_slT, 1)
            pe.wait_ge(s_w, 7 * 16)
            pe.wait_ge(s_set, 1)
            pe.wait_ge(s_sl, 5)

            def transpose_x(b, i):
                item(pe, s_xn, b)
                reused(pe, s_vs, b, 1)
                for hf in range(2):
                    mm = pe.transpose(bank_x[0:HALF, hf * T:(hf + 1) * T], xn[:, i % 2, hf * HALF:(hf + 1) * HALF],
                                      g.ident[0:T, 0:T])
                mm.then_inc(s_xTp, 1)

            def project(b, i):
                item(pe, s_xTs, b)
                reused(pe, s_qks, b, 1)
                k = i % 2
                for m in range(4):
                    pe.matmul(bank_qk[:, m, :], wqk[0:HALF, 0, m * HALF:(m + 1) * HALF], xT[0:HALF, k, 0, :],
                              start=True, stop=False)
                    mm = pe.matmul(bank_qk[:, m, :], wqk[:, 1, m * HALF:(m + 1) * HALF], xT[:, k, 1, :],
                                   start=False, stop=True)
                mm.then_inc(s_qkp, 1)
                pe.matmul(bank_x[0:T, 2 * T:2 * T + D], xT[0:HALF, k, 0, :], wv[0:HALF, 0, :], start=True, stop=False)
                pe.matmul(bank_x[0:T, 2 * T:2 * T + D], xT[:, k, 1, :], wv[:, 1, :], start=False, stop=True).then_inc(s_vp, 1)

            def score(b, i):
                item(pe, s_kb, b)
                reused(pe, s_sub, b, 1)
                k = i % 2
                q = [qk[:, k, hf, :] for hf in range(2)]
                for hf, h0, n, r, c in ((0, 0, 4, 0, 0), (0, 4, 2, 1, 0), (1, 0, 2, 1, 2), (1, 2, 4, 2, 0)):
                    mm = pe.matmul(g.ps[0:T, 3 + r, c * T:(c + n) * T], q[hf],
                                   kb[:, k, hf, h0:h0 + n, :].rearrange("p h t -> p (h t)"), start=True, stop=True)
                mm.then_inc(s_sc, 1)

            def turn(b, i, r):
                for j in range(HG):
                    mm = pe.transpose(bank_pT[r][:, j * T:(j + 1) * T], p[:, i % 2, r * HG + j, :], g.ident[0:T, 0:T])
                mm.then_inc(s_pTp, 1)

            def values(b, i, r):
                pe.wait_ge(s_pTs, b * NG + r + 1)
                for j in range(HG):
                    mm = pe.matmul(bank_oT[HPAD * j:HPAD * (j + 1), r, :], vv[:, i, r * HG + j, :], pT[:, r, j, :],
                                   start=True, stop=True, tile_position=(0, HPAD * j))
                return mm

            def turn_first(b, i):
                item(pe, s_exp, b)
                reused(pe, s_pTs, b, 1, NG)
                turn(b, i, 0)
                reused(pe, s_rTs, b, 1)
                turn(b, i, 1)

            def attend(b, i):
                item(pe, s_vs, b)
                reused(pe, s_res, b, 2)
                reused(pe, s_oTs, b, 1)
                values(b, i, 0)
                turn(b, i, 2)
                values(b, i, 1)
                pe.wait_ge(s_rw, b + 1)
                for r in range(NG):
                    mm = pe.transpose(bank_rT[:, r, :], rw[:, i % 2, r * HG:(r + 1) * HG, :].rearrange("p h w -> p (h w)"),
                                      g.ident[0:T, 0:T])
                mm.then_inc(s_rTp, 1)
                values(b, i, 2).then_inc(s_oTp, 1)

            def output(b, i):
                item(pe, s_oTs, b)
                reused(pe, s_res, b, 1)
                for r in range(NG):
                    mm = pe.matmul(bank_out, oT[:, r, :], wo[:, r, :], start=(r == 0), stop=(r == NG - 1))
                mm.then_inc(s_op, 1)

            steps(pe, B, [(project, 1), (turn_first, 3), (score, 2), (transpose_x, 0), (attend, 3), (output, 4)])


def soft_moe(nc, A, g):
    with ExitStack() as ctx:
        def sb(name, shape, dt=F32):
            return ctx.enter_context(nc.sbuf_tensor("m_" + name, shape, dt))

        g.yT = sb("yT", [HALF, 2, NS, B])
        g.combT = sb("combT", [NS, B, T])
        dispatch(nc, A, g)
        g.y2 = sb("y2", [NS, B, D])
        slot_ffn(nc, A, g)
        combine(nc, A, g)


def dispatch(nc, A, g):
    NP = B // 2
    CH = 4
    NQ = B // CH
    with ExitStack() as ctx:
        def sem(name):
            return g.phase_sem("d_" + name)

        def sb(name, shape, dt=F32):
            return ctx.enter_context(nc.sbuf_tensor("d_" + name, shape, dt))

        u = sb("u", [T, B, D])
        junk = sb("junk", [T, D])
        xT = sb("xT", [HALF, 2, 2, 2, T])
        lg = sb("lg", [T, B, NS])
        dm = sb("dm", [NS, 2, CH, T])
        dT = sb("dT", [T, 2, CH, NS])
        cs = sb("cs", [T, 2, 3, CH])
        dsm = sb("dsm", [NS, 2, 3, CH])
        neg_mean = sb("neg_mean", [T, B])
        in_scale = sb("in_scale", [T, B])
        lg_scale = sb("lg_scale", [T, B])
        ss = sb("ss", [T, B])
        root = sb("root", [T, 2, B])
        t_ms = sb("t_ms", [T, B])
        (s_neg, s_u, s_sq, s_xTp, s_xTs, s_raw, s_ms, s_root, s_chain, s_scales, s_lg, s_lgT, s_cmx, s_csub, s_cexp,
         s_csum, s_crs, s_c, s_dmx, s_dsub, s_dexp, s_dsum, s_drs, s_d, s_dTp, s_cTp, s_dTs, s_cTs, s_yp, s_ys) = (
             sem(n) for n in ("neg", "u", "sq", "xTp", "xTs", "raw", "ms", "root", "chain", "scales", "lg", "lgT",
                              "cmx", "csub", "cexp", "csum", "crs", "c", "dmx", "dsub", "dexp", "dsum", "drs", "d",
                              "dTp", "cTp", "dTs", "cTs", "yp", "ys"))
        b_x = [g.ps[0:HALF, i, 0:4 * T].rearrange("p (b k t) -> p b k t", b=2, k=2) for i in range(2)]
        raw = g.ps[0:T, 4:8, :].rearrange("p n (b s) -> p (n b) s", s=NS)
        b_lgT = g.ps[0:NS, 0, 0:CH * T].rearrange("p (b t) -> p b t", b=CH)
        b_dT = g.ps[0:T, 1, 0:CH * NS].rearrange("p (b s) -> p b s", b=CH)
        b_cT = g.ps[0:NS, 2, 0:CH * T].rearrange("p (b t) -> p b t", b=CH)
        b_y = g.ps[0:HALF, 3, 0:2 * CH * NS].rearrange("p (b k s) -> p b k s", b=CH, k=2)
        block = ctx.enter_context(nc.Block())

        def wide(small, n):
            return small.unsqueeze(2).broadcast_to([small.shape[0], small.shape[1], n])

        def chunk(q):
            return slice(q * CH, (q + 1) * CH)

        @block.vector
        def _(v):
            v.tensor_scalar(neg_mean[:, :], g.lnt[:, 0, :], -0.5, None, ALU.mult).then_inc(s_neg, 1)
            v.tensor_tensor(t_ms[:, :], g.rstd[:, :], g.rstd[:, :], ALU.mult).then_inc(s_chain, 1)
            v.wait_ge(s_chain, 1)
            v.tensor_scalar(t_ms[:, :], t_ms[:, :], -EPS, 1.0 + EPS, ALU.mult, ALU.add).then_inc(s_ms, 1)
            v.wait_ge(s_neg, 1)
            with v.Fori(0, B // UNROLL) as j:
                for i in range(UNROLL):
                    b = j * UNROLL + i
                    v.scalar_tensor_tensor(u[:, bass.ds(b, 1), :], g.h[:, bass.ds(b, 1), :], neg_mean[:, bass.ds(b, 1)],
                                           g.nw[:, :].unsqueeze(1), ALU.add, ALU.mult).then_inc(s_u, 1)
            v.wait_ge(s_root, 1)
            v.reciprocal(in_scale[:, :], root[:, 0, :]).then_inc(s_chain, 1)
            v.wait_ge(s_chain, 2)
            v.tensor_tensor(in_scale[:, :], in_scale[:, :], g.rstd[:, :], ALU.mult).then_inc(s_chain, 1)
            v.wait_ge(s_chain, 3)
            v.wait_ge(s_root, 2)
            v.tensor_tensor(ss[:, :], in_scale[:, :], root[:, 1, :], ALU.mult).then_inc(s_chain, 1)
            v.wait_ge(s_chain, 4)
            v.tensor_scalar(ss[:, :], ss[:, :], EPS, None, ALU.max).then_inc(s_chain, 1)
            v.wait_ge(s_chain, 5)
            v.reciprocal(lg_scale[:, :], ss[:, :]).then_inc(s_chain, 1)
            v.wait_ge(s_chain, 6)
            v.tensor_tensor(lg_scale[:, :], lg_scale[:, :], in_scale[:, :], ALU.mult).then_inc(s_scales, 1)
            v.wait_ge(s_scales, 1)
            v.wait_ge(s_raw, NP)

            def logits(q, i):
                v.tensor_tensor(lg[:, chunk(q), :], raw[:, chunk(q), :], wide(lg_scale[:, chunk(q)], NS),
                                ALU.mult).then_inc(s_lg, 1)
                item(v, s_lg, q)
                reused(v, s_csub, q, 2)
                v.tensor_reduce(cs[:, i, 0, :], lg[:, chunk(q), :], AX.X, ALU.max).then_inc(s_cmx, 1)

            def dispatch_max(q, i):
                item(v, s_lgT, q)
                v.tensor_reduce(dsm[:, i, 0, :], b_lgT, AX.X, ALU.max).then_inc(s_dmx, 1)
                item(v, s_dmx, q)
                reused(v, s_dTp, q, 2)
                v.tensor_tensor(dm[:, i, :, :], b_lgT, wide(dsm[:, i, 0, :], T), ALU.subtract).then_inc(s_dsub, 1)

            def combine_sum(q, i):
                item(v, s_cexp, q)
                v.tensor_reduce(cs[:, i, 1, :], lg[:, chunk(q), :], AX.X, ALU.add).then_inc(s_csum, 1)
                item(v, s_csum, q)
                reused(v, s_c, q, 2)
                v.reciprocal(cs[:, i, 2, :], cs[:, i, 1, :]).then_inc(s_crs, 1)

            def dispatch_sum(q, i):
                item(v, s_dexp, q)
                v.tensor_reduce(dsm[:, i, 1, :], dm[:, i, :, :], AX.X, ALU.add).then_inc(s_dsum, 1)
                item(v, s_dsum, q)
                reused(v, s_d, q, 2)
                v.reciprocal(dsm[:, i, 2, :], dsm[:, i, 1, :]).then_inc(s_drs, 1)

            def scale_turned(q, i):
                item(v, s_dTp, q)
                reused(v, s_yp, q, 2)
                v.tensor_tensor(dT[:, i, :, :], b_dT, wide(in_scale[:, chunk(q)], NS), ALU.mult).then_inc(s_dTs, 1)

            few_steps(NQ, [(dispatch_max, 1), (logits, 0), (scale_turned, 2), (dispatch_sum, 1), (combine_sum, 1)])

        @block.gpsimd
        def _(pool):
            def combine_sub(q, i):
                item(pool, s_cmx, q)
                item(pool, s_lgT, q)
                pool.tensor_tensor(lg[:, chunk(q), :], lg[:, chunk(q), :], wide(cs[:, i, 0, :], NS),
                                   ALU.subtract).then_inc(s_csub, 1)

            def scale_c(q, i):
                item(pool, s_crs, q)
                pool.tensor_tensor(lg[:, chunk(q), :], lg[:, chunk(q), :], wide(cs[:, i, 2, :], NS),
                                   ALU.mult).then_inc(s_c, 1)

            def scale_d(q, i):
                item(pool, s_drs, q)
                pool.tensor_tensor(dm[:, i, :, :], dm[:, i, :, :], wide(dsm[:, i, 2, :], T), ALU.mult).then_inc(s_d, 1)

            few_steps(NQ, [(combine_sub, 0), (scale_d, 1), (scale_c, 1)])

        @block.scalar
        def _(act):
            act.wait_ge(s_ms, 1)
            act.activation(root[:, 0, :], t_ms[:, :], ACT.Sqrt).then_inc(s_root, 1)

            def x_copy(q, i):
                item(act, s_xTp, q)
                reused(act, s_raw, q, 2)
                act.activation(xT[:, i % 2, :, :, :], b_x[i % 2], ACT.Copy).then_inc(s_xTs, 1)

            def square(q, i):
                for b in range(2):
                    act.wait_ge(s_u, q * 2 + b + 1)
                    reused(act, s_sq, q, 1, 2)
                    act.activation(junk[:, :].unsqueeze(1), u[:, bass.ds(q * 2 + b, 1), :], ACT.Square,
                                   accum_out=ss[:, bass.ds(q * 2 + b, 1)]).then_inc(s_sq, 1)
                    act.wait_ge(s_sq, q * 2 + b + 1)

            steps(act, NP, [(x_copy, 1), (square, 0)])
            act.activation(root[:, 1, :], ss[:, :], ACT.Sqrt).then_inc(s_root, 1)

            def combine_exp(q, i):
                item(act, s_csub, q)
                act.activation(lg[:, chunk(q), :], lg[:, chunk(q), :], ACT.Exp).then_inc(s_cexp, 1)

            def dispatch_exp(q, i):
                item(act, s_dsub, q)
                act.activation(dm[:, i, :, :], dm[:, i, :, :], ACT.Exp).then_inc(s_dexp, 1)

            def turned_copy(q, i):
                item(act, s_cTp, q)
                act.activation(g.combT[:, chunk(q), :], b_cT, ACT.Copy).then_inc(s_cTs, 1)

            def y_copy(q, i):
                item(act, s_yp, q)
                act.activation(g.yT[:, :, :, chunk(q)].rearrange("p k s b -> p b k s"), b_y,
                               ACT.Copy).then_inc(s_ys, 1)

            few_steps(NQ, [(dispatch_exp, 1), (combine_exp, 1), (turned_copy, 2), (y_copy, 3)])

        @block.tensor
        def _(pe):
            def transpose_x(q, i):
                item(pe, s_u, q, 2)
                reused(pe, s_xTs, q, 2)
                for b in range(2):
                    for k in range(2):
                        mm = pe.transpose(b_x[i % 2][:, b, k, :], u[:, q * 2 + b, k * HALF:(k + 1) * HALF],
                                          g.ident[0:T, 0:T])
                mm.then_inc(s_xTp, 1)

            def products(q, i):
                item(pe, s_xTs, q)
                for b in range(2):
                    for k in range(2):
                        mm = pe.matmul(raw[:, q * 2 + b, :], xT[:, i % 2, b, k, :], g.slT[:, k, :], start=(k == 0), stop=(k == 1))
                mm.then_inc(s_raw, 1)

            def transpose_logits(q, i):
                item(pe, s_lg, q)
                reused(pe, s_dsub, q, 1)
                for b in range(CH):
                    mm = pe.transpose(b_lgT[:, b, :], lg[:, q * CH + b, :],
                                      g.ident[0:T, 0:T])
                mm.then_inc(s_lgT, 1)

            def transpose_weights(q, i):
                item(pe, s_d, q)
                reused(pe, s_dTs, q, 1)
                for b in range(CH):
                    mm = pe.transpose(b_dT[:, b, :], dm[:, i, b, :], g.ident[0:NS, 0:NS])
                mm.then_inc(s_dTp, 1)
                item(pe, s_c, q)
                reused(pe, s_cTs, q, 1)
                for b in range(CH):
                    mm = pe.transpose(b_cT[:, b, :], lg[:, q * CH + b, :],
                                      g.ident[0:T, 0:T])
                mm.then_inc(s_cTp, 1)

            def gather(q, i):
                item(pe, s_dTs, q)
                reused(pe, s_ys, q, 1)
                for b in range(CH):
                    for k in range(2):
                        mm = pe.matmul(b_y[:, b, k, :], u[:, q * CH + b, k * HALF:(k + 1) * HALF], dT[:, i, b, :],
                                       start=True, stop=True)
                mm.then_inc(s_yp, 1)

            few_steps(NP, [(transpose_x, 0), (products, 1)])
            few_steps(NQ, [(transpose_logits, 0), (transpose_weights, 2), (gather, 3)])


def slot_ffn(nc, A, g):
    with ExitStack() as ctx:
        def sem(name):
            return g.phase_sem("f_" + name)

        def sb(name, shape, dt=F32):
            return ctx.enter_context(nc.sbuf_tensor("f_" + name, shape, dt))

        yg = sb("yg", [HALF + 1, 2, 2, GS, B])
        hid = sb("hid", [128, 2, F])
        hT = sb("hT", [128, 2, FC, 128])
        b2 = sb("b2", [128, NGR, D])
        y2g = sb("y2g", [128, 2, D])
        s_b2, s_one, s_yg, s_h1, s_gelu, s_hTp, s_hTs, s_y2p, s_y2s = (
            sem(n) for n in ("b2", "one", "yg", "h1", "gelu", "hTp", "hTs", "y2p", "y2s"))
        s_y2 = [sem(f"y2_{i}") for i in range(2)]
        N2 = F // 2
        block = ctx.enter_context(nc.Block())

        @block.sync
        def _(sp):
            bias = A["fc2_b"].rearrange("(g s) d -> s g d", s=GS)
            for s in range(GS):
                sp.dma_start(b2[B * s:B * (s + 1), :, :], bias[s].unsqueeze(0).broadcast_to([B, NGR, D])).then_inc(s_b2, 16)
            with sp.Fori(1, NGR // 2) as j:
                for u in range(2):
                    load_slots(sp, A, g, j * 2 + u, u, lambda: sp.wait_ge(s_h1, j * 2 + (u - 1)),
                               lambda: sp.wait_ge(s_y2p, j * 2 + (u - 1)))

        @block.gpsimd
        def _(pool):
            pool.memset(yg[HALF:HALF + 1, :, 1, :, :], 1.0).then_inc(s_one, 1)

            def pick(gr, i):
                reused(pool, s_h1, gr, 2)
                pool.tensor_copy(yg[0:HALF, i, :, :, :], g.yT[:, :, bass.ds(gr * GS, GS), :]).then_inc(s_yg, 1)

            steps(pool, NGR, [(pick, 0)], unroll=2, depth=2)

        @block.scalar
        def _(act):
            def gelu(gr, i):
                reused(act, s_hTp, gr, 2, 2)
                for n in range(2):
                    act.wait_ge(s_h1, gr + 1)
                    act.activation(hid[:, i, n * N2:(n + 1) * N2], g.ps[:, n, 0:N2], ACT.Gelu).then_inc(s_gelu, 1)

            def put(gr, i):
                item(act, s_y2s, gr)
                act.dma_start(g.y2[gr * GS:(gr + 1) * GS, :, :], y2g[:, i, :]).then_inc(s_y2[i], 16)

            for t in range(NGR + 1):
                if t < NGR:
                    gelu(t, t % 2)
                if t >= 1:
                    put(t - 1, (t - 1) % 2)
            for i in range(2):
                act.wait_ge(s_y2[i], 16 * NGR // 2)

        @block.vector
        def _(v):
            v.wait_ge(s_b2, 16 * GS)

            def turn_copy(gr, i):
                reused(v, s_y2p, gr, 2)
                for n in range(2):
                    v.wait_ge(s_hTp, gr * 2 + n + 1)
                    v.tensor_copy(hT[:, i, 3 * n:3 * n + 3, :], g.ps[:, 2 + n, 0:384].rearrange("p (k m) -> p k m", k=3)).then_inc(s_hTs, 1)

            def add_bias(gr, i):
                item(v, s_y2p, gr)
                if not isinstance(gr, int):
                    v.wait_ge(s_y2[i], (gr - i) * 8)
                elif gr >= 2:
                    v.wait_ge(s_y2[i], 16 * (gr // 2))
                v.tensor_tensor(y2g[:, i, :].unsqueeze(1), g.ps[:, 4, 0:D].unsqueeze(1),
                                b2[:, bass.ds(gr, 1), :], ALU.add).then_inc(s_y2s, 1)

            steps(v, NGR, [(turn_copy, 1), (add_bias, 1)], unroll=2, depth=2)

        @block.tensor
        def _(pe):
            pe.wait_ge(s_one, 1)

            def loaded(sems, gr, i, dmas):
                if isinstance(gr, int):
                    pe.wait_ge(sems[i], 16 * dmas * (gr // 2 + 1))
                else:
                    pe.wait_ge(sems[i], (gr - i) * (8 * dmas) + 16 * dmas)

            def first(gr, i):
                item(pe, s_yg, gr)
                loaded(g.s_w1, gr, i, W1_DMAS)
                reused(pe, s_gelu, gr, 1, 2)
                for n in range(2):
                    for k in range(2):
                        rows = HALF + k
                        for s in range(GS):
                            mm = pe.matmul(g.ps[B * s:B * (s + 1), n, 0:N2], yg[0:rows, i, k, s, :],
                                           g.w1[0:rows, i, k, s, n * N2:(n + 1) * N2],
                                           start=(k == 0), stop=(k == 1), tile_position=(0, B * s))
                mm.then_inc(s_h1, 1)

            def turn(gr, i):
                item(pe, s_gelu, gr, 2)
                for n in range(2):
                    if not isinstance(gr, int) or gr >= 1:
                        pe.wait_ge(s_hTs, gr * 2 + n - 1)
                    for k in range(3):
                        mm = pe.transpose(g.ps[:, 2 + n, 128 * k:128 * (k + 1)], hid[:, i, 3 * n + k:F:FC], g.ident[:, :])
                    mm.then_inc(s_hTp, 1)

            def second(gr, i):
                item(pe, s_hTs, gr, 2)
                loaded(g.s_w2, gr, i, 1)
                reused(pe, s_y2s, gr, 1)
                for k in range(FC):
                    for s in range(GS):
                        mm = pe.matmul(g.ps[B * s:B * (s + 1), 4, 0:D], hT[:, i, k, B * s:B * (s + 1)],
                                       g.w2[:, i, s, k * D:(k + 1) * D], start=(k == 0), stop=(k == FC - 1),
                                       tile_position=(0, B * s))
                mm.then_inc(s_y2p, 1)

            steps(pe, NGR, [(turn, 1), (first, 0), (second, 1)], unroll=2, depth=2)


def combine(nc, A, g):
    with ExitStack() as ctx:
        def sem(name):
            return g.phase_sem("c_" + name)

        cT = ctx.enter_context(nc.sbuf_tensor("c_cT", [NS, UNROLL, T], F32))
        s_cT, s_mm, s_res, s_st, s_ln = (sem(n) for n in ("cT", "mm", "res", "st", "ln"))
        block = ctx.enter_context(nc.Block())

        @block.gpsimd
        def _(pool):
            def pick(b, i):
                reused(pool, s_mm, b, 4)
                pool.tensor_copy(cT[:, i, :].unsqueeze(1), g.combT[:, bass.ds(b, 1), :]).then_inc(s_cT, 1)

            steps(pool, B, [(pick, 0)])

        @block.tensor
        def _(pe):
            def mix(b, i):
                item(pe, s_cT, b)
                reused(pe, s_res, b, 4)
                pe.matmul(g.ps[0:T, i, 0:D], cT[:, i, :], g.y2[:, bass.ds(b, 1), :].rearrange("p a d -> p (a d)"),
                          start=True, stop=True).then_inc(s_mm, 1)

            steps(pe, B, [(mix, 0)])

        @block.vector
        def _(v):
            def residual(b, i):
                item(v, s_mm, b)
                hb = g.h[:, bass.ds(b, 1), :]
                v.tensor_tensor(hb, g.ps[0:T, i, 0:D].unsqueeze(1), hb, ALU.add).then_inc(s_res, 1)

            def statistics(b, i):
                item(v, s_res, b)
                v.bn_stats(g.stats[:, bass.ds(b, 1), :].rearrange("p a s -> p (a s)"),
                           g.h[:, bass.ds(b, 1), :].rearrange("p a d -> p (a d)")).then_inc(s_st, 1)

            steps(v, B, [(residual, 0), (statistics, 1)])
            v.wait_ge(s_st, B)
            layernorm_scale(v, None, g, s_ln)

        @block.scalar
        def _(act):
            layernorm_scale(None, act, g, s_ln)


def attention1(nc, A, g):
    with ExitStack() as ctx:
        def sem(name):
            return g.phase_sem("b_" + name)

        def sb(name, shape, dt=F32):
            return ctx.enter_context(nc.sbuf_tensor("b_" + name, shape, dt))

        wqkv = sb("wqkv", [HALF, 2, 3 * D])
        cos = sb("cos", [T, 2 * D])
        sin = sb("sin", [T, D])
        nsin = sb("nsin", [T, D])
        mask = sb("mask", [T, T])
        xn = sb("xn", [T, 2, D])
        xT = sb("xT", [HALF, 2, 2, T])
        vv = sb("vv", [T, 4, D])
        ra = sb("ra", [T, 2, 2 * D])
        rb = sb("rb", [T, 2, 2 * D])
        qkT = sb("qkT", [HALF, 2, 4, T])
        p = sb("p", [T, 2, T])
        pT = sb("pT", [T, 2, T])
        sc = sb("sc", [T, 4, 4])
        hn = sb("hn", [T, 4, D])
        hT = sb("hT", [HALF, 2, 2, T])
        wr = sb("wr", [HALF, 2, NE])
        ones = sb("ones", [HALF, T])
        s_keep, s_hTp, s_hTs, s_gp, s_gs, s_ones, s_cs = (
            sem(n) for n in ("keep", "hTp", "hTs", "gp", "gs", "ones", "cs"))
        (s_w, s_xn, s_xTp, s_xTs, s_qk, s_v, s_vs, s_ra, s_rot, s_rTp, s_rTs, s_sc, s_msk, s_mx, s_nm, s_exp, s_rs,
         s_pTp, s_pTs, s_o, s_res, s_st, s_ln) = (sem(n) for n in (
             "w", "xn", "xTp", "xTs", "qk", "v", "vs", "ra", "rot", "rTp", "rTs", "sc", "msk", "mx", "nm", "exp", "rs",
             "pTp", "pTs", "o", "res", "st", "ln"))
        b_x = g.ps[0:HALF, 0, 0:2 * T].rearrange("p (k t) -> p k t", k=2)
        b_qk = g.ps[0:T, 1, 0:2 * D]
        b_v = g.ps[0:T, 2, 0:D]
        b_rT = g.ps[0:HALF, 3, 0:4 * T].rearrange("p (m t) -> p m t", m=4)
        b_sc = g.ps[0:T, 4, 0:T]
        b_pT = g.ps[0:T, 5, 0:T]
        b_o = g.ps[0:T, 6, 0:D]
        b_hT = g.ps[0:HALF, 7, 0:2 * T].rearrange("p (k t) -> p k t", k=2)
        b_g = g.ps[0:T, 7, 2 * T:2 * T + NE]
        b_cs = g.ps[0:T, 7, 2 * T + NE:2 * T + 2 * NE]
        SCALE = D ** -0.5
        block = ctx.enter_context(nc.Block())

        @block.sync
        def _(sp):
            sp.dma_start(wqkv[:, :, :], A["a1_wqkv"].rearrange("(k p) n -> p k n", k=2)).then_inc(s_w, 16)
            sp.dma_start(cos[:, :], A["rope_cos"]).then_inc(s_w, 16)
            sp.dma_start(sin[:, :], A["rope_sin"]).then_inc(s_w, 16)
            sp.dma_start(nsin[:, :], A["rope_nsin"]).then_inc(s_w, 16)
            sp.dma_start(mask[:, :], A["causal"]).then_inc(s_w, 16)
            sp.dma_start(wr[:, :, :], A["moe_wr"].rearrange("(k p) e -> p k e", k=2)).then_inc(s_w, 16)
            sp.dma_start(g.iota[:, :], A["iota"]).then_inc(g.s_rw, 16)
            sp.dma_start(g.padrow[:, :], A["padrow"]).then_inc(g.s_rw, 16)
            sp.dma_start(g.before[:, :], A["before"]).then_inc(g.s_rw, 16)
            sp.dma_start(g.tokid[:, :], A["tokid"]).then_inc(g.s_rw, 16)
            for k in range(2):
                sp.dma_start(g.e1[0:HALF, k, :, :], A["moe_w1"][:, k * HALF:(k + 1) * HALF, :].rearrange(
                    "e p n -> p e n")).then_inc(g.s_e, 16)
            sp.dma_start(g.e1[HALF:HALF + 1, 1, :, :], A["moe_b1"].unsqueeze(0)).then_inc(g.s_e, 16)
            for k in range(FC):
                sp.dma_start(g.e2[:, k, :, :], A["moe_w2"][:, k * 128:(k + 1) * 128, :].rearrange(
                    "e p n -> p e n")).then_inc(g.s_e, 16)

        @block.vector
        def _(v):
            v.wait_ge(s_w, 6 * 16)

            def norm_input(b, i):
                reused(v, s_xTp, b, 2)
                v.tensor_scalar(xn[:, i % 2, :].unsqueeze(1), g.h[:, bass.ds(b, 1), :], g.rstd[:, bass.ds(b, 1)],
                                g.nmr[:, bass.ds(b, 1)], ALU.mult, ALU.add).then_inc(s_xn, 1)

            def rotate(b, i):
                k = i % 2
                item(v, s_qk, b)
                reused(v, s_rTp, b, 2)
                pair = b_qk.rearrange("p (n two) -> p n two", two=2)
                out = rb[:, k, :].rearrange("p (n two) -> p n two", two=2)
                v.tensor_tensor(ra[:, k, :], b_qk, cos[:, :], ALU.mult)
                v.tensor_tensor(out[:, :, 0], pair[:, :, 1], nsin[:, :], ALU.mult)
                v.tensor_tensor(out[:, :, 1], pair[:, :, 0], sin[:, :], ALU.mult).then_inc(s_ra, 1)

            def soften(b, i):
                k = i % 2
                item(v, s_sc, b)
                reused(v, s_pTp, b, 2)
                v.tensor_tensor(p[:, k, :], b_sc, mask[:, :], ALU.add).then_inc(s_msk, 1)
                item(v, s_msk, b)
                v.tensor_reduce(sc[:, i, 0:1], p[:, k, :], AX.X, ALU.max).then_inc(s_mx, 1)
                item(v, s_mx, b)
                v.tensor_scalar(sc[:, i, 1:2], sc[:, i, 0:1], -SCALE, None, ALU.mult).then_inc(s_nm, 1)

            def inverse(b, i):
                item(v, s_exp, b)
                v.reciprocal(sc[:, i, 3:4], sc[:, i, 2:3]).then_inc(s_rs, 1)

            def residual(b, i):
                item(v, s_rs, b)
                item(v, s_o, b)
                reused(v, s_hTp, b, 4)
                reused(v, s_keep, b, 4)
                v.scalar_tensor_tensor(hn[:, i, :].unsqueeze(1), b_o.unsqueeze(1), sc[:, i, 3:4], g.h[:, bass.ds(b, 1), :],
                                       ALU.mult, ALU.add).then_inc(s_res, 1)

            def statistics(b, i):
                item(v, s_res, b)
                v.bn_stats(g.stats[:, bass.ds(b, 1), :].rearrange("p a s -> p (a s)"), hn[:, i, :]).then_inc(s_st, 1)

            def gate_copy(b, i):
                item(v, s_gp, b)
                v.tensor_copy(g.lg[:, bass.ds(b, 1), :], b_g.unsqueeze(1)).then_inc(s_gs, 1)

            v.wait_ge(s_cs, 1)
            v.tensor_copy(g.colsum[:, :], b_cs).then_inc(s_cs, 1)
            steps(v, B, [(residual, 5), (norm_input, 0), (gate_copy, 7), (statistics, 5), (inverse, 4), (rotate, 2),
                         (soften, 3)])
            v.wait_ge(s_st, B)
            layernorm_scale(v, None, g, s_ln)

        @block.gpsimd
        def _(pool):
            pool.memset(ones[:, :], 1.0).then_inc(s_ones, 1)

            def keep(b, i):
                item(pool, s_res, b)
                pool.tensor_copy(g.h[:, bass.ds(b, 1), :], hn[:, i, :].unsqueeze(1)).then_inc(s_keep, 1)

            def add_parts(b, i):
                k = i % 2
                item(pool, s_ra, b)
                pool.tensor_tensor(ra[:, k, :], ra[:, k, :], rb[:, k, :], ALU.add).then_inc(s_rot, 1)

            steps(pool, B, [(keep, 5), (add_parts, 2)])

        @block.scalar
        def _(act):
            def x_copy(b, i):
                item(act, s_xTp, b)
                reused(act, s_v, b, 2)
                act.activation(xT[:, i % 2, :, :], b_x, ACT.Copy).then_inc(s_xTs, 1)

            def r_copy(b, i):
                item(act, s_rTp, b)
                reused(act, s_sc, b, 2)
                act.activation(qkT[:, i % 2, :, :], b_rT, ACT.Copy).then_inc(s_rTs, 1)

            def p_copy(b, i):
                item(act, s_pTp, b)
                reused(act, s_o, b, 2)
                act.activation(pT[:, i % 2, :], b_pT, ACT.Copy).then_inc(s_pTs, 1)

            def v_copy(b, i):
                item(act, s_v, b)
                reused(act, s_o, b, 4)
                act.activation(vv[:, i, :], b_v, ACT.Copy).then_inc(s_vs, 1)

            def exponent(b, i):
                item(act, s_nm, b)
                reused(act, s_res, b, 4)
                act.activation(p[:, i % 2, :], p[:, i % 2, :], ACT.Exp, scale=SCALE, bias=sc[:, i, 1:2],
                               accum_out=sc[:, i, 2:3]).then_inc(s_exp, 1)

            def h_copy(b, i):
                item(act, s_hTp, b)
                reused(act, s_gp, b, 2)
                act.activation(hT[:, i % 2, :, :], b_hT, ACT.Copy).then_inc(s_hTs, 1)

            steps(act, B, [(x_copy, 1), (r_copy, 3), (p_copy, 4), (h_copy, 6), (v_copy, 2), (exponent, 3)])
            layernorm_scale(None, act, g, s_ln)

        @block.tensor
        def _(pe):
            pe.wait_ge(s_w, 6 * 16)
            pe.wait_ge(s_ones, 1)
            for k in range(2):
                mm = pe.matmul(b_cs, ones[:, :], wr[:, k, :], start=(k == 0), stop=(k == 1))
            mm.then_inc(s_cs, 1)

            def transpose_x(b, i):
                item(pe, s_xn, b)
                reused(pe, s_xTs, b, 1)
                for k in range(2):
                    mm = pe.transpose(b_x[:, k, :], xn[:, i % 2, k * HALF:(k + 1) * HALF], g.ident[0:T, 0:T])
                mm.then_inc(s_xTp, 1)

            def transpose_qk(b, i):
                item(pe, s_rot, b)
                reused(pe, s_rTs, b, 1)
                for m in range(4):
                    mm = pe.transpose(b_rT[:, m, :], ra[:, i % 2, m * HALF:(m + 1) * HALF], g.ident[0:T, 0:T])
                mm.then_inc(s_rTp, 1)

            def transpose_p(b, i):
                item(pe, s_exp, b)
                reused(pe, s_pTs, b, 1)
                pe.transpose(b_pT, p[:, i % 2, :], g.ident[0:T, 0:T]).then_inc(s_pTp, 1)

            def project(b, i):
                item(pe, s_xTs, b)
                reused(pe, s_ra, b, 1)
                for k in range(2):
                    mm = pe.matmul(b_qk, xT[:, i % 2, k, :], wqkv[:, k, 0:2 * D], start=(k == 0), stop=(k == 1))
                mm.then_inc(s_qk, 1)

            def project_v(b, i):
                reused(pe, s_vs, b, 1)
                for k in range(2):
                    mm = pe.matmul(b_v, xT[:, i % 2, k, :], wqkv[:, k, 2 * D:3 * D], start=(k == 0), stop=(k == 1))
                mm.then_inc(s_v, 1)

            def score(b, i):
                item(pe, s_rTs, b)
                reused(pe, s_msk, b, 1)
                for k in range(2):
                    mm = pe.matmul(b_sc, qkT[:, i % 2, k, :], qkT[:, i % 2, 2 + k, :], start=(k == 0), stop=(k == 1))
                mm.then_inc(s_sc, 1)

            def attend(b, i):
                item(pe, s_pTs, b)
                item(pe, s_vs, b)
                reused(pe, s_res, b, 1)
                pe.matmul(b_o, pT[:, i % 2, :], vv[:, i, :], start=True, stop=True).then_inc(s_o, 1)

            def turn_h(b, i):
                item(pe, s_res, b)
                reused(pe, s_hTs, b, 1)
                reused(pe, s_gs, b, 1)
                for k in range(2):
                    mm = pe.transpose(b_hT[:, k, :], hn[:, i, k * HALF:(k + 1) * HALF], g.ident[0:T, 0:T])
                mm.then_inc(s_hTp, 1)

            def gate(b, i):
                item(pe, s_hTs, b)
                for k in range(2):
                    mm = pe.matmul(b_g, hT[:, i % 2, k, :], wr[:, k, :], start=(k == 0), stop=(k == 1))
                mm.then_inc(s_gp, 1)

            pe.wait_ge(s_cs, 2)
            steps(pe, B, [(gate, 7), (transpose_x, 1), (project, 2), (transpose_qk, 3), (transpose_p, 4), (turn_h, 6),
                          (project_v, 2), (score, 3), (attend, 4)])


def route(nc, A, g):
    with ExitStack() as ctx:
        def sem(name):
            return g.phase_sem("r1_" + name)

        def sb(name, shape, dt=F32):
            return ctx.enter_context(nc.sbuf_tensor("r1_" + name, shape, dt))

        iota, padrow, before, tokid = g.iota, g.padrow, g.before, g.tokid
        ones = sb("ones", [T, 256])
        key = sb("key", [T, B, NE])
        oh = sb("oh", [T, 2, B, NE])
        lg2 = sb("lg2", [T, B, NE])
        both = sb("both", [T, B, NE])
        m = sb("m", [T, 2, B])
        ex = sb("ex", [T, B])
        c = sb("c", [T, 2, B])
        cnt = sb("cnt", [T, NE, B])
        cum = sb("cum", [T, NE, B])
        pos = sb("pos", [T, NE, B])
        e8 = sb("e8", [T, 6, NE])
        place = sb("place", [T, 2, B])
        tile = sb("tile", [T, 2, B])
        row = sb("row", [T, 2, B])
        PART = NPAIR // 4
        ohp = sb("ohp", [T, 2, PART, 128], F32R)
        info = sb("info", [T, 4, PART, 4, NTILES], F32R)
        c_hi = sb("c_hi", [T, 2, B], F32R)
        c_lo = sb("c_lo", [T, 2, B], F32R)
        tge = sb("tge", [T, NTILES, NE])
        tef = sb("tef", [T, NTILES])
        lst = sb("lst", [128, 2, NTILES])
        zero = sb("zero", [128, D])
        s_h, s_zero, s_norm, s_tab = (sem(n) for n in ("h", "zero", "norm", "tab"))
        s_ones, s_v, s_d, s_ex, s_both, s_pre, s_occ, s_info, s_ohp, s_part, s_chi, s_clo, s_list = (
            sem(n) for n in ("ones", "v", "d", "ex", "both", "pre", "occ", "info", "ohp", "part", "chi", "clo", "list"))
        MAGIC = 1.5 * 2 ** 23
        b_intra = g.ps[0:T, 0, 0:256].rearrange("p (e b) -> p e b", e=NE)
        b_cnt = g.ps[0:T, 1, 0:256].rearrange("p (e b) -> p e b", e=NE)
        b_list = g.ps[:, 2, 0:4 * NTILES].rearrange("p (c n) -> p c n", c=4)
        block = ctx.enter_context(nc.Block())

        @block.sync
        def _(sp):
            sp.dma_start(A["out"][0:NTOK, :].rearrange("(b t) d -> t b d", t=T), g.h[:, :, :]).then_inc(s_h, 16)
            sp.wait_ge(s_zero, 1)
            sp.dma_start(A["out"][NTOK:NTOK + 128, :], zero[:, :]).then_inc(s_tab, 16)
            sp.dma_start(A["xtab"][NTOK:NTOK + 128, :], zero[:, :]).then_inc(s_tab, 16)
            rows = A["xtab"][0:NTOK, :].rearrange("(b t) d -> t b d", t=T)
            for q in range(4):
                sp.wait_ge(s_norm, (q + 1) * B // 4)
                part = slice(q * B // 4, (q + 1) * B // 4)
                sp.dma_start(rows[:, part, :], g.h[:, part, :]).then_inc(s_tab, 16)
            sp.wait_ge(s_tab, 6 * 16)

        @block.gpsimd
        def _(pool):
            pool.memset(ones[:, :], 1.0).then_inc(s_ones, 1)
            pool.memset(zero[:, :], 0.0).then_inc(s_zero, 1)
            pool.wait_ge(s_clo, 1)
            for q in range(4):
                pool.wait_ge(s_occ, q + 1)
                occ = info[:, q, :, 0, :].bitcast(F32)
                cols = slice(PART * (q % 2), PART * (q % 2) + PART)
                pool.tensor_tensor(info[:, q, :, 1, :], occ, tokid[:, cols].unsqueeze(2).broadcast_to([T, PART, NTILES]),
                                   ALU.mult).then_inc(s_info, 1)
                pool.tensor_tensor(info[:, q, :, 3, :], occ, c_lo[:, q // 2, cols].bitcast(F32).unsqueeze(2).broadcast_to(
                    [T, PART, NTILES]), ALU.mult).then_inc(s_info, 1)

        @block.scalar
        def _(act):
            act.wait_ge(s_d, 1)
            act.activation(ex[:, :], ex[:, :], ACT.Exp).then_inc(s_ex, 1)
            act.wait_ge(s_h, 16)
            with act.Fori(0, B // UNROLL) as j:
                for i in range(UNROLL):
                    hb = g.h[:, bass.ds(j * UNROLL + i, 1), :]
                    act.activation(hb, hb, ACT.Identity, scale=g.rstd[:, bass.ds(j * UNROLL + i, 1)],
                                   bias=g.nmr[:, bass.ds(j * UNROLL + i, 1)]).then_inc(s_norm, 1)

        @block.vector
        def _(v):
            done = [0]

            def link(ins):
                done[0] += 1
                ins.then_inc(s_v, 1)
                v.wait_ge(s_v, done[0])

            def wide(x, n):
                return x.unsqueeze(2).broadcast_to([x.shape[0], x.shape[1], n])

            v.wait_ge(g.s_rw, 64)
            v.wait_ge(s_ones, 1)
            link(v.tensor_tensor(g.lg[:, :, :], g.lg[:, :, :], wide(g.rstd[:, :], NE), ALU.mult))
            link(v.tensor_tensor(key[:, :, :], wide(g.nmr[:, :], NE),
                                 g.colsum[:, :].unsqueeze(1).broadcast_to([T, B, NE]), ALU.mult))
            link(v.tensor_tensor(g.lg[:, :, :], g.lg[:, :, :], key[:, :, :], ALU.add))
            experts = iota[0:T, 0:NE].unsqueeze(1).broadcast_to([T, B, NE])
            for k in range(2):
                src = g.lg if k == 0 else lg2
                link(v.tensor_reduce(m[:, k, :], src[:, :, :], AX.X, ALU.max))
                link(v.tensor_tensor(key[:, :, :], src[:, :, :], wide(m[:, k, :], NE), ALU.is_equal))
                link(v.scalar_tensor_tensor(key[:, :, :], key[:, :, :], -float(NE), experts, ALU.mult, ALU.add))
                link(v.tensor_reduce(place[:, 0, :], key[:, :, :], AX.X, ALU.min))
                link(v.tensor_tensor(oh[:, k, :, :], key[:, :, :], wide(place[:, 0, :], NE), ALU.is_equal))
                if k == 0:
                    link(v.scalar_tensor_tensor(lg2[:, :, :], oh[:, 0, :, :], -1e30, g.lg[:, :, :], ALU.mult, ALU.add))
            v.tensor_tensor(ex[:, :], m[:, 1, :], m[:, 0, :], ALU.subtract).then_inc(s_d, 1)
            v.tensor_tensor(both[:, :, :], oh[:, 0, :, :], oh[:, 1, :, :], ALU.add).then_inc(s_both, 1)
            v.wait_ge(s_ex, 1)
            link(v.tensor_scalar(c[:, 1, :], ex[:, :], 1.0, None, ALU.add))
            link(v.reciprocal(c[:, 0, :], c[:, 1, :]))
            link(v.tensor_tensor(c[:, 1, :], ex[:, :], c[:, 0, :], ALU.mult))
            v.wait_ge(s_pre, 1)
            link(v.tensor_copy(cnt[:, :, :], b_cnt))
            link(v.tensor_tensor_scan(cum[:, :, :].rearrange("p e b -> p (e b)"), ones[:, :],
                                      cnt[:, :, :].rearrange("p e b -> p (e b)"), 0.0, ALU.mult, ALU.add))
            upto_, n_, tiles, ctiles, shift = (e8[:, i, :] for i in range(5))
            start = e8[:, 5, :]
            link(v.tensor_copy(upto_, cum[:, :, B - 1]))
            link(v.memset(start, 0.0))
            link(v.tensor_copy(e8[:, 5, 1:NE], e8[:, 0, 0:NE - 1]))
            link(v.tensor_tensor(n_, upto_, start, ALU.subtract))
            link(v.tensor_scalar(tiles, n_, 1.0 / 128, 127.0 / 128 - 0.5 + 1.0 / 256, ALU.mult, ALU.add))
            link(v.tensor_scalar(tiles, tiles, MAGIC, None, ALU.add))
            link(v.tensor_scalar(tiles, tiles, -MAGIC, None, ALU.add))
            link(v.tensor_tensor_scan(ctiles, ones[:, 0:NE], tiles, 0.0, ALU.mult, ALU.add))
            link(v.tensor_tensor(shift, ctiles, tiles, ALU.subtract))
            link(v.scalar_tensor_tensor(shift, shift, 128.0, start, ALU.mult, ALU.subtract))
            link(v.tensor_tensor(pos[:, :, :], cum[:, :, :], cnt[:, :, :], ALU.subtract))
            link(v.tensor_tensor(pos[:, :, :], b_intra, pos[:, :, :], ALU.add))
            link(v.tensor_tensor(pos[:, :, :], pos[:, :, :], wide(shift, B), ALU.add))
            for k in range(2):
                link(v.tensor_tensor(key[:, :, :], pos[:, :, :].rearrange("p e b -> p b e"), oh[:, k, :, :], ALU.mult))
                link(v.tensor_reduce(place[:, k, :], key[:, :, :], AX.X, ALU.add))
            link(v.tensor_scalar(tile[:, :, :], place[:, :, :], 1.0 / 128, -0.5 + 1.0 / 256, ALU.mult, ALU.add))
            link(v.tensor_scalar(tile[:, :, :], tile[:, :, :], MAGIC, None, ALU.add))
            link(v.tensor_scalar(tile[:, :, :], tile[:, :, :], -MAGIC, None, ALU.add))
            link(v.scalar_tensor_tensor(row[:, :, :], tile[:, :, :], -128.0, place[:, :, :], ALU.mult, ALU.add))
            flat = lambda x: x[:, :, :].rearrange("p k b -> p (k b)")
            v.tensor_copy(c_hi[:, :, :], c[:, :, :]).then_inc(s_chi, 1)
            v.wait_ge(s_chi, 1)
            v.tensor_tensor(c_lo[:, :, :], c[:, :, :], c_hi[:, :, :].bitcast(F32), ALU.subtract).then_inc(s_clo, 1)
            for q in range(4):
                cols = slice(PART * q, PART * q + PART)
                v.tensor_tensor(info[:, q, :, 0, :], iota[0:T, 0:NTILES].unsqueeze(1).broadcast_to([T, PART, NTILES]),
                                wide(flat(tile)[:, cols], NTILES), ALU.is_equal).then_inc(s_occ, 1)
                if q >= 2:
                    v.wait_ge(s_part, q - 1)
                v.tensor_tensor(ohp[:, q % 2, :, :], iota[0:T, :].unsqueeze(1).broadcast_to([T, PART, 128]),
                                wide(flat(row)[:, cols], 128), ALU.is_equal).then_inc(s_ohp, 1)
                v.wait_ge(s_occ, q + 1)
                v.tensor_tensor(info[:, q, :, 2, :], info[:, q, :, 0, :].bitcast(F32),
                                wide(flat(c_hi)[:, cols].bitcast(F32), NTILES), ALU.mult).then_inc(s_ohp, 1)
            link(v.tensor_tensor(tge[:, :, :], wide(iota[0:T, 0:NTILES], NE),
                                 ctiles.unsqueeze(1).broadcast_to([T, NTILES, NE]), ALU.is_ge))
            link(v.tensor_reduce(tef[:, :], tge[:, :, :], AX.X, ALU.add))
            link(v.tensor_scalar(g.te[0:T, :], tef[:, :], float(NE - 1), None, ALU.min))
            v.wait_ge(s_list, 1)
            link(v.tensor_copy(lst[:, 0, :], b_list[:, 0, :]))
            link(v.scalar_tensor_tensor(lst[:, 1, :], lst[:, 0, :], padrow[:, 1:2], b_list[:, 1, :], ALU.mult, ALU.add))
            link(v.tensor_scalar(g.idx[:, :], lst[:, 1, :], padrow[:, 0:1], None, ALU.add))
            link(v.tensor_copy(g.cw[:, :], b_list[:, 2, :]))
            link(v.tensor_tensor(g.cw[:, :], b_list[:, 3, :], g.cw[:, :], ALU.add))

        @block.tensor
        def _(pe):
            pe.wait_ge(s_both, 1)
            flat = both[:, :, :].rearrange("p b e -> p e b")
            pe.matmul(b_intra, before[:, :], flat, start=True, stop=True)
            pe.matmul(b_cnt, ones[:, 0:T], flat, start=True, stop=True).then_inc(s_pre, 1)
            for q in range(4):
                pe.wait_ge(s_ohp, 2 * q + 2)
                pe.wait_ge(s_info, 2 * q + 2)
                for j in range(PART):
                    mm = pe.matmul(b_list, ohp[:, q % 2, j, :], info[:, q, j, :, :], start=(q == 0 and j == 0),
                                   stop=(q == 3 and j == PART - 1))
                mm.then_inc(s_list if q == 3 else s_part, 1)


def expert_tiles(nc, A, g):
    NCOL = NE // 4 * F
    with ExitStack() as ctx:
        def sem(name):
            return g.phase_sem("x_" + name)

        def sb(name, shape, dt=F32):
            return ctx.enter_context(nc.sbuf_tensor("x_" + name, shape, dt))

        e1_lo = sb("e1_lo", [128, 2, NE, F], F32R)
        pairs = sb("pairs", [128, 2, FC - 1, NE, D], F32R)
        e1_hi = sb("e1_hi", [HALF + 1, 2, NE, F], F32R)
        last = sb("last", [128, 2, NE, D], F32R)
        e2 = [pairs[:, :, k, :, :] for k in range(FC - 1)] + [last[:, :, :, :]]
        pieces = [(g.e1[0:HALF + k, k, q:q + 2, :], e1_hi[0:HALF + k, k, q:q + 2, :], e1_lo[0:HALF + k, k, q:q + 2, :])
                  for k in range(2) for q in range(0, NE, 2)]
        n1 = len(pieces)
        pieces += [(g.e2[:, k, :, :], e2[k][:, 1], e2[k][:, 0]) for k in (FC - 1, *range(1, FC - 1), 0)]
        on_pool = (2, 5, n1 + 2, n1 + 4)
        on_vector = [n for n in range(len(pieces)) if n not in on_pool]
        early, late = range(n1, n1 + 3), range(n1 + 3, len(pieces))
        xg = sb("xg", [128, NX, D])
        x_hi = sb("x_hi", [HALF + 1, 2, 128], F32R)
        x_lo = sb("x_lo", [HALF, 2, 128], F32R)
        hid = sb("hid", [128, F])
        h_hi = sb("h_hi", [128, FC, 128], F32R)
        h_lo = sb("h_lo", [128, FC, 128], F32R)
        b2 = sb("b2", [128, NE, D])
        ys = sb("ys", [128, 2, D])
        s_sum = sem("sum")
        s_b2, s_mem, s_one, s_hi, s_lo_v, s_lo_p, s_xTp, s_xh, s_xl, s_h1, s_r0, s_r1, s_hTp, s_hh, s_hl, s_y, s_ya, s_ys = (
            sem(n) for n in ("b2", "mem", "one", "hi", "lo_v", "lo_p", "xTp", "xh", "xl", "h1", "r0", "r1", "hTp", "hh",
                             "hl", "y", "ya", "ys"))
        N2 = F // 2
        s_x, s_add = g.s_x, g.s_add
        b_x = g.ps[0:HALF, 0, 0:256].rearrange("p (k t) -> p k t", k=2)
        b_h = [g.ps[:, 1 + n, 0:N2] for n in range(2)]
        b_hT = [g.ps[:, 3 + n, 0:3 * 128].rearrange("p (k t) -> p k t", k=3) for n in range(2)]
        b_y = [g.ps[:, 5 + i, 0:2 * D].rearrange("p (two d) -> p two d", two=2) for i in range(2)]
        block = ctx.enter_context(nc.Block())

        @block.sync
        def _(sp):
            sp.dma_start(b2[:, :, :], A["moe_b2"].unsqueeze(0).broadcast_to([128, NE, D])).then_inc(s_b2, 16)

        @block.gpsimd
        def _(pool):
            pool.memset(hid[HALF:HALF + 1, 0:128], 1.0).then_inc(s_mem, 1)
            pool.wait_ge(s_mem, 1)
            pool.tensor_copy(x_hi[HALF:HALF + 1, 1, :], hid[HALF:HALF + 1, 0:128]).then_inc(s_one, 1)
            pool.wait_ge(s_one, 1)
            for t in range(NTILES + 4):
                if t < NTILES:
                    if t >= NX:
                        pool.wait_ge(s_xTp, t - NX + 1)
                    pool.indirect_dma_start(out=xg[:, t % NX, :], out_offset=None, in_=A["xtab"][:, :],
                                            in_offset=bass.IndirectOffsetOnAxis(ap=g.idx[:, t:t + 1], axis=0)
                                            ).then_inc(s_x[t % NX], 16)
                if t == NX - 1:
                    for n in on_pool:
                        pool.wait_ge(s_hi, n + 1)
                        full, hi, lo = pieces[n]
                        pool.tensor_tensor(lo, full, hi.bitcast(F32), ALU.subtract).then_inc(s_lo_p, 1)
                i = t - 4
                if i >= 0:
                    pool.wait_ge(s_ys, i + 1)
                    if i >= 1:
                        pool.wait_ge(s_add, 16 * i)
                    pool.indirect_dma_start(out=A["out"][:, :],
                                            out_offset=bass.IndirectOffsetOnAxis(ap=g.idx[:, i:i + 1], axis=0),
                                            in_=ys[:, i % 2, :], in_offset=None, compute_op=ALU.add).then_inc(s_add, 16)
            pool.wait_ge(s_add, 16 * NTILES)

        @block.scalar
        def _(act):
            act.wait_ge(g.s_e, 16 * 9)

            def split(numbers):
                for n in numbers:
                    full, hi, _ = pieces[n]
                    if n == len(pieces) - 1:
                        act.wait_ge(s_lo_v, on_vector.index(n1) + 1)
                    act.activation(hi, full, ACT.Copy).then_inc(s_hi, 1)

            split(range(n1))

            def x_copy(i, u):
                item(act, s_xTp, i)
                reused(act, s_h1, i, 1, 2)
                act.activation(x_hi[0:HALF, :, :], b_x, ACT.Copy).then_inc(s_xh, 1)
                if isinstance(i, int) and i == 0:
                    split(early)

            def relu(i, u):
                reused(act, s_hTp, i, 1, 2)
                act.wait_ge(s_h1, i * 2 + 1)
                act.activation(hid[:, 0:N2], b_h[0], ACT.Relu).then_inc(s_r0, 1)

            def turn_copy(i, u):
                reused(act, s_y, i, 1)
                for n in range(2):
                    act.wait_ge(s_hTp, i * 2 + n + 1)
                    act.activation(h_hi[:, 3 * n:3 * n + 3, :], b_hT[n], ACT.Copy).then_inc(s_hh, 1)
                if isinstance(i, int) and i == 0:
                    split(late)

            def weigh(i, u):
                item(act, s_ya, i)
                act.activation(ys[:, u % 2, :], ys[:, u % 2, :], ACT.Copy,
                               scale=g.cw[:, bass.ds(i, 1)]).then_inc(s_ys, 1)

            steps(act, NTILES, [(relu, 1), (x_copy, 0), (turn_copy, 1), (weigh, 2)])

        @block.vector
        def _(v):
            def split(numbers):
                for n in numbers:
                    if n in on_vector:
                        v.wait_ge(s_hi, n + 1)
                        full, hi, lo = pieces[n]
                        v.tensor_tensor(lo, full, hi.bitcast(F32), ALU.subtract).then_inc(s_lo_v, 1)

            split(range(n1))
            v.wait_ge(s_b2, 16)
            v.wait_ge(s_one, 1)

            def x_rest(i, u):
                item(v, s_xh, i)
                v.tensor_tensor(x_lo[:, :, :], b_x, x_hi[0:HALF, :, :].bitcast(F32), ALU.subtract).then_inc(s_xl, 1)
                if isinstance(i, int) and i == 0:
                    split(early)

            def relu(i, u):
                reused(v, s_hTp, i, 1, 2)
                v.wait_ge(s_h1, i * 2 + 2)
                v.tensor_scalar(hid[:, N2:F], b_h[1], 0.0, None, ALU.max).then_inc(s_r1, 1)

            def turn_rest(i, u):
                for n in range(2):
                    v.wait_ge(s_hh, i * 2 + n + 1)
                    v.tensor_tensor(h_lo[:, 3 * n:3 * n + 3, :], b_hT[n], h_hi[:, 3 * n:3 * n + 3, :].bitcast(F32),
                                    ALU.subtract).then_inc(s_hl, 1)
                if isinstance(i, int) and i == 0:
                    split(late)

            def add_bias(i, u):
                e = v.value_load(g.te[0:1, bass.ds(i, 1)], min_val=0, max_val=NE - 1)
                item(v, s_y, i)
                if not isinstance(i, int) or i >= 2:
                    v.wait_ge(s_add, i * 16 - 16)
                v.tensor_tensor(ys[:, u % 2, :].unsqueeze(1), b_y[u % 2][:, 0, :].unsqueeze(1), b2[:, bass.ds(e, 1), :],
                                ALU.add).then_inc(s_sum, 1)
                item(v, s_sum, i)
                v.tensor_tensor(ys[:, u % 2, :], b_y[u % 2][:, 1, :], ys[:, u % 2, :], ALU.add).then_inc(s_ya, 1)

            steps(v, NTILES, [(relu, 1), (x_rest, 0), (turn_rest, 1), (add_bias, 2)])

        @block.tensor
        def _(pe):
            pe.wait_ge(s_one, 1)

            regs = [pe.alloc_register(f"tile_expert{u}") for u in range(UNROLL)]

            def pick(i, u):
                pe.reg_load(regs[u], g.te[0:1, bass.ds(i, 1)])

            def expert(u):
                return pe.snap(regs[u], min_val=0, max_val=NE - 1)

            def transpose_x(i, u):
                if isinstance(i, int):
                    pe.wait_ge(s_x[u], 16 * (i // NX + 1))
                else:
                    pe.wait_ge(s_x[u], (i - u) * (16 // NX) + 16)
                reused(pe, s_xl, i, 1)
                for k in range(2):
                    mm = pe.transpose(b_x[:, k, :], xg[:, u, k * HALF:(k + 1) * HALF], g.ident[:, :])
                mm.then_inc(s_xTp, 1)

            def first(i, u):
                if isinstance(i, int) and i == 0:
                    pe.wait_ge(s_lo_v, sum(n < n1 for n in on_vector))
                    pe.wait_ge(s_lo_p, sum(n < n1 for n in on_pool))
                e = expert(u)
                item(pe, s_xl, i)
                for n in range(2):
                    m = 0
                    for k in range(2):
                        for x, w, rows in ((x_lo, e1_hi, HALF), (x_hi, e1_lo, HALF + k), (x_hi, e1_hi, HALF + k)):
                            mm = pe.matmul(b_h[n], x[0:rows, k, :],
                                           w[0:rows, k, bass.ds(e, 1), n * N2:(n + 1) * N2].rearrange("p a f -> p (a f)"),
                                           start=(m == 0), stop=(m == 5))
                            m += 1
                    mm.then_inc(s_h1, 1)

            def turn(i, u):
                item(pe, s_r0, i)
                item(pe, s_r1, i)
                reused(pe, s_hl, i, 1, 2)
                for n in range(2):
                    for k in range(3):
                        c = 3 * n + k
                        mm = pe.transpose(b_hT[n][:, k, :], hid[:, c * 128:(c + 1) * 128], g.ident[:, :])
                    mm.then_inc(s_hTp, 1)

            def second(i, u):
                if isinstance(i, int) and i == 0:
                    pe.wait_ge(s_lo_v, len(on_vector))
                    pe.wait_ge(s_lo_p, len(on_pool))
                e = expert(u)
                reused(pe, s_ya, i, 2)
                for k in range(FC):
                    pe.wait_ge(s_hl, i * 2 + k // 3 + 1)
                    pe.matmul(b_y[u % 2], h_hi[:, k, :], e2[k][:, :, bass.ds(e, 1), :].rearrange("p two a d -> p two (a d)"),
                              start=(k == 0), stop=False)
                    mm = pe.matmul(b_y[u % 2][:, 1, :], h_lo[:, k, :], e2[k][:, 1, bass.ds(e, 1), :].rearrange("p a d -> p (a d)"),
                                   start=False, stop=(k == FC - 1))
                mm.then_inc(s_y, 1)

            steps(pe, NTILES, [(pick, 0), (transpose_x, 0), (second, 2), (turn, 1), (first, 0)])


def lay_out(i):
    a = {k: np.asarray(v) for k, v in i.items()}
    x = a["x"]
    xs = np.zeros_like(x)
    xs[:, :, 1:, 1:] = x[:, :, :-1, :-1]
    n = 128 // PATCH
    xs = xs.reshape(B, CIN, n, PATCH, n, PATCH).transpose(3, 5, 1, 0, 2, 4).reshape(KC, 128, B * n * n)
    w = a["L0_tok_weight"].transpose(2, 3, 1, 0).reshape(KP, D)
    kw = (np.arange(KP) // CIN) % PATCH
    q = {
        "x_patches": xs,
        "txt": a["txt"],
        "tok_w": w,
        "tok_move": np.tile(a["L0_tok_move_bias"], KP // CIN).reshape(KC, 128).T,
        "tok_keep": (kw != 0).astype(np.float32).reshape(KC, 128).T,
        "ident": np.eye(128, dtype=np.float32),
        "head_mask": np.kron(np.eye(HH), np.ones((DH, 1))).astype(np.float32),
        "a0_wqk": np.concatenate([np.concatenate([a["L0_attn_Wq"], a["L0_attn_Wk"]], 1),
                                  np.concatenate([a["L0_attn_bq"], a["L0_attn_bk"]])[None]], 0),
        "a0_wv": np.concatenate([a["L0_attn_Wv"], a["L0_attn_bv"][None]], 0),
        "a0_bo": a["L0_attn_bo"],
    }
    q.update({"norm_w": a["L0_ffn_norm_weight"], "slots": a["L0_ffn_slots"], "slot_scale": a["L0_ffn_scale"],
              "fc1_w": a["L0_ffn_fc1_weight"], "fc1_b": a["L0_ffn_fc1_bias"],
              "fc2_w": a["L0_ffn_fc2_weight"], "fc2_b": a["L0_ffn_fc2_bias"]})
    theta = np.float32(10000.0) ** (-2.0 * np.arange(D // 2, dtype=np.float32) / np.float32(D))
    angle = np.arange(T, dtype=np.float32)[:, None] * theta[None, :].astype(np.float32)
    cos, sin = np.cos(angle).astype(np.float32), np.sin(angle).astype(np.float32)
    q["rope_cos"] = np.tile(np.repeat(cos, 2, axis=1), (1, 2))
    q["rope_sin"] = np.tile(sin, (1, 2))
    q["rope_nsin"] = -q["rope_sin"]
    q["causal"] = np.where(np.tril(np.ones((T, T), bool)), 0.0, -1e30).astype(np.float32)
    q["a1_wqkv"] = np.concatenate([a["L1_attn_Wq"], a["L1_attn_Wk"], a["L1_attn_Wv"]], 1)
    q.update({"moe_wr": a["L1_ffn_Wr"], "moe_w1": a["L1_ffn_W1"], "moe_b1": a["L1_ffn_b1"],
              "moe_w2": a["L1_ffn_W2"], "moe_b2": a["L1_ffn_b2"]})
    q["iota"] = np.tile(np.arange(128, dtype=np.float32), (128, 1))
    pad = NTOK + np.arange(128, dtype=np.float32)
    q["padrow"] = np.stack([pad, -pad], 1)
    q["before"] = np.triu(np.ones((T, T), np.float32), 1)
    q["tokid"] = (np.arange(T)[:, None] + T * np.arange(B)[None, :]).astype(np.float32)
    wo = np.zeros((NH, HPAD, D), np.float32)
    wo[:, :DH] = a["L0_attn_Wo"].reshape(NH, DH, D)
    q["a0_wo"] = wo.reshape(NH * HPAD, D)
    return {k: np.ascontiguousarray(v) for k, v in q.items()}


def declare(nc, arrays):
    A = {k: nc.dram_tensor(f"in_{k}", v.shape, mybir.dt.from_np(v.dtype), kind="ExternalInput").ap()
         for k, v in arrays.items()}
    A["out"] = nc.dram_tensor("out_h", (NTOK + 128, D), F32, kind="ExternalOutput").ap()
    A["xtab"] = nc.dram_tensor("xtab", (NTOK + 128, D), F32, kind="Internal").ap()
    return A


def kernel(**inputs):
    import concourse.bacc as bacc
    from concourse.bass_utils import run_bass_kernel_spmd as run
    arrays = lay_out(inputs)
    nc = bacc.Bacc("TRN2", target_bir_lowering=False, num_devices=1)
    build(nc, declare(nc, arrays))
    r = run(nc, [{f"in_{k}": v for k, v in arrays.items()}], core_ids=[0])
    return r.results[0]["out_h"][:NTOK].reshape(B, T, D)
```
